# Optimizing a Trainium2 kernel written in Bass

```python
import numpy as np
import jax
import jax.numpy as jnp

def _softmax(x, axis=-1):
    return jax.nn.softmax(x, axis=axis)

def _gelu(x):
    return jax.nn.gelu(x, approximate=True)

def _silu(x):
    return jax.nn.silu(x)

def _sigmoid(x):
    return jax.nn.sigmoid(x)

def _layernorm(x, axis=-1, eps=1e-05):
    m = jnp.mean(x, axis=axis, keepdims=True)
    v = jnp.var(x, axis=axis, keepdims=True)
    return (x - m) / jnp.sqrt(v + eps)

def _scatter_add(tgt, idx, src, axis=0):
    return tgt.at[idx].add(src)

def _segment_sum(src, seg, n):
    return jax.ops.segment_sum(src, seg, n)
kernel_name = 'mk_macaron_d1_jaxref_r4_9d4e77'

def setup_inputs(seed: int=0):
    np.random.seed(seed)
    _w = jnp.asarray

    def _L0_attn_setup():
        import math
        import jax, jax.numpy as jnp
        import numpy as np
        NUM_HEADS = 16
        EMBED = 256
        B, T = (2, 512)
        key = jax.random.key(seed)
        k1, k2 = jax.random.split(key)
        x = jax.random.normal(k1, (B, T, EMBED), dtype=jnp.float32)
        bound = 1.0 / math.sqrt(NUM_HEADS * EMBED)
        weight = jax.random.uniform(k2, (NUM_HEADS * EMBED, EMBED), dtype=jnp.float32, minval=-bound, maxval=bound)
        return {'x': x, 'weight': weight}
    _L0_attn_in = _L0_attn_setup()

    def _L0_ffn_setup():
        import jax, jax.numpy as jnp
        import numpy as np
        DIM = 256
        DEPTH = 2
        HEADS = 8
        DIM_HEAD = 64
        WINDOW = 128
        INNER = HEADS * DIM_HEAD
        HID = int(DIM * 4 * 2 / 3)
        B, N = (2, 2048)
        QK_SCALE = 8.0

        def shift_token(t):
            t1, t2 = jnp.split(t, 2, axis=-1)
            t2 = jnp.pad(t2, ((0, 0), (1, 0), (0, 0)))[:, :-1]
            return jnp.concatenate([t1, t2], axis=-1)

        def l2norm(t):
            return t / jnp.clip(jnp.linalg.norm(t, axis=-1, keepdims=True), 1e-12)

        def rotate_half(x):
            x1, x2 = jnp.split(x, 2, axis=-1)
            return jnp.concatenate([-x2, x1], axis=-1)

        def rotary_xpos(q, k):
            n = q.shape[-2]
            half_idx = jnp.arange(0, DIM_HEAD, 2, dtype=jnp.float32)
            inv_freq = 1.0 / 10000.0 ** (half_idx / DIM_HEAD)
            t = jnp.arange(n, dtype=jnp.float32)
            freqs = t[:, None] * inv_freq[None, :]
            freqs = jnp.concatenate([freqs, freqs], axis=-1)
            base = (half_idx + 0.4 * DIM_HEAD) / (1.4 * DIM_HEAD)
            power = (t - n // 2) / float(WINDOW // 2)
            scale = base[None, :] ** power[:, None]
            scale = jnp.concatenate([scale, scale], axis=-1)
            cos, sin = (jnp.cos(freqs), jnp.sin(freqs))
            q = q * cos * scale + rotate_half(q) * sin * scale
            k = k * cos / scale + rotate_half(k) * sin / scale
            return (q, k)

        def local_attention(q, k, v):
            b, h, n, d = q.shape
            w = n // WINDOW
            bq = q.reshape(b, h, w, WINDOW, d) * QK_SCALE
            bk = k.reshape(b, h, w, WINDOW, d)
            bv = v.reshape(b, h, w, WINDOW, d)

            def look_around(t):
                p = jnp.pad(t, ((0, 0), (0, 0), (1, 0), (0, 0), (0, 0)))
                return jnp.concatenate([p[:, :, :w], p[:, :, 1:]], axis=3)
            bk, bv = (look_around(bk), look_around(bv))
            bt = jnp.arange(n).reshape(w, WINDOW)
            btp = jnp.pad(bt, ((1, 0), (0, 0)), constant_values=-1)
            btk = jnp.concatenate([btp[:w], btp[1:]], axis=1)
            sim = jnp.einsum('bhwid,bhwjd->bhwij', bq, bk)
            i = bt[:, :, None]
            j = btk[:, None, :]
            mask = (i < j) | (i > j + WINDOW) | (j == -1)
            sim = jnp.where(mask, -jnp.finfo(sim.dtype).max, sim)
            attn = jax.nn.softmax(sim, axis=-1)
            out = jnp.einsum('bhwij,bhwjd->bhwid', attn, bv)
            return out.reshape(b, h, n, d)

        def _layer(x, wqkv, qs, ksc, wo, lg, lb, w1, b1, w2, b2):
            b, n, _ = x.shape
            h = shift_token(x)
            qkv = h @ wqkv
            q, k, v = jnp.split(qkv, 3, axis=-1)
            to_heads = lambda t: t.reshape(b, n, HEADS, DIM_HEAD).transpose(0, 2, 1, 3)
            q, k, v = (to_heads(q), to_heads(k), to_heads(v))
            q = l2norm(q) * qs
            k = l2norm(k) * ksc
            q, k = rotary_xpos(q, k)
            o = local_attention(q, k, v)
            o = o.transpose(0, 2, 1, 3).reshape(b, n, INNER)
            x = x + o @ wo
            h = shift_token(x)
            mu = h.mean(-1, keepdims=True)
            var = h.var(-1, keepdims=True)
            h = (h - mu) / jnp.sqrt(var + 1e-05) * lg + lb
            h = h @ w1 + b1
            a, g = jnp.split(h, 2, axis=-1)
            h = a * jax.nn.gelu(g, approximate=False)
            x = x + h @ w2 + b2
            return x
        key = jax.random.key(seed)
        ks = jax.random.split(key, 6)
        return {'x': jax.random.normal(ks[0], (B, N, DIM), jnp.float32), 'wqkv': jax.random.normal(ks[1], (DEPTH, DIM, 3 * INNER), jnp.float32) * 0.02, 'q_scale': jnp.ones((DEPTH, DIM_HEAD), jnp.float32), 'k_scale': jnp.ones((DEPTH, DIM_HEAD), jnp.float32), 'wo': jax.random.normal(ks[2], (DEPTH, INNER, DIM), jnp.float32) * 0.02, 'ln_g': jnp.ones((DEPTH, DIM), jnp.float32), 'ln_b': jnp.zeros((DEPTH, DIM), jnp.float32), 'w1': jax.random.normal(ks[3], (DEPTH, DIM, 2 * HID), jnp.float32) * 0.02, 'b1': jnp.zeros((DEPTH, 2 * HID), jnp.float32), 'w2': jax.random.normal(ks[4], (DEPTH, HID, DIM), jnp.float32) * 0.02, 'b2': jnp.zeros((DEPTH, DIM), jnp.float32)}
    _L0_ffn_in = _L0_ffn_setup()
    _d = {'L0_attn_x': _L0_attn_in['x'], 'L0_attn_weight': _L0_attn_in['weight'], 'L0_ffn_wqkv': _L0_ffn_in['wqkv'], 'L0_ffn_q_scale': _L0_ffn_in['q_scale'], 'L0_ffn_k_scale': _L0_ffn_in['k_scale'], 'L0_ffn_wo': _L0_ffn_in['wo'], 'L0_ffn_ln_g': _L0_ffn_in['ln_g'], 'L0_ffn_ln_b': _L0_ffn_in['ln_b'], 'L0_ffn_w1': _L0_ffn_in['w1'], 'L0_ffn_b1': _L0_ffn_in['b1'], 'L0_ffn_w2': _L0_ffn_in['w2'], 'L0_ffn_b2': _L0_ffn_in['b2']}
    _x0 = _d['L0_attn_x']
    _d['L0_attn_x'] = jax.random.normal(jax.random.fold_in(jax.random.key(seed), 1), (8, 512, 256), dtype=_x0.dtype)
    del _x0
    return _d

def reference(L0_attn_x, L0_attn_weight, L0_ffn_wqkv, L0_ffn_q_scale, L0_ffn_k_scale, L0_ffn_wo, L0_ffn_ln_g, L0_ffn_ln_b, L0_ffn_w1, L0_ffn_b1, L0_ffn_w2, L0_ffn_b2):

    def _L0_attn_ref(x, weight):
        import math
        import jax, jax.numpy as jnp
        import numpy as np
        NUM_HEADS = 16
        EMBED = 256
        B, T = (2, 512)
        b, t, c = x.shape
        nh = NUM_HEADS
        hs = c // nh
        y = x.reshape(b, t, nh, hs).transpose(0, 2, 1, 3)
        scores = jnp.einsum('bhtk,bhsk->bhts', y, y) / math.sqrt(hs)
        attn = jax.nn.softmax(scores, axis=-1)
        o = jnp.einsum('bhts,bsc->bhtc', attn, x)
        o = o.transpose(0, 2, 1, 3).reshape(b, t, nh * c)
        return o @ weight

    def _L0_ffn_ref(x, wqkv, q_scale, k_scale, wo, ln_g, ln_b, w1, b1, w2, b2):
        import jax, jax.numpy as jnp
        import numpy as np
        DIM = 256
        DEPTH = 2
        HEADS = 8
        DIM_HEAD = 64
        WINDOW = 128
        INNER = HEADS * DIM_HEAD
        HID = int(DIM * 4 * 2 / 3)
        B, N = (2, 2048)
        QK_SCALE = 8.0

        def shift_token(t):
            t1, t2 = jnp.split(t, 2, axis=-1)
            t2 = jnp.pad(t2, ((0, 0), (1, 0), (0, 0)))[:, :-1]
            return jnp.concatenate([t1, t2], axis=-1)

        def l2norm(t):
            return t / jnp.clip(jnp.linalg.norm(t, axis=-1, keepdims=True), 1e-12)

        def rotate_half(x):
            x1, x2 = jnp.split(x, 2, axis=-1)
            return jnp.concatenate([-x2, x1], axis=-1)

        def rotary_xpos(q, k):
            n = q.shape[-2]
            half_idx = jnp.arange(0, DIM_HEAD, 2, dtype=jnp.float32)
            inv_freq = 1.0 / 10000.0 ** (half_idx / DIM_HEAD)
            t = jnp.arange(n, dtype=jnp.float32)
            freqs = t[:, None] * inv_freq[None, :]
            freqs = jnp.concatenate([freqs, freqs], axis=-1)
            base = (half_idx + 0.4 * DIM_HEAD) / (1.4 * DIM_HEAD)
            power = (t - n // 2) / float(WINDOW // 2)
            scale = base[None, :] ** power[:, None]
            scale = jnp.concatenate([scale, scale], axis=-1)
            cos, sin = (jnp.cos(freqs), jnp.sin(freqs))
            q = q * cos * scale + rotate_half(q) * sin * scale
            k = k * cos / scale + rotate_half(k) * sin / scale
            return (q, k)

        def local_attention(q, k, v):
            b, h, n, d = q.shape
            w = n // WINDOW
            bq = q.reshape(b, h, w, WINDOW, d) * QK_SCALE
            bk = k.reshape(b, h, w, WINDOW, d)
            bv = v.reshape(b, h, w, WINDOW, d)

            def look_around(t):
                p = jnp.pad(t, ((0, 0), (0, 0), (1, 0), (0, 0), (0, 0)))
                return jnp.concatenate([p[:, :, :w], p[:, :, 1:]], axis=3)
            bk, bv = (look_around(bk), look_around(bv))
            bt = jnp.arange(n).reshape(w, WINDOW)
            btp = jnp.pad(bt, ((1, 0), (0, 0)), constant_values=-1)
            btk = jnp.concatenate([btp[:w], btp[1:]], axis=1)
            sim = jnp.einsum('bhwid,bhwjd->bhwij', bq, bk)
            i = bt[:, :, None]
            j = btk[:, None, :]
            mask = (i < j) | (i > j + WINDOW) | (j == -1)
            sim = jnp.where(mask, -jnp.finfo(sim.dtype).max, sim)
            attn = jax.nn.softmax(sim, axis=-1)
            out = jnp.einsum('bhwij,bhwjd->bhwid', attn, bv)
            return out.reshape(b, h, n, d)

        def _layer(x, wqkv, qs, ksc, wo, lg, lb, w1, b1, w2, b2):
            b, n, _ = x.shape
            h = shift_token(x)
            qkv = h @ wqkv
            q, k, v = jnp.split(qkv, 3, axis=-1)
            to_heads = lambda t: t.reshape(b, n, HEADS, DIM_HEAD).transpose(0, 2, 1, 3)
            q, k, v = (to_heads(q), to_heads(k), to_heads(v))
            q = l2norm(q) * qs
            k = l2norm(k) * ksc
            q, k = rotary_xpos(q, k)
            o = local_attention(q, k, v)
            o = o.transpose(0, 2, 1, 3).reshape(b, n, INNER)
            x = x + o @ wo
            h = shift_token(x)
            mu = h.mean(-1, keepdims=True)
            var = h.var(-1, keepdims=True)
            h = (h - mu) / jnp.sqrt(var + 1e-05) * lg + lb
            h = h @ w1 + b1
            a, g = jnp.split(h, 2, axis=-1)
            h = a * jax.nn.gelu(g, approximate=False)
            x = x + h @ w2 + b2
            return x
        for l in range(DEPTH):
            x = _layer(x, wqkv[l], q_scale[l], k_scale[l], wo[l], ln_g[l], ln_b[l], w1[l], b1[l], w2[l], b2[l])
        return x
    x = L0_attn_x
    x = x + 0.5 * _L0_ffn_ref(_layernorm(x, axis=-1), L0_ffn_wqkv, L0_ffn_q_scale, L0_ffn_k_scale, L0_ffn_wo, L0_ffn_ln_g, L0_ffn_ln_b, L0_ffn_w1, L0_ffn_b1, L0_ffn_w2, L0_ffn_b2)
    x = x + _L0_attn_ref(_layernorm(x, axis=-1), L0_attn_weight)
    x = x + 0.5 * _L0_ffn_ref(_layernorm(x, axis=-1), L0_ffn_wqkv, L0_ffn_q_scale, L0_ffn_k_scale, L0_ffn_wo, L0_ffn_ln_g, L0_ffn_ln_b, L0_ffn_w1, L0_ffn_b1, L0_ffn_w2, L0_ffn_b2)
    return x

_drawn_inputs = setup_inputs


def setup_inputs(seed=0):
    import zlib

    import numpy as np

    out = dict(_drawn_inputs(seed))
    spreads = {'L0_ffn_q_scale': (1.0, 0.6),
     'L0_ffn_k_scale': (1.0, 0.6),
     'L0_ffn_ln_g': (1.0, 0.6),
     'L0_ffn_ln_b': (0.0, 0.8),
     'L0_ffn_b1': (0.0, 0.697),
     'L0_ffn_b2': (0.0, 0.1)}
    factors = {}
    for name, (base, spread) in spreads.items():
        noise = np.random.default_rng([zlib.crc32(name.encode()), seed]).standard_normal(out[name].shape)
        drawn = base * np.exp(spread * noise) if base else spread * noise
        out[name] = jnp.asarray(drawn.astype(out[name].dtype))
    for name, factor in factors.items():
        out[name] = (out[name] * factor).astype(out[name].dtype)
    return out
```

```python
from contextlib import ExitStack

import numpy as np

import concourse.bass as bass
from concourse import mybir

ALU = mybir.AluOpType
ACT = mybir.ActivationFunctionType
AX = mybir.AxisListType
F32 = mybir.dt.float32
F32R = mybir.dt.float32r

P = 128
B, N, D = 8, 512, 256
NT = N // P
KD = D // P
HEADS, DH = 8, 64
PAIRS = HEADS // 2
INNER = HEADS * DH
HID = int(D * 4 * 2 / 3)
FJ = HID // P
HR = HID - FJ * P
QK_SCALE = 8.0
EPS = 1e-5
LAYERS = 2
ROUNDS = LAYERS * B
GH = 16
GS = D // GH
GSCALE = float(GS) ** -0.5
MASKED = -1e37

PHASE1 = ("q0 k0 v0 q1 k1 v1 n0 g0 Q0 q2 a0 K0 k2 g1 u0 v2 Q1 a1 q3 g2 K1 k3 w0 u1 a2 v3 g3 Q2 w1 u2 "
          "a3 K2 g4 w2 u3 a4 Q3 g5 w3 u4 a5 K3 w4 u5 w5").split()

SLOTS = 12
AV_OUT = (5, 7, 9, 11)
PREP = 9


def rotary_tables():
    f = np.float32
    half = np.arange(0, DH, 2, dtype=f)
    inv_freq = (f(1.0) / f(10000.0) ** (half / f(DH))).astype(f)
    t = np.arange(N, dtype=f)
    freqs = t[:, None] * inv_freq[None, :]
    freqs = np.concatenate([freqs, freqs], axis=-1)
    base = (half + f(0.4 * DH)) / f(1.4 * DH)
    power = (t - f(N // 2)) / f(P // 2)
    scale = (base[None, :] ** power[:, None]).astype(f)
    scale = np.concatenate([scale, scale], axis=-1)
    sign = np.where(np.arange(DH) < DH // 2, f(-1), f(1))[None, :]
    cos, sin = np.cos(freqs), np.sin(freqs) * sign
    tables = np.stack([cos * scale, sin * scale, cos / scale, sin / scale]).astype(f)
    return np.ascontiguousarray(tables.reshape(4, NT, P, DH).transpose(2, 0, 1, 3))


def build_macaron(nc, x, g_w, wqkv, q_scale, k_scale, wo, ln_g, ln_b, w1, b1, w2, b2, tables, out):
    with ExitStack() as ctx, nc.allow_non_contiguous_dma(reason="vectors by feature"):
        build(nc, ctx, x, g_w, wqkv, q_scale, k_scale, wo, ln_g, ln_b, w1, b1, w2, b2, tables, out)


def build(nc, ctx, x, g_w, wqkv, q_scale, k_scale, wo, ln_g, ln_b, w1, b1, w2, b2, tables, out):
    def sb(name, shape, dt=F32, c=ctx):
        return c.enter_context(nc.sbuf_tensor(name, shape, dt))

    def sem(name):
        return ctx.enter_context(nc.semaphore(name))

    def need(eng, s, value):
        if isinstance(value, int) and value <= 0:
            return
        eng.wait_ge(s, value)

    def need_apart(eng, *waits):
        for s, v in waits:
            need(eng, s, v)
            eng.sem_inc(S["apart"], 1)

    def f32(ap):
        return ap.bitcast(F32)

    stream = nc.dram_tensor("stream", (2 * ROUNDS, N, D), F32, kind="Internal").ap()
    x_mid = nc.dram_tensor("x_mid", (2, B, N, D), F32, kind="Internal").ap()

    def tokens(ap, row):
        if isinstance(row, int):
            return ap[row].rearrange("(t p) d -> p t d", p=P)
        return ap[bass.ds(row, 1)].rearrange("o (t p) d -> p (o t) d", p=P)

    ident = sb("ident", [P, P])
    mask = sb("mask", [P, 2 * P])
    minus_half = sb("minus_half", [P, 2 * HEADS])
    rope = sb("rope", [P, 4, NT, DH])
    qks = sb("qks", [P, 2, DH])
    lnp = sb("lnp", [P, 2, KD])
    b1t = sb("b1t", [P, 2 * (FJ + 1)])
    wqkv_s = [sb(f"wqkv_{s}", [P, KD, 3 * INNER], F32R) for s in ("hi", "lo")]
    wo_s = [sb(f"wo_{s}", [P, PAIRS, D], F32R) for s in ("hi", "lo")]
    w1_s = [sb(f"w1_{s}", [P, KD, 2 * HID], F32R) for s in ("hi", "lo")]
    w2_s = [sb(f"w2_{s}", [P, FJ + 1, D], F32R) for s in ("hi", "lo")]
    probs = sb("probs", [P, 3, NT, 2 * P])
    flat = probs[:].rearrange("p a b c -> p a (b c)")
    m2 = [[flat[:, w, r * N:(r + 1) * N] for r in range(2)] for w in range(2)]
    sq = [flat[:, 2, 0:N], flat[:, 2, N:2 * N]]
    raw = flat.rearrange("p a b -> p (a b)")

    ffn_mem = ExitStack()
    with ExitStack() as first:
        x_all = sb("x_all", [P, B * NT, D], c=first)
        st0 = sb("st0", [P, B * NT, 6], c=first)
        mv0 = sb("mv0", [P, B * NT, 2], c=first)
        ve0 = sb("ve0", [P, B * NT], c=first)
        rs0 = sb("rs0", [P, B * NT], c=first)
        half0 = sb("half0", [P, B * NT], c=first)
    xnext = sb("xnext", [P, NT, D], c=ffn_mem)
    xin = sb("xin", [P, NT, D], c=ffn_mem)
    xmid = sb("xmid", [P, NT, D], c=ffn_mem)
    nrm = sb("nrm", [P, NT, D], c=ffn_mem)
    hT = [sb(f"hT_{s}", [P, KD, N], F32R, ffn_mem) for s in ("hi", "lo")]
    nT = [sb(f"nT_{s}", [P, KD, N], F32R, ffn_mem) for s in ("hi", "lo")]
    turned_qk = sb("turned_qk", [P, 2, 2, INNER], c=ffn_mem)
    m1 = [[turned_qk[:, w, r, :] for r in range(2)] for w in range(2)]
    qT = sb("qT", [P, PAIRS, N], c=ffn_mem)
    kT = sb("kT", [P, PAIRS, N], c=ffn_mem)
    v_s = [sb(f"v_{s}", [P, NT, PAIRS, 3 * DH], F32R, ffn_mem) for s in ("hi", "lo")]
    pT = [sb(f"pT_{s}", [P, 2, 7 * P], F32R, ffn_mem) for s in ("hi", "lo")]
    oT = [sb(f"oT_{s}", [P, 2, N], F32R, ffn_mem) for s in ("hi", "lo")]
    gate = sb("gate", [P, 2, N], c=ffn_mem)
    hid = sb("hid", [P, 2, N], c=ffn_mem)
    hid_r = sb("hid_r", [P, N], c=ffn_mem)
    ssq = sb("ssq", [P, NT, 2 * HEADS], c=ffn_mem)
    rinv = sb("rinv", [P, NT, 2 * HEADS], c=ffn_mem)
    rq = sb("rq", [P, 2, NT, HEADS], c=ffn_mem)
    mx = sb("mx", [P, HEADS, NT], c=ffn_mem)
    nb = sb("nb", [P, HEADS, NT], c=ffn_mem)
    zs = sb("zs", [P, HEADS, NT], c=ffn_mem)
    rz = sb("rz", [P, HEADS, NT], c=ffn_mem)
    st = sb("st", [P, NT, 2, 6], c=ffn_mem)
    mv = sb("mv", [P, NT, 2], c=ffn_mem)
    ve = sb("ve", [P, NT], c=ffn_mem)
    rs = sb("rs", [P, NT], c=ffn_mem)
    ffn_mem.close()

    glb_mem = ExitStack()
    gw = [sb(f"gw_{s}", [P, GH * KD, D], F32R, glb_mem) for s in ("hi", "lo")]
    gx = sb("gx", [P, NT, D], c=glb_mem)
    gy = [sb(f"gy_{s}", [P, NT, D], F32R, glb_mem) for s in ("hi", "lo")]
    ga = raw[:, 0:2 * NT * GH * GS].rearrange("p (s t h c g) -> p s t h c g", s=2, t=NT, h=GH // 4, c=4)
    gaT = sb("gaT", [P, 2, 2, N], F32R, glb_mem)
    ge = sb("ge", [P, 4, N], c=glb_mem)
    ges = [sb(f"ge_{s}", [P, 4, N], F32R, glb_mem) for s in ("hi", "lo")]
    goT = [sb(f"goT_{s}", [P, KD, N], F32R, glb_mem) for s in ("hi", "lo")]
    gz = sb("gz", [P, GH, NT], c=glb_mem)
    grz = sb("grz", [P, GH, NT], c=glb_mem)
    gst = sb("gst", [P, NT, 6], c=glb_mem)
    gmv = sb("gmv", [P, NT, 2], c=glb_mem)
    gve = sb("gve", [P, NT], c=glb_mem)
    grs = sb("grs", [P, NT], c=glb_mem)
    gn = ge[:, 0:2, :].rearrange("p a (b d) -> p (a b) d", d=D)
    glb_mem.close()

    psum = ctx.enter_context(nc.psum_tensor("psum", [P, 8, N], F32))
    RB = [psum[:, 0, :], psum[:, 1, :]]
    TB = [psum[:, 2, :], psum[:, 3, :]]
    AV = psum[:, 4, :]
    UB = psum[:, 5, :]
    ACC = [psum[:, 6, :], psum[:, 7, :]]

    names = """apart consts x0_in x0_stats x0_var x0_rs x0_z stage
        w_in0 w_in1 w_hi w_lo w_small rope_ok bias_mm bias_ok
        x_in x_stored shift_in xold_in
        pe_z pe_qkv pe_qk_t pe_s pe_p pe_av pe_wo pe_n pe_w1 pe_w2
        act_x act_z act_sq act_v act_qk act_exp act_p act_av act_n act_gate act_u
        dve_z dve_rope dve_sum dve_ssq dve_v dve_rq dve_add dve_red dve_s dve_nb dve_rz dve_p dve_av dve_wo
        dve_st dve_mv dve_var dve_n dve_nlo dve_hid dve_w2
        pool_r pool_q pool_m pool_k pool_n pool_rs pool_u
        g_in g_out g_st g_mv g_var g_rs g_y g_yhi g_ylo g_pack g_t g_tc g_s g_exp g_hi g_lo g_o g_ohi g_olo
        g_rz g_w g_acc g_st2 g_mv2 g_var2 g_rs2 g_z""".split()
    S = {n: sem(n) for n in names}

    def stage_end(eng, k):
        eng.drain().then_inc(S["stage"], 1)
        eng.wait_ge(S["stage"], 5 * (k + 1))

    block = ctx.enter_context(nc.Block())

    def rounds(eng, call, prep, a_round, w_a, w_f, last_f):
        n0 = call * ROUNDS
        w_a(2 * call)
        w_f(2 * call)
        prep(n0, None)
        a_round(n0, f=None, final=False, nxt="first")
        a_round(n0 + 1, f=n0, final=False, nxt="loop0")
        with eng.Fori(n0 + 2, n0 + B) as n:
            a_round(n, f=n - 1, final=False, nxt="loop0")
        w_a(2 * call + 1)
        a_round(n0 + B, f=n0 + B - 1, final=False, nxt="loop1")
        w_f(2 * call + 1)
        with eng.Fori(n0 + B + 1, n0 + ROUNDS - 1) as n:
            a_round(n, f=n - 1, final=True, nxt="loop1")
        a_round(n0 + ROUNDS - 1, f=n0 + ROUNDS - 2, final=True, nxt=None)
        last_f(n0 + ROUNDS - 1)

    W_A, W_F = 3, 3
    WBUF = [raw[:, 0:3 * INNER], raw[:, 3 * INNER:6 * INNER]]
    G_CHUNKS = 8
    G_COLS = GH * KD // G_CHUNKS

    def w_base(stage):
        return stage * (W_A + W_F) + (G_CHUNKS if stage >= 2 else 0)

    G_BASE = 2 * (W_A + W_F)
    CHUNK_DMAS = [1, 1, 1, 1, 1, 3] * 2 + [1] * G_CHUNKS + [1, 1, 1, 1, 1, 3] * 2

    def chunk_in(eng, k):
        eng.wait_ge(S[f"w_in{k % 2}"], 16 * sum(CHUNK_DMAS[k % 2:k + 1:2]))

    def weights_done(eng, k):
        eng.wait_ge(S["w_lo"], k)

    @block.sync
    def _(sp):
        for b in range(B):
            sp.dma_start(x_all[:, b * NT:(b + 1) * NT, :], tokens(x, b)).then_inc(S["x0_in"], 16)
        for b in range(B):
            sp.wait_ge(S["x0_z"], NT * (b + 1))
            sp.dma_start(tokens(stream, b), x_all[:, b * NT:(b + 1) * NT, :]).then_inc(S["x0_in"], 16)
        sp.wait_ge(S["x0_in"], 16 * 2 * B)
        stage_end(sp, 0)

        def chunk(k, dst_src):
            if k >= 2:
                sp.wait_ge(S["w_lo"], k - 1)
            for dst, src in dst_src:
                sp.dma_start(dst, src).then_inc(S[f"w_in{k % 2}"], 16)

        def w_a(stage):
            l, k = stage % LAYERS, w_base(stage)
            if stage:
                sp.wait_ge(S["pe_p"], 2 * HEADS * B * stage)
                sp.wait_ge(S["pe_s"], 2 * HEADS * B * stage)
            sp.dma_start(rope[:], tables).then_inc(S["w_small"], 16)
            for i, ap in enumerate((q_scale, k_scale)):
                sp.dma_start(qks[:, i, :], ap[l:l + 1, :].to_broadcast([P, DH])).then_inc(S["w_small"], 16)
            for kt in range(KD):
                chunk(k + kt, [(WBUF[(k + kt) % 2], wqkv[l, kt * P:(kt + 1) * P, :])])
            chunk(k + 2, [(WBUF[(k + 2) % 2][:, 0:PAIRS * D].rearrange("p (k d) -> p k d", d=D),
                           wo[l].rearrange("(k p) d -> p k d", p=P))])

        def w_f(stage):
            l, k = stage % LAYERS, w_base(stage) + W_A
            if stage % LAYERS:
                sp.wait_ge(S["pe_p"], 2 * HEADS * (B * stage + 1))
                sp.wait_ge(S["dve_w2"], 2 * B * stage)
            sp.dma_start(lnp[:, 0, :], ln_g[l].rearrange("(k p) -> p k", p=P)).then_inc(S["w_small"], 16)
            sp.dma_start(lnp[:, 1, :], ln_b[l].rearrange("(k p) -> p k", p=P)).then_inc(S["w_small"], 16)
            b1v = b1t[:].rearrange("p (j c) -> p c j", c=2)
            for c in range(2):
                lo = HID * (1 - c)
                sp.dma_start(b1v[:, c, 0:FJ], b1[l, lo:lo + FJ * P].rearrange("(j p) -> p j", p=P)
                             ).then_inc(S["w_small"], 16)
                sp.dma_start(b1v[0:HR, c, FJ:FJ + 1], b1[l, lo + FJ * P:lo + HID].rearrange("(p o) -> p o", o=1)
                             ).then_inc(S["w_small"], 16)
            for kt in range(KD):
                chunk(k + kt, [(WBUF[(k + kt) % 2][:, 0:2 * HID], w1[l, kt * P:(kt + 1) * P, :])])
            v = WBUF[(k + 2) % 2].rearrange("p (k d) -> p k d", d=D)
            sp.wait_ge(S["bias_mm"], stage + 1)
            chunk(k + 2, [(v[:, 0:FJ, :], w2[l, 0:FJ * P, :].rearrange("(k p) d -> p k d", p=P)),
                          (v[0:HR, FJ, :], w2[l, FJ * P:HID, :]), (v[HR:HR + 1, FJ, :], b2[l:l + 1, :])])

        def prep(n, stored):
            waits = [(S["pe_z"], KD * n), (S["act_x"], n)]
            if stored is not None:
                waits.append((S["x_stored"], stored))
            need_apart(sp, *waits)
            sp.dma_start(xnext[:], tokens(stream, n)).then_inc(S["x_in"], 16)

        def f_part(m, final):
            sp.wait_ge(S["dve_wo"], 2 * m + 2)
            need(sp, S["pe_n"], KD * m)
            need(sp, S["dve_w2"], 2 * m)
            sp.dma_start(nrm[1:P, :, P:D], xmid[0:P - 1, :, P:D]).then_inc(S["shift_in"], 16)
            sp.dma_start(nrm[0:1, 1:NT, P:D], xmid[P - 1:P, 0:NT - 1, P:D]).then_inc(S["shift_in"], 16)
            return final

        def f_tail(m, final, call):
            if final:
                need_apart(sp, (S["pe_n"], KD * (m + 1)))
                before = x if call == 0 else x_mid[1]
                sp.dma_start(nrm[:], tokens(before, m - call * ROUNDS - B)).then_inc(S["xold_in"], 16)
            need_apart(sp, (S["dve_w2"], 2 * m + 2))
            if final:
                after = x_mid[0] if call == 0 else out
                sp.dma_start(tokens(after, m - call * ROUNDS - B), xmid[:]).then_inc(S["x_stored"], 16)
            else:
                sp.dma_start(tokens(stream, m + B), xmid[:]).then_inc(S["x_stored"], 16)

        for call in range(2):
            def a_round(n, f, final, nxt, call=call):
                if f is not None:
                    f_part(f, final)
                if nxt:
                    prep(n + 1, {"first": None, "loop0": 16 * (n - 1), "loop1": 16 * (n - 6)}[nxt])
                if f is not None:
                    f_tail(f, final, call)

            def last_f(m, call=call):
                f_part(m, True)
                f_tail(m, True, call)
                sp.wait_ge(S["x_stored"], 16 * (m + 1))
                stage_end(sp, 1 + 2 * call)

            rounds(sp, call, prep, a_round, w_a, w_f, last_f)
            if call == 0:
                for c in range(G_CHUNKS):
                    chunk(G_BASE + c, [(WBUF[(G_BASE + c) % 2][:, 0:G_COLS * D].rearrange("p (k d) -> p k d", d=D),
                                        g_w[c * G_COLS * P:(c + 1) * G_COLS * P, :].rearrange("(k p) d -> p k d", p=P))])
                with sp.Fori(0, B) as b:
                    sp.dma_start(gx[:], tokens(x_mid[0], b)).then_inc(S["g_in"], 16)
                    need_apart(sp, (S["g_acc"], NT * GH * (b + 1)))
                    sp.dma_start(tokens(x_mid[1], b), gx[:]).then_inc(S["g_out"], 16)
                    need_apart(sp, (S["g_z"], NT * (b + 1)))
                    sp.dma_start(tokens(stream, b + ROUNDS), gn[:]).then_inc(S["g_out"], 16)
                    need_apart(sp, (S["g_out"], 32 * (b + 1)))
                stage_end(sp, 2)

    @block.gpsimd
    def _(pool):
        nc.gpsimd.memset(ident[:], 0.0)
        nc.gpsimd.memset(mask[:], 0.0)
        nc.gpsimd.memset(half0[:], -0.5)
        nc.gpsimd.memset(minus_half[:], -0.5).then_inc(S["consts"], 1)
        pool.wait_ge(S["consts"], 1)
        nc.gpsimd.affine_select(out=ident[:], in_=ident[:], compare_op=ALU.not_equal, fill=1.0, base=0,
                                pattern=[[-1, P]], channel_multiplier=1)
        nc.gpsimd.affine_select(out=mask[:, 0:P], in_=mask[:, 0:P], compare_op=ALU.is_ge, fill=MASKED, base=0,
                                pattern=[[1, P]], channel_multiplier=-1)
        nc.gpsimd.affine_select(out=mask[:, P:2 * P], in_=mask[:, P:2 * P], compare_op=ALU.is_ge, fill=MASKED,
                                base=0, pattern=[[-1, P]], channel_multiplier=1).then_inc(S["consts"], 1)
        pool.wait_ge(S["x0_var"], 1)
        pool.wait_ge(S["consts"], 2)
        nc.gpsimd.tensor_tensor(rs0[:], ve0[:], half0[:], ALU.pow).then_inc(S["x0_rs"], 1)
        stage_end(pool, 0)

        def prep(n, stored):
            pass

        def w_a(stage):
            pass

        def w_f(stage):
            pass

        def phase1(n, m):
            for step in PHASE1:
                kind, i = step[0], int(step[1])
                if kind == "k" and n is not None:
                    r = i % 2
                    pool.wait_ge(S["dve_rope"], 2 * (NT * n + i) + 1)
                    nc.gpsimd.tensor_tensor(m1[0][r], m1[0][r], m2[0][r], ALU.add).then_inc(S["pool_q"], 1)
                    pool.wait_ge(S["dve_rope"], 2 * (NT * n + i) + 2)
                    nc.gpsimd.tensor_tensor(m1[1][r], m1[1][r], m2[1][r], ALU.add).then_inc(S["pool_m"], 1)
                    pool.wait_ge(S["dve_ssq"], NT * n + i + 1)
                    need(pool, S["act_exp"], HEADS * n)
                    nc.gpsimd.tensor_tensor(rinv[:, i, :], ssq[:, i, :], minus_half[:], ALU.pow
                                            ).then_inc(S["pool_r"], 1)
                    pool.wait_ge(S["pool_r"], NT * n + i + 1)
                    pool.wait_ge(S["pool_m"], NT * n + i + 1)
                    kv = m1[1][r].rearrange("p (h d) -> p h d", h=HEADS)
                    nc.gpsimd.tensor_tensor(kv, kv, rinv[:, i, HEADS:2 * HEADS].unsqueeze(2).to_broadcast([P, HEADS, DH]),
                                            ALU.mult).then_inc(S["pool_k"], 1)
                if m is None:
                    continue
                if kind == "v" and i == 0:
                    pool.wait_ge(S["dve_var"], m + 1)
                    nc.gpsimd.tensor_tensor(rs[:], ve[:], minus_half[:, 0:NT], ALU.pow).then_inc(S["pool_rs"], 1)
                if kind == "u":
                    hr, s = (hid[:, i % 2, :], P) if i < FJ else (hid_r[0:HR + 1, :], HR + 1)
                    pool.wait_ge(S["act_u"], (FJ + 1) * m + i + 1)
                    nc.gpsimd.tensor_tensor(pT[1][0:s, i % 2, 0:N], hr, f32(pT[0][0:s, i % 2, 0:N]), ALU.subtract
                                            ).then_inc(S["pool_u"], 1)

        def a_round(n, f, final, nxt):
            phase1(n, f)
            for h in range(HEADS):
                need_apart(pool, (S["dve_rz"], HEADS * n + h + 1))
                for i in range(NT):
                    a = P if i == 0 else 0
                    last = nc.gpsimd.tensor_scalar(probs[:, h % 3, i, a:], probs[:, h % 3, i, a:], rz[:, h, i:i + 1],
                                                   1.0, ALU.mult, ALU.mult)
                last.then_inc(S["pool_n"], 1)

        for call in range(2):
            def last_f(m, call=call):
                phase1(None, m)
                stage_end(pool, 1 + 2 * call)

            rounds(pool, call, prep, a_round, w_a, w_f, last_f)
            if call == 0:
                with pool.Fori(0, B) as b:
                    pool.wait_ge(S["g_var"], b + 1)
                    nc.gpsimd.tensor_tensor(grs[:], gve[:], minus_half[:, 0:NT], ALU.pow).then_inc(S["g_rs"], 1)
                    for h in range(GH):
                        for t in range(NT):
                            k = h * NT + t
                            pool.wait_ge(S["g_hi"], GH * NT * b + k + 1)
                            if k >= 4:
                                pool.wait_ge(S["g_o"], GH * NT * b + k - 3)
                            nc.gpsimd.tensor_tensor(ges[1][:, k % 4, :], ge[:, k % 4, :], f32(ges[0][:, k % 4, :]),
                                                    ALU.subtract).then_inc(S["g_lo"], 1)
                    pool.wait_ge(S["g_var2"], b + 1)
                    nc.gpsimd.tensor_tensor(grs[:], gve[:], minus_half[:, 0:NT], ALU.pow).then_inc(S["g_rs2"], 1)
                stage_end(pool, 2)

    @block.scalar
    def _(act):
        copy = nc.scalar.copy
        stage_end(act, 0)

        def split_hi(k, outs):
            chunk_in(act, k)
            for o, i, scale in outs:
                if scale is None:
                    last = copy(o, i)
                else:
                    last = nc.scalar.activation(o, i, ACT.Copy, scale=scale)
            last.then_inc(S["w_hi"], 1)

        def w_a(stage):
            k = w_base(stage)
            need(act, S["pe_qkv"], 12 * B * stage)
            need(act, S["pe_wo"], PAIRS * B * stage)
            for kt in range(KD):
                split_hi(k + kt, [(wqkv_s[0][:, kt, :], WBUF[(k + kt) % 2], None)])
            split_hi(k + 2, [(wo_s[0][:].rearrange("p k d -> p (k d)"), WBUF[(k + 2) % 2][:, 0:PAIRS * D], None)])
            weights_done(act, k + W_A)

        def w_f(stage):
            k = w_base(stage) + W_A
            need(act, S["dve_w2"], 2 * B * stage)
            act.wait_ge(S["w_small"], 16 * (9 * stage + 9))
            for kt in range(KD):
                split_hi(k + kt, [(w1_s[0][:, kt, :], WBUF[(k + kt) % 2][:, 0:2 * HID], lnp[:, 0, kt:kt + 1])])
            v = WBUF[(k + 2) % 2].rearrange("p (k d) -> p k d", d=D)
            split_hi(k + 2, [(w2_s[0][:, 0:FJ, :], v[:, 0:FJ, :], None),
                             (w2_s[0][0:HR + 1, FJ, :], v[0:HR + 1, FJ, :], None)])
            weights_done(act, k + W_F)

        def prep(n, stored):
            need(act, S["pe_qkv"], 12 * n)
            for half in range(KD):
                act.wait_ge(S["pe_z"], KD * n + half + 1)
                if half == 0:
                    copy(hT[0][:, 0, :], TB[0]).then_inc(S["act_z"], 1)
                else:
                    copy(hT[0][:, 1, 1:N], TB[1][:, 0:N - 1]).then_inc(S["act_z"], 1)

        def phase1(n, m):
            tb = 0
            for step in PHASE1:
                kind, i = step[0], int(step[1])
                if n is not None:
                    if kind == "q" and i == 0:
                        act.wait_ge(S["x_in"], 16 * (n + 1))
                        need(act, S["dve_wo"], 2 * n)
                        copy(xin[:], xnext[:]).then_inc(S["act_x"], 1)
                    if kind in "qk":
                        w = "qk".index(kind)
                        act.wait_ge(S["dve_rope"], 2 * (NT * n + i) + w + 1)
                        if i == 0:
                            need(act, S["pe_p"], 2 * HEADS * n)
                        else:
                            act.wait_ge(S["dve_sum"], 2 * (NT * n + i) - 1 + w)
                        nc.scalar.activation(sq[w], RB[(3 * i + w) % 2], ACT.Square).then_inc(S["act_sq"], 1)
                    if kind == "v":
                        act.wait_ge(S["pe_qkv"], 12 * n + 3 * i + 3)
                        need(act, S["pe_av"], HEADS * n)
                        copy(v_s[0][:, i].rearrange("p a (s d) -> p a s d", s=3)[:, :, ::2, :],
                             RB[(3 * i + 2) % 2].rearrange("p (a s d) -> p a s d", a=PAIRS, s=2)).then_inc(S["act_v"], 1)
                    if kind in "QK":
                        w = "QK".index(kind)
                        act.wait_ge(S["pe_qk_t"], 2 * (NT * n + i) + w + 1)
                        need(act, S["pe_s"], 2 * HEADS * n)
                        copy((qT, kT)[w][:, :, i * P:(i + 1) * P],
                             TB[(2 * i + w) % 2].rearrange("p (a q) -> p a q", a=PAIRS)).then_inc(S["act_qk"], 1)
                if m is not None:
                    if kind == "n":
                        need(act, S["pe_w1"], 12 * m)
                        for half in range(KD):
                            act.wait_ge(S["pe_n"], KD * m + half + 1)
                            copy(nT[0][:, half, :], TB[half]).then_inc(S["act_n"], 1)
                    if kind == "g":
                        s = P if i < FJ else HR
                        act.wait_ge(S["pe_w1"], 12 * m + 2 * i + 1)
                        act.wait_ge(S["bias_ok"], 1)
                        need(act, S["dve_hid"], (FJ + 1) * m + max(i - 1, 0))
                        nc.scalar.activation(gate[0:s, i % 2, :], UB[0:s, :], ACT.Gelu,
                                             bias=b1t[0:s, 2 * i:2 * i + 1]).then_inc(S["act_gate"], 1)
                    if kind == "u":
                        hr, s = (hid[:, i % 2, :], P) if i < FJ else (hid_r[0:HR + 1, :], HR + 1)
                        act.wait_ge(S["dve_hid"], (FJ + 1) * m + i + 1)
                        if i < 2:
                            act.wait_ge(S["pe_av"], HEADS * (m + 1))
                        else:
                            act.wait_ge(S["pe_w2"], (FJ + 1) * m + i - 1)
                        copy(pT[0][0:s, i % 2, 0:N], hr).then_inc(S["act_u"], 1)

        def a_round(n, f, final, nxt):
            phase1(n, f)
            for s in range(SLOTS):
                if 0 <= s - 2 < HEADS:
                    h = s - 2
                    for half in range(2):
                        act.wait_ge(S["pe_p"], 2 * (HEADS * n + h) + half + 1)
                        if half == 0 and h >= 2:
                            act.wait_ge(S["pe_av"], HEADS * n + h - 1)
                        elif half == 0 and f is not None:
                            act.wait_ge(S["pe_w2"], (FJ + 1) * (f + 1))
                        w = 4 * P if half == 0 else 3 * P
                        copy(pT[0][:, h % 2, half * 4 * P:half * 4 * P + w], TB[half][:, 0:w]).then_inc(S["act_p"], 1)
                if s in AV_OUT:
                    p = AV_OUT.index(s)
                    act.wait_ge(S["pe_av"], HEADS * n + 2 * p + 2)
                    if p >= 2:
                        act.wait_ge(S["pe_wo"], PAIRS * n + p - 1)
                    copy(oT[0][:, p % 2, :], AV).then_inc(S["act_av"], 1)
                if s < HEADS:
                    act.wait_ge(S["dve_nb"], HEADS * n + s + 1)
                    if s == 0:
                        act.wait_ge(S["dve_rq"], n + 1)
                    for i in range(NT):
                        a = P if i == 0 else 0
                        last = nc.scalar.activation(probs[:, s % 3, i, a:], probs[:, s % 3, i, a:], ACT.Exp,
                                                    bias=nb[:, s, i:i + 1], scale=rq[:, 0, i, s:s + 1],
                                                    accum_out=zs[:, s, i:i + 1])
                    last.then_inc(S["act_exp"], 1)
                if s == PREP and nxt:
                    prep(n + 1, None)

        for call in range(2):
            def last_f(m, call=call):
                phase1(None, m)
                stage_end(act, 1 + 2 * call)

            rounds(act, call, prep, a_round, w_a, w_f, last_f)
            if call == 0:
                for c in range(G_CHUNKS):
                    k = G_BASE + c
                    split_hi(k, [(gw[0][:, c * G_COLS:(c + 1) * G_COLS, :].rearrange("p k d -> p (k d)"),
                                  WBUF[k % 2][:, 0:G_COLS * D], None)])
                weights_done(act, G_BASE + G_CHUNKS)
                with act.Fori(0, B) as b:
                    act.wait_ge(S["g_y"], b + 1)
                    copy(gy[0][:].rearrange("p t d -> p (t d)"), gn.rearrange("p t d -> p (t d)")).then_inc(S["g_yhi"], 1)

                    def turned(pp):
                        for side in range(2):
                            act.wait_ge(S["g_t"], GH * b + 2 * pp + side + 1)
                            if pp >= 2:
                                act.wait_ge(S["g_s"], GH * NT * b + 8 * (pp - 1))
                            copy(gaT[:, pp % 2, side, :], TB[side]).then_inc(S["g_tc"], 1)

                    def out_hi(h):
                        act.wait_ge(S["g_o"], NT * (GH * b + h) + NT)
                        if h >= 1:
                            act.wait_ge(S["g_w"], GH * b + h)
                        for c in range(KD):
                            copy(goT[0][:, c, :], psum[:, 4 + c, :]).then_inc(S["g_ohi"], 1)

                    turned(0)
                    for k in range(GH * NT + 2):
                        if k % 8 == 2 and k // 8 + 1 < GH // 2:
                            turned(k // 8 + 1)
                        if k < GH * NT:
                            h, t = k // NT, k % NT
                            act.wait_ge(S["g_s"], GH * NT * b + k + 1)
                            if k == 0:
                                act.wait_ge(S["g_ylo"], b + 1)
                            if k >= 4:
                                act.wait_ge(S["g_lo"], GH * NT * b + k - 3)
                            nc.scalar.activation(ge[:, k % 4, :], RB[k % 2], ACT.Exp, scale=GSCALE,
                                                 accum_out=gz[:, h, t:t + 1]).then_inc(S["g_exp"], 1)
                        if k >= 5 and (k - 5) % 4 == 0:
                            out_hi((k - 5) // 4)
                stage_end(act, 2)

    @block.vector
    def _(dve):
        V = nc.vector
        for b in range(B):
            dve.wait_ge(S["x0_in"], 16 * B)
            for t in range(b * NT, (b + 1) * NT):
                V.bn_stats(st0[:, t, :], x_all[:, t, :]).then_inc(S["x0_stats"], 1)
        dve.wait_ge(S["x0_stats"], B * NT)
        for t in range(B * NT):
            V.bn_aggr(mv0[:, t, :], st0[:, t, :]).then_inc(S["x0_stats"], 1)
        dve.wait_ge(S["x0_stats"], 2 * B * NT)
        V.tensor_scalar(ve0[:], mv0[:, :, 1], EPS, None, ALU.add).then_inc(S["x0_var"], 1)
        dve.wait_ge(S["x0_rs"], 1)
        for t in range(B * NT):
            V.tensor_scalar(x_all[:, t, :], x_all[:, t, :], mv0[:, t, 0:1], rs0[:, t:t + 1], ALU.subtract, ALU.mult
                            ).then_inc(S["x0_z"], 1)
        stage_end(dve, 0)

        def split_lo(k, outs):
            dve.wait_ge(S["w_hi"], k + 1)
            for lo, hi, i, scale in outs:
                if scale is None:
                    last = V.tensor_tensor(lo, i, f32(hi), ALU.subtract)
                else:
                    last = V.scalar_tensor_tensor(lo, i, scale, f32(hi), ALU.mult, ALU.subtract)
            last.then_inc(S["w_lo"], 1)

        def w_a(stage):
            k = w_base(stage)
            if stage % LAYERS == 0:
                V.memset(f32(v_s[0][:]), 0.0)
                V.memset(f32(v_s[1][:]), 0.0)
                V.memset(f32(hT[0][:, 1, 0:1]), 0.0)
                V.memset(f32(hT[1][:, 1, 0:1]), 0.0)
                V.memset(hid_r[:], 1.0)
            dve.wait_ge(S["w_small"], 16 * (9 * stage + 3))
            for i in range(2):
                V.tensor_tensor(rope[:, 2 * i], rope[:, 2 * i], qks[:, i].unsqueeze(1).to_broadcast([P, NT, DH]), ALU.mult)
                for half in range(2):
                    a, o = half * DH // 2, (1 - half) * DH // 2
                    last = V.tensor_tensor(rope[:, 2 * i + 1, :, a:a + DH // 2], rope[:, 2 * i + 1, :, a:a + DH // 2],
                                           qks[:, i, o:o + DH // 2].unsqueeze(1).to_broadcast([P, NT, DH // 2]), ALU.mult)
            last.then_inc(S["rope_ok"], 1)
            for kt in range(KD):
                split_lo(k + kt, [(wqkv_s[1][:, kt, :], wqkv_s[0][:, kt, :], WBUF[(k + kt) % 2], None)])
            flat_wo = [w[:].rearrange("p k d -> p (k d)") for w in wo_s]
            split_lo(k + 2, [(flat_wo[1], flat_wo[0], WBUF[(k + 2) % 2][:, 0:PAIRS * D], None)])
            dve.wait_ge(S["rope_ok"], stage + 1)

        def w_f(stage):
            k = w_base(stage) + W_A
            for kt in range(KD):
                split_lo(k + kt, [(w1_s[1][:, kt, :], w1_s[0][:, kt, :], WBUF[(k + kt) % 2][:, 0:2 * HID],
                                   lnp[:, 0, kt:kt + 1])])
            v = WBUF[(k + 2) % 2].rearrange("p (k d) -> p k d", d=D)
            split_lo(k + 2, [(w2_s[1][:, 0:FJ, :], w2_s[0][:, 0:FJ, :], v[:, 0:FJ, :], None),
                             (w2_s[1][0:HR + 1, FJ, :], w2_s[0][0:HR + 1, FJ, :], v[0:HR + 1, FJ, :], None)])
            dve.wait_ge(S["bias_mm"], stage + 1)
            V.tensor_tensor(b1t[:, 0:2 * FJ], b1t[:, 0:2 * FJ], UB[:, 0:2 * FJ], ALU.add)
            V.tensor_tensor(b1t[0:HR, 2 * FJ:], b1t[0:HR, 2 * FJ:], UB[0:HR, 2 * FJ:2 * FJ + 2], ALU.add
                            ).then_inc(S["bias_ok"], 1)
            dve.wait_ge(S["bias_ok"], stage + 1)

        def prep(n, stored):
            for half in range(KD):
                dve.wait_ge(S["act_z"], KD * n + half + 1)
                a = half
                V.tensor_tensor(hT[1][:, half, a:N], TB[half][:, 0:N - a], f32(hT[0][:, half, a:N]), ALU.subtract
                                ).then_inc(S["dve_z"], 1)

        def phase1(n, m, final):
            for step in PHASE1:
                kind, i = step[0], int(step[1])
                if n is not None:
                    if kind in "qk":
                        w = "qk".index(kind)
                        dve.wait_ge(S["pe_qkv"], 12 * n + 3 * i + w + 1)
                        if i < 2:
                            need(dve, S["pe_p"], 2 * HEADS * n)
                        else:
                            dve.wait_ge(S["pe_qk_t"], 2 * (NT * n + i) - 3 + w)
                        src = RB[(3 * i + w) % 2]
                        h64 = "p (h d) -> p h d"
                        V.tensor_tensor(m1[w][i % 2].rearrange(h64, h=HEADS), src.rearrange(h64, h=HEADS),
                                        rope[:, 2 * w, i].unsqueeze(1).to_broadcast([P, HEADS, DH]), ALU.mult)
                        h232 = "p (h s d) -> p h s d"
                        sin = rope[:, 2 * w + 1, i].rearrange("p (s d) -> p s d", s=2)
                        V.tensor_tensor(m2[w][i % 2].rearrange(h232, h=HEADS, s=2), src.rearrange(h232, h=HEADS, s=2)[:, :, ::-1, :],
                                        sin.unsqueeze(1).to_broadcast([P, HEADS, 2, DH // 2]), ALU.mult
                                        ).then_inc(S["dve_rope"], 1)
                    if kind == "v":
                        dve.wait_ge(S["act_v"], NT * n + i + 1)
                        v3 = [v[:, i].rearrange("p a (s d) -> p a s d", s=3)[:, :, ::2, :] for v in v_s]
                        V.tensor_tensor(v3[1], RB[(3 * i + 2) % 2].rearrange("p (a s d) -> p a s d", a=PAIRS, s=2),
                                        f32(v3[0]), ALU.subtract).then_inc(S["dve_v"], 1)
                        for w in range(2):
                            dve.wait_ge(S["act_sq"], 2 * (NT * n + i) + w + 1)
                            V.tensor_reduce(ssq[:, i, w * HEADS:(w + 1) * HEADS],
                                            sq[w].rearrange("p (h d) -> p h d", h=HEADS), AX.X, ALU.add
                                            ).then_inc(S["dve_sum"], 1)
                        dve.wait_ge(S["dve_sum"], 2 * (NT * n + i) + 2)
                        V.tensor_scalar(ssq[:, i, :], ssq[:, i, :], 1e-24, None, ALU.max).then_inc(S["dve_ssq"], 1)
                if m is not None:
                    if kind == "v" and i == 0:
                        need(dve, S["pe_n"], KD * m)
                        V.memset(nrm[0:1, 0, P:D], 0.0).then_inc(S["dve_st"], 1)
                        dve.wait_ge(S["dve_wo"], 2 * m + 2)
                        for t in range(NT):
                            V.bn_stats(st[:, t, 0, :], xmid[:, t, 0:P])
                        dve.wait_ge(S["shift_in"], 32 * (m + 1))
                        dve.wait_ge(S["dve_st"], 2 * m + 1)
                        for t in range(NT):
                            last = V.bn_stats(st[:, t, 1, :], nrm[:, t, P:D])
                        last.then_inc(S["dve_st"], 1)
                        need_apart(dve, (S["dve_st"], 2 * m + 2))
                        for t in range(NT):
                            last = V.bn_aggr(mv[:, t, :], st[:, t])
                        last.then_inc(S["dve_mv"], 1)
                        dve.wait_ge(S["dve_mv"], m + 1)
                        V.tensor_scalar(ve[:], mv[:, :, 1], EPS, None, ALU.add).then_inc(S["dve_var"], 1)
                    if kind == "k" and i == 1:
                        dve.wait_ge(S["pool_rs"], m + 1)
                        for t in range(NT):
                            V.tensor_scalar(nrm[:, t, 0:P], xmid[:, t, 0:P], mv[:, t, 0:1], rs[:, t:t + 1],
                                            ALU.subtract, ALU.mult)
                            last = V.tensor_scalar(nrm[:, t, P:D], nrm[:, t, P:D], mv[:, t, 0:1], rs[:, t:t + 1],
                                                   ALU.subtract, ALU.mult)
                        last.then_inc(S["dve_n"], 1)
                    if kind == "n":
                        for half in range(KD):
                            dve.wait_ge(S["act_n"], KD * m + half + 1)
                            V.tensor_tensor(nT[1][:, half, :], TB[half], f32(nT[0][:, half, :]), ALU.subtract
                                            ).then_inc(S["dve_nlo"], 1)
                    if kind == "a":
                        hr, s = (hid[:, i % 2, :], P) if i < FJ else (hid_r[0:HR, :], HR)
                        dve.wait_ge(S["act_gate"], (FJ + 1) * m + i + 1)
                        dve.wait_ge(S["pe_w1"], 12 * m + 2 * i + 2)
                        need(dve, S["pool_u"], (FJ + 1) * m + max(i - 1, 0))
                        V.scalar_tensor_tensor(hr, UB[0:s, :], b1t[0:s, 2 * i + 1:2 * i + 2], gate[0:s, i % 2, :],
                                               ALU.add, ALU.mult).then_inc(S["dve_hid"], 1)
                    if kind == "w" and i == FJ:
                        dve.wait_ge(S["pe_w2"], (FJ + 1) * (m + 1))
                        for b in range(2):
                            xv = xmid[:, 2 * b:2 * b + 2, :].rearrange("p t d -> p (t d)")
                            ins = V.tensor_tensor(xv, ACC[b], xv, ALU.add)
                            ins.then_inc(S["dve_add" if final else "dve_w2"], 1)
                            if final:
                                continue
                        if final:
                            dve.wait_ge(S["xold_in"], 16 * finals(m))
                            dve.wait_ge(S["dve_add"], 2 * finals(m))
                            for b in range(2):
                                xv = xmid[:, 2 * b:2 * b + 2, :].rearrange("p t d -> p (t d)")
                                V.scalar_tensor_tensor(xv, xv, 0.5, nrm[:, 2 * b:2 * b + 2, :].rearrange("p t d -> p (t d)"),
                                                       ALU.mult, ALU.add).then_inc(S["dve_w2"], 1)

        def a_round(n, f, final, nxt):
            phase1(n, f, final)
            dve.wait_ge(S["pool_r"], NT * (n + 1))
            need(dve, S["act_exp"], HEADS * n)
            V.tensor_scalar(rq[:, 0], rinv[:, :, 0:HEADS], QK_SCALE, None, ALU.mult)
            V.tensor_scalar(rq[:, 1], rinv[:, :, 0:HEADS], -QK_SCALE, None, ALU.mult).then_inc(S["dve_rq"], 1)
            for s in range(-1, SLOTS):
                if 0 <= s - 1 < HEADS:
                    h = s - 1
                    dve.wait_ge(S["act_exp"], HEADS * n + h + 1)
                    V.reciprocal(rz[:, h, :], zs[:, h, :]).then_inc(S["dve_rz"], 1)
                if 0 <= s - 2 < HEADS:
                    h = s - 2
                    for half in range(2):
                        dve.wait_ge(S["act_p"], 2 * (HEADS * n + h) + half + 1)
                        a, w = half * 4 * P, (4 - half) * P
                        V.tensor_tensor(pT[1][:, h % 2, a:a + w], TB[half][:, 0:w], f32(pT[0][:, h % 2, a:a + w]),
                                        ALU.subtract).then_inc(S["dve_p"], 1)
                if s in AV_OUT:
                    p = AV_OUT.index(s)
                    dve.wait_ge(S["act_av"], PAIRS * n + p + 1)
                    V.tensor_tensor(oT[1][:, p % 2, :], AV, f32(oT[0][:, p % 2, :]), ALU.subtract
                                    ).then_inc(S["dve_av"], 1)
                if s + 1 < HEADS:
                    h = s + 1
                    for half in range(2):
                        waits = [(S["pe_s"], 2 * (HEADS * n + h) + half + 1)]
                        if half == 0 and h == 0:
                            waits.append((S["pe_qk_t"], 2 * NT * (n + 1)))
                        if half == 0 and h >= 3:
                            waits.append((S["pe_p"], 2 * (HEADS * n + h - 2)))
                        need_apart(dve, *waits)
                        for i in (2 * half, 2 * half + 1):
                            a = P if i == 0 else 0
                            last = V.tensor_tensor_reduce(probs[:, h % 3, i, a:],
                                                          RB[half][:, (i % 2) * 2 * P + a:(i % 2 + 1) * 2 * P],
                                                          mask[:, a:], 1.0, -3e38, ALU.add, ALU.max, mx[:, h, i:i + 1])
                        last.then_inc(S["dve_s"], 1)
                    dve.wait_ge(S["dve_s"], 2 * (HEADS * n + h) + 2)
                    if h == 0:
                        dve.wait_ge(S["dve_rq"], n + 1)
                    V.tensor_tensor(nb[:, h, :], mx[:, h, :], rq[:, 1, :, h], ALU.mult).then_inc(S["dve_nb"], 1)
                if s == PREP and nxt:
                    prep(n + 1, None)
            dve.wait_ge(S["pe_wo"], PAIRS * (n + 1))
            dve.wait_ge(S["act_x"], n + 1)
            if f is not None:
                dve.wait_ge(S["x_stored"], 16 * n)
            for b in range(2):
                V.tensor_tensor(xmid[:, 2 * b:2 * b + 2, :].rearrange("p t d -> p (t d)"), ACC[b],
                                xin[:, 2 * b:2 * b + 2, :].rearrange("p t d -> p (t d)"), ALU.add
                                ).then_inc(S["dve_wo"], 1)

        for call in range(2):
            def finals(m, call=call):
                return m + 1 - B * (call + 1)

            def last_f(m, call=call):
                phase1(None, m, True)
                stage_end(dve, 1 + 2 * call)

            rounds(dve, call, prep, a_round, w_a, w_f, last_f)
            if call == 0:
                for c in range(G_CHUNKS):
                    k = G_BASE + c
                    g2 = [g[:, c * G_COLS:(c + 1) * G_COLS, :].rearrange("p k d -> p (k d)") for g in gw]
                    split_lo(k, [(g2[1], g2[0], WBUF[k % 2][:, 0:G_COLS * D], None)])
                dve.wait_ge(S["w_lo"], G_BASE + G_CHUNKS)
                with dve.Fori(0, B) as b:

                    def norm(src, sems, done):
                        st_, mv_, var_, rs_ = sems
                        for t in range(NT):
                            last = V.bn_stats(gst[:, t, :], src[:, t, :])
                        last.then_inc(S[st_], 1)
                        need_apart(dve, (S[st_], b + 1))
                        for t in range(NT):
                            last = V.bn_aggr(gmv[:, t, :], gst[:, t, :])
                        last.then_inc(S[mv_], 1)
                        dve.wait_ge(S[mv_], b + 1)
                        V.tensor_scalar(gve[:], gmv[:, :, 1], EPS, None, ALU.add).then_inc(S[var_], 1)
                        dve.wait_ge(S[rs_], b + 1)
                        for t in range(NT):
                            last = V.tensor_scalar(gn[:, t, :], src[:, t, :], gmv[:, t, 0:1], grs[:, t:t + 1],
                                                   ALU.subtract, ALU.mult)
                            if done == "g_z":
                                last.then_inc(S["g_z"], 1)
                        if done != "g_z":
                            last.then_inc(S[done], 1)

                    dve.wait_ge(S["g_in"], 16 * (b + 1))
                    norm(gx, ("g_st", "g_mv", "g_var", "g_rs"), "g_y")
                    dve.wait_ge(S["g_yhi"], b + 1)
                    dve.wait_ge(S["g_y"], b + 1)
                    V.tensor_tensor(gy[1][:].rearrange("p t d -> p (t d)"), gn.rearrange("p t d -> p (t d)"),
                                    f32(gy[0][:].rearrange("p t d -> p (t d)")), ALU.subtract).then_inc(S["g_ylo"], 1)
                    dve.wait_ge(S["g_ylo"], b + 1)

                    def add_head(h):
                        dve.wait_ge(S["g_w"], GH * b + h + 1)
                        dve.wait_ge(S["g_rz"], GH * b + h + 1)
                        if h:
                            dve.wait_ge(S["g_acc"], NT * (GH * b + h))
                        for t in range(NT):
                            V.scalar_tensor_tensor(gx[:, t, :], ACC[t // 2][:, (t % 2) * D:(t % 2 + 1) * D],
                                                   grz[:, h, t:t + 1], gx[:, t, :], ALU.mult, ALU.add
                                                   ).then_inc(S["g_acc"], 1)

                    def pack(quarter):
                        if quarter:
                            dve.wait_ge(S["g_t"], GH * b + 4 * quarter)
                        cols = slice(quarter * 4 * GS, (quarter + 1) * 4 * GS)
                        for side, parts in enumerate(((0, 1, 0, 1), (0, 0, 1, 1))):
                            for c, part in enumerate(parts):
                                last = V.tensor_copy(ga[:, side, :, :, c, :],
                                                     f32(gy[part][:, :, cols]).rearrange("p t (h g) -> p t h g", g=GS))
                        last.then_inc(S["g_pack"], 1)

                    pack(0)
                    for k in range(GH * NT + 8):
                        if k < GH * NT:
                            dve.wait_ge(S["g_exp"], GH * NT * b + k + 1)
                            if k >= 4:
                                dve.wait_ge(S["g_o"], GH * NT * b + k - 3)
                            V.tensor_copy(ges[0][:, k % 4, :], ge[:, k % 4, :]).then_inc(S["g_hi"], 1)
                        if k % 16 == 4 and k // 16 < 3:
                            pack(k // 16 + 1)
                        if k >= 5 and (k - 5) % 4 == 0 and (k - 5) // 4 < GH:
                            h = (k - 5) // 4
                            V.reciprocal(grz[:, h, :], gz[:, h, :]).then_inc(S["g_rz"], 1)
                            for c in range(KD):
                                dve.wait_ge(S["g_ohi"], KD * (GH * b + h) + c + 1)
                                V.tensor_tensor(goT[1][:, c, :], psum[:, 4 + c, :], f32(goT[0][:, c, :]), ALU.subtract
                                                ).then_inc(S["g_olo"], 1)
                        if k >= 11 and (k - 11) % 4 == 0 and (k - 11) // 4 < GH:
                            h = (k - 11) // 4
                            add_head(h)
                    dve.wait_ge(S["g_acc"], GH * NT * (b + 1))
                    norm(gx, ("g_st2", "g_mv2", "g_var2", "g_rs2"), "g_z")
                stage_end(dve, 2)

    @block.tensor
    def _(pe):
        mm, turn = nc.tensor.matmul, nc.tensor.transpose
        stage_end(pe, 0)

        def three(out_, lhs, rhs, start, stop, **kw):
            mm(out_, lhs[0], rhs[0], start=start, stop=False, **kw)
            mm(out_, lhs[1], rhs[0], start=False, stop=False, **kw)
            return mm(out_, lhs[0], rhs[1], start=False, stop=stop, **kw)

        def w_a(stage):
            weights_done(pe, w_base(stage) + W_A)

        def w_f(stage):
            k = w_base(stage) + W_A
            chunk_in(pe, k)
            chunk_in(pe, k + 1)
            pe.wait_ge(S["w_small"], 16 * (9 * stage + 9))
            need(pe, S["dve_hid"], (FJ + 1) * B * stage)
            for j in range(FJ + 1):
                s = P if j < FJ else HR
                for c in range(2):
                    lo = HID * (1 - c) + j * P
                    for kt in range(KD):
                        last = mm(UB[0:s, 2 * j + c:2 * j + c + 1], WBUF[(k + kt) % 2][:, lo:lo + s],
                                  lnp[:, 1, kt:kt + 1], start=kt == 0, stop=kt == KD - 1, skip_group_check=True)
            last.then_inc(S["bias_mm"], 1)
            pe.wait_ge(S["bias_ok"], stage + 1)
            weights_done(pe, k + W_F)

        def prep(n, stored):
            pe.wait_ge(S["x_in"], 16 * (n + 1))
            for half in range(KD):
                if stored == "inside":
                    pe.wait_ge(S["dve_p"], 2 * (HEADS * n - 1) + half + 1)
                for t in range(NT):
                    last = turn(TB[half][:, t * P:(t + 1) * P], xnext[:, t, half * P:(half + 1) * P], ident[:])
                last.then_inc(S["pe_z"], 1)

        def phase1(n, m):
            for step in PHASE1:
                kind, i = step[0], int(step[1])
                if n is not None:
                    if kind in "qkv":
                        w = "qkv".index(kind)
                        k = 3 * i + w
                        if k == 0:
                            pe.wait_ge(S["dve_z"], KD * (n + 1))
                        if k < 2:
                            need(pe, S["dve_s"], 2 * HEADS * n)
                        elif (k - 2) % 3 == 2:
                            pe.wait_ge(S["dve_v"], NT * n + (k - 2) // 3 + 1)
                        else:
                            r = 2 * ((k - 2) // 3) + (k - 2) % 3 + 1
                            pe.wait_ge(S["act_sq"], 2 * NT * n + r)
                        for kt in range(KD):
                            last = three(RB[k % 2], [h[:, kt, i * P:(i + 1) * P] for h in hT],
                                         [x_[:, kt, w * INNER:(w + 1) * INNER] for x_ in wqkv_s],
                                         kt == 0, kt == KD - 1)
                        last.then_inc(S["pe_qkv"], 1)
                    if kind in "QK":
                        w = "QK".index(kind)
                        if w == 0:
                            pe.wait_ge(S["pool_q"], NT * n + i + 1)
                        else:
                            pe.wait_ge(S["pool_k"], NT * n + i + 1)
                        if i:
                            pe.wait_ge(S["act_qk"], 2 * (NT * n + i - 1) + w + 1)
                        elif m is not None:
                            pe.wait_ge(S["dve_nlo"], KD * m + w + 1)
                        else:
                            need(pe, S["dve_p"], 2 * HEADS * n)
                        for a in range(PAIRS):
                            last = turn(TB[w][:, a * P:(a + 1) * P], m1[w][i % 2][:, a * P:(a + 1) * P], ident[:])
                        last.then_inc(S["pe_qk_t"], 1)
                if m is not None:
                    if kind == "n":
                        pe.wait_ge(S["dve_n"], m + 1)
                        pe.wait_ge(S["dve_p"], 2 * HEADS * (m + 1))
                        for half in range(KD):
                            for t in range(NT):
                                last = turn(TB[half][:, t * P:(t + 1) * P], nrm[:, t, half * P:(half + 1) * P], ident[:])
                            last.then_inc(S["pe_n"], 1)
                    if kind in "ga":
                        c = "ga".index(kind)
                        s = P if i < FJ else HR
                        if c == 0:
                            if i == 0:
                                pe.wait_ge(S["dve_nlo"], KD * m + 2)
                            need(pe, S["dve_hid"], (FJ + 1) * m + i)
                        else:
                            pe.wait_ge(S["act_gate"], (FJ + 1) * m + i + 1)
                        lo = HID * (1 - c) + i * P
                        for kt in range(KD):
                            last = three(UB[0:s, :], [w_[:, kt, lo:lo + s] for w_ in w1_s], [h[:, kt, :] for h in nT],
                                         kt == 0, kt == KD - 1)
                        last.then_inc(S["pe_w1"], 1)
                    if kind == "w":
                        s = P if i < FJ else HR + 1
                        pe.wait_ge(S["pool_u"], (FJ + 1) * m + i + 1)
                        if i == 0:
                            pe.wait_ge(S["dve_wo"], 2 * m + 2)
                        for t in range(NT):
                            last = three(ACC[t // 2][:, (t % 2) * D:(t % 2 + 1) * D],
                                         [u[0:s, i % 2, t * P:(t + 1) * P] for u in pT],
                                         [w_[0:s, i, :] for w_ in w2_s],
                                         i == 0 and t % 2 == 0, i == FJ, skip_group_check=True)
                        last.then_inc(S["pe_w2"], 1)

        def a_round(n, f, final, nxt):
            phase1(n, f)
            for s in range(-1, SLOTS):
                if 0 <= s - 2 < HEADS:
                    h = s - 2
                    pe.wait_ge(S["pool_n"], HEADS * n + h + 1)
                    for half in range(2):
                        if h == 0:
                            pe.wait_ge(S["act_qk"], 2 * NT * (n + 1))
                        else:
                            pe.wait_ge(S["dve_p"], 2 * (HEADS * n + h - 1) + half + 1)
                        col = 0
                        for j in (2 * half, 2 * half + 1):
                            for i in (j, j + 1):
                                if i == NT:
                                    continue
                                a = P if i == j else 0
                                last = turn(TB[half][:, col:col + P], probs[:, h % 3, i, a:a + P], ident[:])
                                col += P
                        last.then_inc(S["pe_p"], 1)
                if s + 1 < HEADS:
                    h = s + 1
                    rows = slice((h % 2) * DH, (h % 2 + 1) * DH)
                    if h == 0:
                        pe.wait_ge(S["act_qk"], 2 * NT * (n + 1))
                    for half in range(2):
                        if h:
                            pe.wait_ge(S["dve_s"], 2 * (HEADS * n + h - 1) + half + 1)
                        elif half == 0:
                            pe.wait_ge(S["act_sq"], 2 * NT * (n + 1))
                        else:
                            pe.wait_ge(S["dve_v"], NT * (n + 1))
                        for i in (2 * half, 2 * half + 1):
                            a = P if i == 0 else 0
                            last = mm(RB[half][:, (i % 2) * 2 * P + a:(i % 2 + 1) * 2 * P],
                                      qT[rows, h // 2, i * P:(i + 1) * P], kT[rows, h // 2, (i - 1) * P + a:(i + 1) * P],
                                      start=True, stop=True)
                        last.then_inc(S["pe_s"], 1)
                if s == PREP and nxt:
                    prep(n + 1, "inside")
                if 0 <= s - 3 < HEADS:
                    h = s - 3
                    p, c = h // 2, (h % 2) * DH
                    pe.wait_ge(S["dve_p"], 2 * (HEADS * n + h) + 2)
                    if h == 0:
                        pe.wait_ge(S["dve_v"], NT * (n + 1))
                    if h % 2 == 0:
                        need(pe, S["dve_av"], PAIRS * n + p)
                    for j in range(NT):
                        w = 2 * P if j < NT - 1 else P
                        last = three(AV[:, j * P:j * P + w], [v[:, j, p, c:c + P] for v in v_s],
                                     [x_[:, h % 2, 2 * j * P:2 * j * P + w] for x_ in pT],
                                     h % 2 == 0 and j == 0, h % 2 == 1 and j == NT - 1, skip_group_check=True)
                    last.then_inc(S["pe_av"], 1)
                if s in AV_OUT:
                    p = AV_OUT.index(s)
                    pe.wait_ge(S["dve_av"], PAIRS * n + p + 1)
                    if p == 0 and f is not None:
                        pe.wait_ge(S["dve_w2"], 2 * (f + 1))
                    for t in range(NT):
                        last = three(ACC[t // 2][:, (t % 2) * D:(t % 2 + 1) * D],
                                     [o[:, p % 2, t * P:(t + 1) * P] for o in oT], [w_[:, p, :] for w_ in wo_s],
                                     p == 0 and t % 2 == 0, p == PAIRS - 1, skip_group_check=True)
                    last.then_inc(S["pe_wo"], 1)

        for call in range(2):
            def last_f(m, call=call):
                phase1(None, m)
                stage_end(pe, 1 + 2 * call)

            rounds(pe, call, prep, a_round, w_a, w_f, last_f)
            if call == 0:
                weights_done(pe, G_BASE + G_CHUNKS)
                with pe.Fori(0, B) as b:

                    def turn_pair(pp):
                        pe.wait_ge(S["g_pack"], 4 * b + pp // 2 + 1)
                        for side in range(2):
                            if pp:
                                pe.wait_ge(S["g_tc"], GH * b + 2 * (pp - 1) + side + 1)
                            for t in range(NT):
                                last = turn(TB[side][:, t * P:(t + 1) * P],
                                            ga[:, side, t, 2 * (pp % 2):2 * (pp % 2) + 2].rearrange("p h c g -> p (h c g)"),
                                            ident[:])
                            last.then_inc(S["g_t"], 1)

                    def project(h):
                        pe.wait_ge(S["g_olo"], KD * (GH * b + h) + 2)
                        if h:
                            pe.wait_ge(S["g_acc"], NT * (GH * b + h))
                        for t in range(NT):
                            for c in range(KD):
                                last = three(ACC[t // 2][:, (t % 2) * D:(t % 2 + 1) * D],
                                             [o[:, c, t * P:(t + 1) * P] for o in goT], [g[:, h * KD + c, :] for g in gw],
                                             t % 2 == 0 and c == 0, c == KD - 1, skip_group_check=True)
                        last.then_inc(S["g_w"], 1)

                    turn_pair(0)
                    for k in range(GH * NT + 2):
                        if k % 8 == 1 and k // 8 + 1 < GH // 2:
                            turn_pair(k // 8 + 1)
                        if k < GH * NT:
                            h, t = k // NT, k % NT
                            rows = slice((h % 2) * 4 * GS, (h % 2 + 1) * 4 * GS)
                            if k % 8 == 0:
                                pe.wait_ge(S["g_tc"], GH * b + 2 * (h // 2) + 2)
                            if k >= 2:
                                pe.wait_ge(S["g_exp"], GH * NT * b + k - 1)
                            mm(RB[k % 2], gaT[rows, (h // 2) % 2, 0, t * P:(t + 1) * P], gaT[rows, (h // 2) % 2, 1, :],
                               start=True, stop=True).then_inc(S["g_s"], 1)
                        if k >= 2:
                            h, t = (k - 2) // NT, (k - 2) % NT
                            pe.wait_ge(S["g_lo"], GH * NT * b + k - 1)
                            if t == 0 and h:
                                need(pe, S["g_olo"], KD * (GH * b + h))
                            for c in range(KD):
                                last = three(psum[:, 4 + c, :], [y[:, t, c * P:(c + 1) * P] for y in gy],
                                             [e[:, (k - 2) % 4, :] for e in ges], t == 0, t == NT - 1)
                            last.then_inc(S["g_o"], 1)
                            if t == NT - 1 and h:
                                project(h - 1)
                    project(GH - 1)
                stage_end(pe, 2)


INPUTS = ["L0_attn_x", "L0_attn_weight", "L0_ffn_wqkv", "L0_ffn_q_scale", "L0_ffn_k_scale", "L0_ffn_wo",
          "L0_ffn_ln_g", "L0_ffn_ln_b", "L0_ffn_w1", "L0_ffn_b1", "L0_ffn_w2", "L0_ffn_b2"]


def kernel(**inputs):
    import concourse.bacc as bacc
    from concourse.bass_utils import run_bass_kernel_spmd

    nc = bacc.Bacc("TRN2", target_bir_lowering=False, num_devices=1)
    arrays, args = {}, []
    for name in INPUTS:
        a = np.ascontiguousarray(inputs[name])
        arrays[name] = a
        args.append(nc.dram_tensor(name, a.shape, mybir.dt.from_np(a.dtype), kind="ExternalInput").ap())
    arrays["rotary"] = rotary_tables()
    args.append(nc.dram_tensor("rotary", arrays["rotary"].shape, F32, kind="ExternalInput").ap())
    args.append(nc.dram_tensor("out", (B, N, D), F32, kind="ExternalOutput").ap())
    build_macaron(nc, *args)
    r = run_bass_kernel_spmd(nc, [arrays], core_ids=[0])
    return r.results[0]["out"]
```

```python
from contextlib import ExitStack

import numpy as np

import concourse.bass as bass
from concourse import mybir

ALU = mybir.AluOpType
ACT = mybir.ActivationFunctionType
AX = mybir.AxisListType
F32 = mybir.dt.float32
F32R = mybir.dt.float32r

P = 128
B, N, D = 8, 512, 256
NT = N // P
KD = D // P
HEADS, DH = 8, 64
PAIRS = HEADS // 2
INNER = HEADS * DH
HID = int(D * 4 * 2 / 3)
FJ = HID // P
HR = HID - FJ * P
QK_SCALE = 8.0
EPS = 1e-5
LAYERS = 2
ROUNDS = LAYERS * B
GH = 16
GS = D // GH
GSCALE = float(GS) ** -0.5
MASKED = -1e37

PHASE1 = ("s0 q1 l0 x0 b0 k1 c0 v1 Q0 s1 q2 b1 j0 K0 k2 n0 c1 Q1 v2 g0 K1 s2 a0 q3 g1 u0 b2 k3 a1 c2 g2 "
          "v3 u1 w0 a2 s3 Q2 u2 g3 K2 b3 w1 a3 u3 c3 g4 Q3 w2 a4 K3 u4 g5 w3 a5 u5 w4 w5 e0").split()

SLOTS = 12
AV_OUT = (5, 7, 9, 11)
PREP = 9
EARLY = {10: ["q0"], 11: ["k0", "v0"]}


def rotary_tables():
    f = np.float32
    half = np.arange(0, DH, 2, dtype=f)
    inv_freq = (f(1.0) / f(10000.0) ** (half / f(DH))).astype(f)
    t = np.arange(N, dtype=f)
    freqs = t[:, None] * inv_freq[None, :]
    freqs = np.concatenate([freqs, freqs], axis=-1)
    base = (half + f(0.4 * DH)) / f(1.4 * DH)
    power = (t - f(N // 2)) / f(P // 2)
    scale = (base[None, :] ** power[:, None]).astype(f)
    scale = np.concatenate([scale, scale], axis=-1)
    sign = np.where(np.arange(DH) < DH // 2, f(-1), f(1))[None, :]
    cos, sin = np.cos(freqs), np.sin(freqs) * sign
    tables = np.stack([cos * scale, sin * scale, cos / scale, sin / scale]).astype(f)
    return np.ascontiguousarray(tables.reshape(4, NT, P, DH).transpose(2, 0, 1, 3))


def build_macaron(nc, x, g_w, wqkv, q_scale, k_scale, wo, ln_g, ln_b, w1, b1, w2, b2, tables, out):
    with ExitStack() as ctx, nc.allow_non_contiguous_dma(reason="vectors by feature"):
        build(nc, ctx, x, g_w, wqkv, q_scale, k_scale, wo, ln_g, ln_b, w1, b1, w2, b2, tables, out)


def build(nc, ctx, x, g_w, wqkv, q_scale, k_scale, wo, ln_g, ln_b, w1, b1, w2, b2, tables, out):
    def sb(name, shape, dt=F32, c=ctx):
        return c.enter_context(nc.sbuf_tensor(name, shape, dt))

    def sem(name):
        return ctx.enter_context(nc.semaphore(name))

    def need(eng, s, value):
        if isinstance(value, int) and value <= 0:
            return
        eng.wait_ge(s, value)

    def need_apart(eng, *waits):
        for s, v in waits:
            need(eng, s, v)
            eng.sem_inc(S["apart"], 1)

    def f32(ap):
        return ap.bitcast(F32)

    stream = nc.dram_tensor("stream", (2 * ROUNDS, N, D), F32, kind="Internal").ap()
    x_mid = nc.dram_tensor("x_mid", (2, B, N, D), F32, kind="Internal").ap()

    def tokens(ap, row):
        if isinstance(row, int):
            return ap[row].rearrange("(t p) d -> p t d", p=P)
        return ap[bass.ds(row, 1)].rearrange("o (t p) d -> p (o t) d", p=P)

    ident = sb("ident", [P, P])
    mask = sb("mask", [P, 2 * P])
    minus_half = sb("minus_half", [P, 2 * HEADS])
    rope = sb("rope", [P, 4, NT, DH])
    qks = sb("qks", [P, 2, DH])
    lnp = sb("lnp", [P, 2, KD])
    b1t = sb("b1t", [P, 2 * (FJ + 1)])
    wqkv_s = [sb(f"wqkv_{s}", [P, KD, 3 * INNER], F32R) for s in ("hi", "lo")]
    wo_s = [sb(f"wo_{s}", [P, PAIRS, D], F32R) for s in ("hi", "lo")]
    w1_s = [sb(f"w1_{s}", [P, KD, 2 * HID], F32R) for s in ("hi", "lo")]
    w2_s = [sb(f"w2_{s}", [P, FJ + 1, D], F32R) for s in ("hi", "lo")]
    probs = sb("probs", [P, 3, NT, 2 * P])
    flat = probs[:].rearrange("p a b c -> p a (b c)")
    m2 = [[flat[:, w, r * N:(r + 1) * N] for r in range(2)] for w in range(2)]
    sq = [flat[:, 2, 0:N], flat[:, 2, N:2 * N]]
    raw = flat.rearrange("p a b -> p (a b)")

    ffn_mem = ExitStack()
    with ExitStack() as first:
        x_all = sb("x_all", [P, B * NT, D], c=first)
        st0 = sb("st0", [P, B * NT, 6], c=first)
        mv0 = sb("mv0", [P, B * NT, 2], c=first)
        ve0 = sb("ve0", [P, B * NT], c=first)
        rs0 = sb("rs0", [P, B * NT], c=first)
        half0 = sb("half0", [P, B * NT], c=first)
    xnext = sb("xnext", [P, NT, D], c=ffn_mem)
    xin = sb("xin", [P, NT, D], c=ffn_mem)
    xmid = sb("xmid", [P, NT, D], c=ffn_mem)
    nrm = sb("nrm", [P, NT, D], c=ffn_mem)
    hT = [sb(f"hT_{s}", [P, KD, N], F32R, ffn_mem) for s in ("hi", "lo")]
    nT = [sb(f"nT_{s}", [P, KD, N], F32R, ffn_mem) for s in ("hi", "lo")]
    turned_qk = sb("turned_qk", [P, 2, 2, INNER], c=ffn_mem)
    m1 = [[turned_qk[:, w, r, :] for r in range(2)] for w in range(2)]
    qT = sb("qT", [P, PAIRS, N], c=ffn_mem)
    kT = sb("kT", [P, PAIRS, N], c=ffn_mem)
    v_s = [sb(f"v_{s}", [P, NT, PAIRS, 3 * DH], F32R, ffn_mem) for s in ("hi", "lo")]
    pT = [sb(f"pT_{s}", [P, 2, 7 * P], F32R, ffn_mem) for s in ("hi", "lo")]
    oT = [sb(f"oT_{s}", [P, 2, N], F32R, ffn_mem) for s in ("hi", "lo")]
    gate = sb("gate", [P, 2, N], c=ffn_mem)
    hid = sb("hid", [P, 2, N], c=ffn_mem)
    hid_r = sb("hid_r", [P, N], c=ffn_mem)
    ssq = sb("ssq", [P, NT, 2 * HEADS], c=ffn_mem)
    rinv = sb("rinv", [P, NT, 2 * HEADS], c=ffn_mem)
    rq = sb("rq", [P, 2, NT, HEADS], c=ffn_mem)
    mx = sb("mx", [P, HEADS, NT], c=ffn_mem)
    nb = sb("nb", [P, HEADS, NT], c=ffn_mem)
    zs = sb("zs", [P, HEADS, NT], c=ffn_mem)
    rz = sb("rz", [P, HEADS, NT], c=ffn_mem)
    st = sb("st", [P, NT, 2, 6], c=ffn_mem)
    mv = sb("mv", [P, NT, 2], c=ffn_mem)
    ve = sb("ve", [P, NT], c=ffn_mem)
    rs = sb("rs", [P, NT], c=ffn_mem)
    wbuf = sb("wbuf", [P, 3 * INNER], c=ffn_mem)
    WBUF = [wbuf[:], kT[:].rearrange("p a n -> p (a n)")[:, 0:3 * INNER]]
    ffn_mem.close()

    glb_mem = ExitStack()
    gw = [sb(f"gw_{s}", [P, GH * KD, D], F32R, glb_mem) for s in ("hi", "lo")]
    gx = [sb(f"gx{r}", [P, NT, D], c=glb_mem) for r in range(2)]
    flat_w1, flat_w2 = [[w_[:].rearrange("p k d -> p (k d)") for w_ in ws] for ws in (w1_s, w2_s)]
    gy0 = [sb(f"gy_{s}", [P, NT, D], F32R, glb_mem)[:] for s in ("hi", "lo")]
    gy = [gy0, [w_[:, 0:NT * D].rearrange("p (t d) -> p t d", d=D) for w_ in flat_w2]]
    goT = [[w_[:, r * KD * N:(r + 1) * KD * N].rearrange("p (c n) -> p c n", n=N) for w_ in flat_w1]
           for r in range(2)]
    ga = raw[:, 0:2 * NT * GH * GS].rearrange("p (s t h c g) -> p s t h c g", s=2, t=NT, h=GH // 4, c=4)
    gaT = sb("gaT", [P, 2, 2, N], F32R, glb_mem)
    ge = sb("ge", [P, 4, N], c=glb_mem)
    ges = [sb(f"ge_{s}", [P, 4, N], F32R, glb_mem) for s in ("hi", "lo")]
    gz = sb("gz", [P, GH, NT], c=glb_mem)
    grz = sb("grz", [P, GH, NT], c=glb_mem)
    gst = sb("gst", [P, NT, 6], c=glb_mem)
    gmv = sb("gmv", [P, NT, 2], c=glb_mem)
    gve = sb("gve", [P, NT], c=glb_mem)
    grs = sb("grs", [P, NT], c=glb_mem)
    gn = sb("gn", [P, NT, D], c=glb_mem)
    gout = sb("gout", [P, NT, D], c=glb_mem)
    G_WBUF = [raw[:, 0:3 * INNER], raw[:, 3 * INNER:6 * INNER]]
    glb_mem.close()

    psum = ctx.enter_context(nc.psum_tensor("psum", [P, 8, N], F32))
    RB = [psum[:, 0, :], psum[:, 1, :]]
    TB = [psum[:, 2, :], psum[:, 3, :]]
    AV = psum[:, 4, :]
    UB = psum[:, 5, :]
    ACC = [psum[:, 6, :], psum[:, 7, :]]

    names = """apart consts x0_in x0_stats x0_var x0_rs x0_z stage
        w_in0 w_in1 w_hi w_lo w_small rope_ok bias_mm bias_ok
        x_in x_stored shift_in xold_in
        pe_z pe_qkv pe_qk_t pe_s pe_p pe_av pe_wo pe_n pe_w1 pe_w2
        act_x act_z act_sq act_v act_qk act_exp act_p act_av act_n act_gate act_u
        dve_z dve_rope dve_sum dve_ssq dve_v dve_rq dve_add dve_ksum dve_k dve_s dve_nb dve_rz dve_p dve_av dve_wo
        dve_st dve_mv dve_var dve_n dve_nlo dve_hid dve_w2
        pool_r pool_q pool_n pool_rs pool_u
        g_in g_sum g_out g_st g_mv g_var g_rs g_y g_yhi g_ylo g_pack g_t g_tc g_s g_exp g_hi g_lo g_o g_ohi g_olo
        g_rz g_w g_acc g_st2 g_mv2 g_var2 g_rs2 g_z""".split()
    S = {n: sem(n) for n in names}

    def stage_end(eng, k):
        eng.drain().then_inc(S["stage"], 1)
        eng.wait_ge(S["stage"], 5 * (k + 1))

    block = ctx.enter_context(nc.Block())

    def before(step, kinds):
        earlier = [x_ for x_ in PHASE1[:PHASE1.index(step)] if x_[0] in kinds]
        return earlier[-1] if earlier else None

    def rounds(eng, call, prep, early, a_round, w_a, w_f, last_f):
        n0 = call * ROUNDS
        w_a(2 * call)
        w_f(2 * call)
        prep(n0, None)
        first_steps = sum(EARLY.values(), [])
        early(n0, first_steps)
        a_round(n0, f=None, final=False, nxt="first", ahead=True)
        a_round(n0 + 1, f=n0, final=False, nxt="loop0", ahead=True)
        with eng.Fori(n0 + 2, n0 + B - 1) as n:
            a_round(n, f=n - 1, final=False, nxt="loop0", ahead=True)
        a_round(n0 + B - 1, f=n0 + B - 2, final=False, nxt="loop0", ahead=False)
        w_a(2 * call + 1)
        early(n0 + B, first_steps)
        a_round(n0 + B, f=n0 + B - 1, final=False, nxt="loop1", ahead=True)
        w_f(2 * call + 1)
        with eng.Fori(n0 + B + 1, n0 + ROUNDS - 1) as n:
            a_round(n, f=n - 1, final=True, nxt="loop1", ahead=True)
        a_round(n0 + ROUNDS - 1, f=n0 + ROUNDS - 2, final=True, nxt=None, ahead=False)
        last_f(n0 + ROUNDS - 1)

    W_A, W_F = 3, 3
    G_CHUNKS = 8
    G_COLS = GH * KD // G_CHUNKS

    def w_base(stage):
        return stage * (W_A + W_F) + (G_CHUNKS if stage >= 2 else 0)

    G_BASE = 2 * (W_A + W_F)
    CHUNK_DMAS = [1, 1, 1, 1, 1, 3] * 2 + [1] * G_CHUNKS + [1, 1, 1, 1, 1, 3] * 2

    def chunk_in(eng, k):
        eng.wait_ge(S[f"w_in{k % 2}"], 16 * sum(CHUNK_DMAS[k % 2:k + 1:2]))

    def weights_done(eng, k):
        eng.wait_ge(S["w_lo"], k)

    G_STEPS = GH * NT

    def sequences(eng, body):
        body(0, 0, "first")
        with eng.Fori(0, B // 2 - 1) as pair:
            body(2 * pair + 1, 1, "middle")
            body(2 * pair + 2, 0, "middle")
        body(B - 1, 1, "last")

    def steps(which, tail):
        return range(G_STEPS + (tail if which == "last" else 0))

    def back(b, r, which, k, lag):
        if k >= lag:
            return (b, r, k - lag) if k - lag < G_STEPS else (None, None, None)
        return (None, None, None) if which == "first" else (b - 1, 1 - r, k - lag + G_STEPS)

    LAG_O = 2
    LAG_W = LAG_O + NT
    LAG_OUT = 5 - (NT - 1)
    LAG_ADD = 11 - (NT - 1)
    LAG_END = LAG_ADD + 1
    TAIL = LAG_END + 4
    NEXT_ST, NEXT_VAR, NEXT_POW, NEXT_N, NEXT_HI, NEXT_LO = 24, 26, 26, 28, 30, 32
    END_ST, END_VAR, END_POW, END_N = LAG_END, LAG_END + 1, LAG_END + 1, LAG_END + 3

    @block.sync
    def _(sp):
        for b in range(B):
            sp.dma_start(x_all[:, b * NT:(b + 1) * NT, :], tokens(x, b)).then_inc(S["x0_in"], 16)
        for b in range(B):
            sp.wait_ge(S["x0_z"], NT * (b + 1))
            sp.dma_start(tokens(stream, b), x_all[:, b * NT:(b + 1) * NT, :]).then_inc(S["x0_in"], 16)
        sp.wait_ge(S["x0_in"], 16 * 2 * B)
        stage_end(sp, 0)

        def chunk(k, dst_src):
            if k >= 2:
                sp.wait_ge(S["w_lo"], k - 1)
            for dst, src in dst_src:
                sp.dma_start(dst, src).then_inc(S[f"w_in{k % 2}"], 16)

        def w_a(stage):
            l, k = stage % LAYERS, w_base(stage)
            if stage:
                sp.wait_ge(S["dve_rope"], 2 * NT * B * stage)
                sp.wait_ge(S["pe_s"], 2 * HEADS * B * stage)
            sp.dma_start(rope[:], tables).then_inc(S["w_small"], 16)
            for i, ap in enumerate((q_scale, k_scale)):
                sp.dma_start(qks[:, i, :], ap[l:l + 1, :].to_broadcast([P, DH])).then_inc(S["w_small"], 16)
            for kt in range(KD):
                chunk(k + kt, [(WBUF[(k + kt) % 2], wqkv[l, kt * P:(kt + 1) * P, :])])
            chunk(k + 2, [(WBUF[(k + 2) % 2][:, 0:PAIRS * D].rearrange("p (k d) -> p k d", d=D),
                           wo[l].rearrange("(k p) d -> p k d", p=P))])

        def w_f(stage):
            l, k = stage % LAYERS, w_base(stage) + W_A
            if stage % LAYERS:
                sp.wait_ge(S["pe_s"], 2 * HEADS * (B * stage + 1))
                sp.wait_ge(S["dve_w2"], 2 * B * stage)
            sp.dma_start(lnp[:, 0, :], ln_g[l].rearrange("(k p) -> p k", p=P)).then_inc(S["w_small"], 16)
            sp.dma_start(lnp[:, 1, :], ln_b[l].rearrange("(k p) -> p k", p=P)).then_inc(S["w_small"], 16)
            b1v = b1t[:].rearrange("p (j c) -> p c j", c=2)
            for c in range(2):
                lo = HID * (1 - c)
                sp.dma_start(b1v[:, c, 0:FJ], b1[l, lo:lo + FJ * P].rearrange("(j p) -> p j", p=P)
                             ).then_inc(S["w_small"], 16)
                sp.dma_start(b1v[0:HR, c, FJ:FJ + 1], b1[l, lo + FJ * P:lo + HID].rearrange("(p o) -> p o", o=1)
                             ).then_inc(S["w_small"], 16)
            for kt in range(KD):
                chunk(k + kt, [(WBUF[(k + kt) % 2][:, 0:2 * HID], w1[l, kt * P:(kt + 1) * P, :])])
            v = WBUF[(k + 2) % 2].rearrange("p (k d) -> p k d", d=D)
            sp.wait_ge(S["bias_mm"], stage + 1)
            chunk(k + 2, [(v[:, 0:FJ, :], w2[l, 0:FJ * P, :].rearrange("(k p) d -> p k d", p=P)),
                          (v[0:HR, FJ, :], w2[l, FJ * P:HID, :]), (v[HR:HR + 1, FJ, :], b2[l:l + 1, :])])

        def prep(n, stored):
            waits = [(S["pe_z"], KD * n), (S["act_x"], n)]
            if stored is not None:
                waits.append((S["x_stored"], stored))
            need_apart(sp, *waits)
            sp.dma_start(xnext[:], tokens(stream, n)).then_inc(S["x_in"], 16)

        def f_part(m, final):
            sp.wait_ge(S["dve_wo"], 2 * m + 2)
            need(sp, S["pe_n"], KD * m)
            need(sp, S["dve_w2"], 2 * m)
            sp.dma_start(nrm[1:P, :, P:D], xmid[0:P - 1, :, P:D]).then_inc(S["shift_in"], 16)
            sp.dma_start(nrm[0:1, 1:NT, P:D], xmid[P - 1:P, 0:NT - 1, P:D]).then_inc(S["shift_in"], 16)
            return final

        def f_tail(m, final, call):
            if final:
                need_apart(sp, (S["pe_n"], KD * (m + 1)))
                before = x if call == 0 else x_mid[1]
                sp.dma_start(nrm[:], tokens(before, m - call * ROUNDS - B)).then_inc(S["xold_in"], 16)
            need_apart(sp, (S["dve_w2"], 2 * m + 2))
            if final:
                after = x_mid[0] if call == 0 else out
                sp.dma_start(tokens(after, m - call * ROUNDS - B), xmid[:]).then_inc(S["x_stored"], 16)
            else:
                sp.dma_start(tokens(stream, m + B), xmid[:]).then_inc(S["x_stored"], 16)

        for call in range(2):
            def a_round(n, f, final, nxt, ahead, call=call):
                if f is not None:
                    f_part(f, final)
                if nxt:
                    prep(n + 1, {"first": None, "loop0": 16 * (n - 1), "loop1": 16 * (n - 6)}[nxt])
                if f is not None:
                    f_tail(f, final, call)

            def last_f(m, call=call):
                f_part(m, True)
                f_tail(m, True, call)
                sp.wait_ge(S["x_stored"], 16 * (m + 1))
                stage_end(sp, 1 + 2 * call)

            rounds(sp, call, prep, lambda n, todo: None, a_round, w_a, w_f, last_f)
            if call == 0:
                for c in range(G_CHUNKS):
                    chunk(G_BASE + c, [(G_WBUF[(G_BASE + c) % 2][:, 0:G_COLS * D].rearrange("p (k d) -> p k d", d=D),
                                        g_w[c * G_COLS * P:(c + 1) * G_COLS * P, :].rearrange("(k p) d -> p k d", p=P))])
                sp.sem_inc(S["g_out"], 1)
                for b in range(2):
                    sp.dma_start(gx[b][:], tokens(x_mid[0], b)).then_inc(S["g_in"], 16)

                def store(b, r):
                    need_apart(sp, (S["g_acc"], NT * GH * (b + 1)))
                    sp.dma_start(tokens(x_mid[1], b), gx[r][:]).then_inc(S["g_sum"], 16)
                    need_apart(sp, (S["g_z"], b + 1))
                    sp.dma_start(tokens(stream, b + ROUNDS), gout[:]).then_inc(S["g_out"], 16)

                def sequence(b, r, which):
                    if which != "first":
                        store(b - 1, 1 - r)
                        if which != "last":
                            need_apart(sp, (S["g_sum"], 16 * b))
                            sp.dma_start(gx[1 - r][:], tokens(x_mid[0], b + 1)).then_inc(S["g_in"], 16)

                sequences(sp, sequence)
                store(B - 1, 1)
                sp.wait_ge(S["g_sum"], 16 * B)
                sp.wait_ge(S["g_out"], 16 * B + 1)
                stage_end(sp, 2)

    @block.gpsimd
    def _(pool):
        nc.gpsimd.memset(ident[:], 0.0)
        nc.gpsimd.memset(mask[:], 0.0)
        nc.gpsimd.memset(half0[:], -0.5)
        nc.gpsimd.memset(minus_half[:], -0.5).then_inc(S["consts"], 1)
        pool.wait_ge(S["consts"], 1)
        nc.gpsimd.affine_select(out=ident[:], in_=ident[:], compare_op=ALU.not_equal, fill=1.0, base=0,
                                pattern=[[-1, P]], channel_multiplier=1)
        nc.gpsimd.affine_select(out=mask[:, 0:P], in_=mask[:, 0:P], compare_op=ALU.is_ge, fill=MASKED, base=0,
                                pattern=[[1, P]], channel_multiplier=-1)
        nc.gpsimd.affine_select(out=mask[:, P:2 * P], in_=mask[:, P:2 * P], compare_op=ALU.is_ge, fill=MASKED,
                                base=0, pattern=[[-1, P]], channel_multiplier=1).then_inc(S["consts"], 1)
        pool.wait_ge(S["x0_var"], 1)
        pool.wait_ge(S["consts"], 2)
        nc.gpsimd.tensor_tensor(rs0[:], ve0[:], half0[:], ALU.pow).then_inc(S["x0_rs"], 1)
        stage_end(pool, 0)

        def prep(n, stored):
            pass

        def w_a(stage):
            pass

        def w_f(stage):
            pass

        def phase1(n, m, todo=PHASE1):
            for step in todo:
                kind, i = step[0], int(step[1])
                if kind == "b" and n is not None:
                    r = i % 2
                    pool.wait_ge(S["dve_rope"], 2 * (NT * n + i) + 1)
                    nc.gpsimd.tensor_tensor(m1[0][r], m1[0][r], m2[0][r], ALU.add).then_inc(S["pool_q"], 1)
                if kind == "s" and n is not None:
                    pool.wait_ge(S["dve_ssq"], NT * n + i + 1)
                    need(pool, S["act_exp"], HEADS * n)
                    nc.gpsimd.tensor_tensor(rinv[:, i, :], ssq[:, i, :], minus_half[:], ALU.pow
                                            ).then_inc(S["pool_r"], 1)
                if m is None:
                    continue
                if kind == "l":
                    pool.wait_ge(S["dve_var"], m + 1)
                    nc.gpsimd.tensor_tensor(rs[:], ve[:], minus_half[:, 0:NT], ALU.pow).then_inc(S["pool_rs"], 1)
                if kind == "u":
                    hr, s = (hid[:, i % 2, :], P) if i < FJ else (hid_r[0:HR + 1, :], HR + 1)
                    pool.wait_ge(S["act_u"], (FJ + 1) * m + i + 1)
                    nc.gpsimd.tensor_tensor(pT[1][0:s, i % 2, 0:N], hr, f32(pT[0][0:s, i % 2, 0:N]), ALU.subtract
                                            ).then_inc(S["pool_u"], 1)

        def early(n, todo):
            phase1(n, None, todo)

        def a_round(n, f, final, nxt, ahead):
            phase1(n, f)
            for h in range(HEADS):
                need_apart(pool, (S["dve_rz"], HEADS * n + h + 1))
                for i in range(NT):
                    a = P if i == 0 else 0
                    last = nc.gpsimd.tensor_scalar(probs[:, h % 3, i, a:], probs[:, h % 3, i, a:], rz[:, h, i:i + 1],
                                                   1.0, ALU.mult, ALU.mult)
                last.then_inc(S["pool_n"], 1)

        for call in range(2):
            def last_f(m, call=call):
                phase1(None, m)
                stage_end(pool, 1 + 2 * call)

            rounds(pool, call, prep, early, a_round, w_a, w_f, last_f)
            if call == 0:
                def power(s_in, s_out, b):
                    pool.wait_ge(S[s_in], b + 1)
                    nc.gpsimd.tensor_tensor(grs[:], gve[:], minus_half[:, 0:NT], ALU.pow).then_inc(S[s_out], 1)

                def sequence(b, r, which):
                    for k in steps(which, TAIL):
                        if k < G_STEPS:
                            pool.wait_ge(S["g_hi"], G_STEPS * b + k + 1)
                            if which != "first" or k >= 4:
                                pool.wait_ge(S["g_o"], KD * (G_STEPS * b + k - 3))
                            nc.gpsimd.tensor_tensor(ges[1][:, k % 4, :], ge[:, k % 4, :], f32(ges[0][:, k % 4, :]),
                                                    ALU.subtract).then_inc(S["g_lo"], 1)
                        if k == NEXT_POW and which != "last":
                            power("g_var", "g_rs", b + 1)
                        c, _, kk = back(b, r, which, k, END_POW)
                        if kk == G_STEPS - 1:
                            power("g_var2", "g_rs2", c)

                power("g_var", "g_rs", 0)
                sequences(pool, sequence)
                stage_end(pool, 2)

    @block.scalar
    def _(act):
        copy = nc.scalar.copy
        stage_end(act, 0)

        def split_hi(k, outs):
            chunk_in(act, k)
            for o, i, scale in outs:
                if scale is None:
                    last = copy(o, i)
                else:
                    last = nc.scalar.activation(o, i, ACT.Copy, scale=scale)
            last.then_inc(S["w_hi"], 1)

        def w_a(stage):
            k = w_base(stage)
            need(act, S["pe_qkv"], 12 * B * stage)
            need(act, S["pe_wo"], PAIRS * B * stage)
            for kt in range(KD):
                split_hi(k + kt, [(wqkv_s[0][:, kt, :], WBUF[(k + kt) % 2], None)])
            split_hi(k + 2, [(wo_s[0][:].rearrange("p k d -> p (k d)"), WBUF[(k + 2) % 2][:, 0:PAIRS * D], None)])
            weights_done(act, k + W_A)

        def w_f(stage):
            k = w_base(stage) + W_A
            need(act, S["dve_w2"], 2 * B * stage)
            act.wait_ge(S["w_small"], 16 * (9 * stage + 9))
            for kt in range(KD):
                split_hi(k + kt, [(w1_s[0][:, kt, :], WBUF[(k + kt) % 2][:, 0:2 * HID], lnp[:, 0, kt:kt + 1])])
            v = WBUF[(k + 2) % 2].rearrange("p (k d) -> p k d", d=D)
            split_hi(k + 2, [(w2_s[0][:, 0:FJ, :], v[:, 0:FJ, :], None),
                             (w2_s[0][0:HR + 1, FJ, :], v[0:HR + 1, FJ, :], None)])
            weights_done(act, k + W_F)

        def prep(n, stored):
            need(act, S["pe_qkv"], 12 * n)
            for half in range(KD):
                act.wait_ge(S["pe_z"], KD * n + half + 1)
                if half == 0:
                    copy(hT[0][:, 0, :], TB[0]).then_inc(S["act_z"], 1)
                else:
                    copy(hT[0][:, 1, 1:N], TB[1][:, 0:N - 1]).then_inc(S["act_z"], 1)

        def phase1(n, m, todo=PHASE1):
            for step in todo:
                kind, i = step[0], int(step[1])
                if n is not None:
                    if kind == "x":
                        act.wait_ge(S["x_in"], 16 * (n + 1))
                        need(act, S["dve_wo"], 2 * n)
                        copy(xin[:], xnext[:]).then_inc(S["act_x"], 1)
                    if kind in "qk":
                        w = "qk".index(kind)
                        act.wait_ge(S["dve_rope"], 2 * (NT * n + i) + w + 1)
                        if i == 0:
                            need(act, S["pe_p"], 2 * HEADS * n)
                        else:
                            act.wait_ge(S["dve_sum"], 2 * (NT * n + i) - 1 + w)
                        nc.scalar.activation(sq[w], RB[(3 * i + w) % 2], ACT.Square).then_inc(S["act_sq"], 1)
                    if kind == "v":
                        act.wait_ge(S["pe_qkv"], 12 * n + 3 * i + 3)
                        need(act, S["pe_av"], HEADS * n)
                        copy(v_s[0][:, i].rearrange("p a (s d) -> p a s d", s=3)[:, :, ::2, :],
                             RB[(3 * i + 2) % 2].rearrange("p (a s d) -> p a s d", a=PAIRS, s=2)).then_inc(S["act_v"], 1)
                    if kind in "QK":
                        w = "QK".index(kind)
                        act.wait_ge(S["pe_qk_t"], 2 * (NT * n + i) + w + 1)
                        need(act, S["pe_s"], 2 * HEADS * n)
                        copy((qT, kT)[w][:, :, i * P:(i + 1) * P],
                             TB[(2 * i + w) % 2].rearrange("p (a q) -> p a q", a=PAIRS)).then_inc(S["act_qk"], 1)
                if m is not None:
                    if kind == "n":
                        need(act, S["pe_w1"], 12 * m)
                        for half in range(KD):
                            act.wait_ge(S["pe_n"], KD * m + half + 1)
                            copy(nT[0][:, half, :], TB[half]).then_inc(S["act_n"], 1)
                    if kind == "g":
                        s = P if i < FJ else HR
                        act.wait_ge(S["pe_w1"], 12 * m + 2 * i + 1)
                        act.wait_ge(S["bias_ok"], 1)
                        need(act, S["dve_hid"], (FJ + 1) * m + max(i - 1, 0))
                        nc.scalar.activation(gate[0:s, i % 2, :], UB[0:s, :], ACT.Gelu,
                                             bias=b1t[0:s, 2 * i:2 * i + 1]).then_inc(S["act_gate"], 1)
                    if kind == "u":
                        hr, s = (hid[:, i % 2, :], P) if i < FJ else (hid_r[0:HR + 1, :], HR + 1)
                        act.wait_ge(S["dve_hid"], (FJ + 1) * m + i + 1)
                        if i < 2:
                            act.wait_ge(S["pe_av"], HEADS * (m + 1))
                        else:
                            act.wait_ge(S["pe_w2"], (FJ + 1) * m + i - 1)
                        copy(pT[0][0:s, i % 2, 0:N], hr).then_inc(S["act_u"], 1)

        def early(n, todo):
            phase1(n, None, todo)

        def a_round(n, f, final, nxt, ahead):
            phase1(n, f)
            for s in range(SLOTS):
                if 0 <= s - 2 < HEADS:
                    h = s - 2
                    for half in range(2):
                        act.wait_ge(S["pe_p"], 2 * (HEADS * n + h) + half + 1)
                        if half == 0 and h >= 2:
                            act.wait_ge(S["pe_av"], HEADS * n + h - 1)
                        elif half == 0 and f is not None:
                            act.wait_ge(S["pe_w2"], (FJ + 1) * (f + 1))
                        w = 4 * P if half == 0 else 3 * P
                        copy(pT[0][:, h % 2, half * 4 * P:half * 4 * P + w], TB[half][:, 0:w]).then_inc(S["act_p"], 1)
                if s in AV_OUT:
                    p = AV_OUT.index(s)
                    act.wait_ge(S["pe_av"], HEADS * n + 2 * p + 2)
                    if p >= 2:
                        act.wait_ge(S["pe_wo"], PAIRS * n + p - 1)
                    copy(oT[0][:, p % 2, :], AV).then_inc(S["act_av"], 1)
                if s < HEADS:
                    act.wait_ge(S["dve_nb"], HEADS * n + s + 1)
                    if s == 0:
                        act.wait_ge(S["dve_rq"], n + 1)
                    for i in range(NT):
                        a = P if i == 0 else 0
                        last = nc.scalar.activation(probs[:, s % 3, i, a:], probs[:, s % 3, i, a:], ACT.Exp,
                                                    bias=nb[:, s, i:i + 1], scale=rq[:, 0, i, s:s + 1],
                                                    accum_out=zs[:, s, i:i + 1])
                    last.then_inc(S["act_exp"], 1)
                if s == PREP and nxt:
                    prep(n + 1, None)
                if s in EARLY and ahead:
                    early(n + 1, EARLY[s])

        for call in range(2):
            def last_f(m, call=call):
                phase1(None, m)
                stage_end(act, 1 + 2 * call)

            rounds(act, call, prep, early, a_round, w_a, w_f, last_f)
            if call == 0:
                for c in range(G_CHUNKS):
                    k = G_BASE + c
                    split_hi(k, [(gw[0][:, c * G_COLS:(c + 1) * G_COLS, :].rearrange("p k d -> p (k d)"),
                                  G_WBUF[k % 2][:, 0:G_COLS * D], None)])
                weights_done(act, G_BASE + G_CHUNKS)
                def y_hi(b, r):
                    act.wait_ge(S["g_y"], b + 1)
                    need(act, S["g_o"], KD * G_STEPS * (b - 1))
                    copy(gy[r][0].rearrange("p t d -> p (t d)"), gn[:].rearrange("p t d -> p (t d)")
                         ).then_inc(S["g_yhi"], 1)

                def turned(b, pp):
                    for side in range(2):
                        act.wait_ge(S["g_t"], GH * b + 2 * pp + side + 1)
                        need(act, S["g_s"], G_STEPS * b + 8 * (pp - 1))
                        copy(gaT[:, pp % 2, side, :], TB[side]).then_inc(S["g_tc"], 1)

                def sequence(b, r, which):
                    for k in steps(which, TAIL):
                        if k % 8 == 2 and k < G_STEPS:
                            pp = k // 8 + 1
                            if pp < GH // 2:
                                turned(b, pp)
                            elif which != "last":
                                turned(b + 1, 0)
                        if k < G_STEPS:
                            h, t = k // NT, k % NT
                            act.wait_ge(S["g_s"], G_STEPS * b + k + 1)
                            if which != "first" or k >= 4:
                                act.wait_ge(S["g_lo"], G_STEPS * b + k - 3)
                            nc.scalar.activation(ge[:, k % 4, :], RB[k % 2], ACT.Exp, scale=GSCALE,
                                                 accum_out=gz[:, h, t:t + 1]).then_inc(S["g_exp"], 1)
                        c, _, kk = back(b, r, which, k, LAG_OUT)
                        if kk is not None and kk % NT == NT - 1:
                            h = kk // NT
                            for half in range(KD):
                                act.wait_ge(S["g_o"], KD * (NT * (GH * c + h) + NT - 1) + half + 1)
                                need(act, S["g_w"], GH * c + h - 1)
                                copy(goT[h % 2][0][:, half, :], psum[:, 4 + half, :]).then_inc(S["g_ohi"], 1)
                        if k == NEXT_HI and which != "last":
                            y_hi(b + 1, 1 - r)

                y_hi(0, 0)
                turned(0, 0)
                sequences(act, sequence)
                stage_end(act, 2)

    @block.vector
    def _(dve):
        V = nc.vector
        for b in range(B):
            dve.wait_ge(S["x0_in"], 16 * B)
            for t in range(b * NT, (b + 1) * NT):
                V.bn_stats(st0[:, t, :], x_all[:, t, :]).then_inc(S["x0_stats"], 1)
        dve.wait_ge(S["x0_stats"], B * NT)
        for t in range(B * NT):
            V.bn_aggr(mv0[:, t, :], st0[:, t, :]).then_inc(S["x0_stats"], 1)
        dve.wait_ge(S["x0_stats"], 2 * B * NT)
        V.tensor_scalar(ve0[:], mv0[:, :, 1], EPS, None, ALU.add).then_inc(S["x0_var"], 1)
        dve.wait_ge(S["x0_rs"], 1)
        for t in range(B * NT):
            V.tensor_scalar(x_all[:, t, :], x_all[:, t, :], mv0[:, t, 0:1], rs0[:, t:t + 1], ALU.subtract, ALU.mult
                            ).then_inc(S["x0_z"], 1)
        stage_end(dve, 0)

        def split_lo(k, outs):
            dve.wait_ge(S["w_hi"], k + 1)
            for lo, hi, i, scale in outs:
                if scale is None:
                    last = V.tensor_tensor(lo, i, f32(hi), ALU.subtract)
                else:
                    last = V.scalar_tensor_tensor(lo, i, scale, f32(hi), ALU.mult, ALU.subtract)
            last.then_inc(S["w_lo"], 1)

        def w_a(stage):
            k = w_base(stage)
            if stage % LAYERS == 0:
                V.memset(f32(v_s[0][:]), 0.0)
                V.memset(f32(v_s[1][:]), 0.0)
                V.memset(f32(hT[0][:, 1, 0:1]), 0.0)
                V.memset(f32(hT[1][:, 1, 0:1]), 0.0)
                V.memset(hid_r[:], 1.0)
            dve.wait_ge(S["w_small"], 16 * (9 * stage + 3))
            for i in range(2):
                V.tensor_tensor(rope[:, 2 * i], rope[:, 2 * i], qks[:, i].unsqueeze(1).to_broadcast([P, NT, DH]), ALU.mult)
                for half in range(2):
                    a, o = half * DH // 2, (1 - half) * DH // 2
                    last = V.tensor_tensor(rope[:, 2 * i + 1, :, a:a + DH // 2], rope[:, 2 * i + 1, :, a:a + DH // 2],
                                           qks[:, i, o:o + DH // 2].unsqueeze(1).to_broadcast([P, NT, DH // 2]), ALU.mult)
            last.then_inc(S["rope_ok"], 1)
            for kt in range(KD):
                split_lo(k + kt, [(wqkv_s[1][:, kt, :], wqkv_s[0][:, kt, :], WBUF[(k + kt) % 2], None)])
            flat_wo = [w[:].rearrange("p k d -> p (k d)") for w in wo_s]
            split_lo(k + 2, [(flat_wo[1], flat_wo[0], WBUF[(k + 2) % 2][:, 0:PAIRS * D], None)])
            dve.wait_ge(S["rope_ok"], stage + 1)

        def w_f(stage):
            k = w_base(stage) + W_A
            for kt in range(KD):
                split_lo(k + kt, [(w1_s[1][:, kt, :], w1_s[0][:, kt, :], WBUF[(k + kt) % 2][:, 0:2 * HID],
                                   lnp[:, 0, kt:kt + 1])])
            v = WBUF[(k + 2) % 2].rearrange("p (k d) -> p k d", d=D)
            split_lo(k + 2, [(w2_s[1][:, 0:FJ, :], w2_s[0][:, 0:FJ, :], v[:, 0:FJ, :], None),
                             (w2_s[1][0:HR + 1, FJ, :], w2_s[0][0:HR + 1, FJ, :], v[0:HR + 1, FJ, :], None)])
            dve.wait_ge(S["bias_mm"], stage + 1)
            V.tensor_tensor(b1t[:, 0:2 * FJ], b1t[:, 0:2 * FJ], UB[:, 0:2 * FJ], ALU.add)
            V.tensor_tensor(b1t[0:HR, 2 * FJ:], b1t[0:HR, 2 * FJ:], UB[0:HR, 2 * FJ:2 * FJ + 2], ALU.add
                            ).then_inc(S["bias_ok"], 1)
            dve.wait_ge(S["bias_ok"], stage + 1)

        def prep(n, stored):
            for half in range(KD):
                dve.wait_ge(S["act_z"], KD * n + half + 1)
                a = half
                V.tensor_tensor(hT[1][:, half, a:N], TB[half][:, 0:N - a], f32(hT[0][:, half, a:N]), ALU.subtract
                                ).then_inc(S["dve_z"], 1)

        def phase1(n, m, final, todo=PHASE1):
            for step in todo:
                kind, i = step[0], int(step[1])
                if n is not None:
                    if kind in "qk":
                        w = "qk".index(kind)
                        dve.wait_ge(S["pe_qkv"], 12 * n + 3 * i + w + 1)
                        if i < 2:
                            need(dve, S["pe_p"], 2 * HEADS * n)
                        else:
                            dve.wait_ge(S["pe_qk_t"], 2 * (NT * n + i) - 3 + w)
                        src = RB[(3 * i + w) % 2]
                        h64 = "p (h d) -> p h d"
                        V.tensor_tensor(m1[w][i % 2].rearrange(h64, h=HEADS), src.rearrange(h64, h=HEADS),
                                        rope[:, 2 * w, i].unsqueeze(1).to_broadcast([P, HEADS, DH]), ALU.mult)
                        h232 = "p (h s d) -> p h s d"
                        sin = rope[:, 2 * w + 1, i].rearrange("p (s d) -> p s d", s=2)
                        V.tensor_tensor(m2[w][i % 2].rearrange(h232, h=HEADS, s=2), src.rearrange(h232, h=HEADS, s=2)[:, :, ::-1, :],
                                        sin.unsqueeze(1).to_broadcast([P, HEADS, 2, DH // 2]), ALU.mult
                                        ).then_inc(S["dve_rope"], 1)
                    if kind == "v":
                        dve.wait_ge(S["act_v"], NT * n + i + 1)
                        v3 = [v[:, i].rearrange("p a (s d) -> p a s d", s=3)[:, :, ::2, :] for v in v_s]
                        V.tensor_tensor(v3[1], RB[(3 * i + 2) % 2].rearrange("p (a s d) -> p a s d", a=PAIRS, s=2),
                                        f32(v3[0]), ALU.subtract).then_inc(S["dve_v"], 1)
                    if kind == "s":
                        for w in range(2):
                            dve.wait_ge(S["act_sq"], 2 * (NT * n + i) + w + 1)
                            V.tensor_reduce(ssq[:, i, w * HEADS:(w + 1) * HEADS],
                                            sq[w].rearrange("p (h d) -> p h d", h=HEADS), AX.X, ALU.add
                                            ).then_inc(S["dve_sum"], 1)
                        dve.wait_ge(S["dve_sum"], 2 * (NT * n + i) + 2)
                        V.tensor_scalar(ssq[:, i, :], ssq[:, i, :], 1e-24, None, ALU.max).then_inc(S["dve_ssq"], 1)
                    if kind == "c":
                        kr = m1[1][i % 2]
                        dve.wait_ge(S["dve_rope"], 2 * (NT * n + i) + 2)
                        V.tensor_tensor(kr, kr, m2[1][i % 2], ALU.add).then_inc(S["dve_ksum"], 1)
                        dve.wait_ge(S["dve_ksum"], NT * n + i + 1)
                        dve.wait_ge(S["pool_r"], NT * n + i + 1)
                        kv = kr.rearrange("p (h d) -> p h d", h=HEADS)
                        V.tensor_tensor(kv, kv, rinv[:, i, HEADS:2 * HEADS].unsqueeze(2).to_broadcast([P, HEADS, DH]),
                                        ALU.mult).then_inc(S["dve_k"], 1)
                if m is not None:
                    if kind == "l":
                        need(dve, S["pe_n"], KD * m)
                        V.memset(nrm[0:1, 0, P:D], 0.0).then_inc(S["dve_st"], 1)
                        dve.wait_ge(S["dve_wo"], 2 * m + 2)
                        for t in range(NT):
                            V.bn_stats(st[:, t, 0, :], xmid[:, t, 0:P])
                        dve.wait_ge(S["shift_in"], 32 * (m + 1))
                        dve.wait_ge(S["dve_st"], 2 * m + 1)
                        for t in range(NT):
                            last = V.bn_stats(st[:, t, 1, :], nrm[:, t, P:D])
                        last.then_inc(S["dve_st"], 1)
                        need_apart(dve, (S["dve_st"], 2 * m + 2))
                        for t in range(NT):
                            last = V.bn_aggr(mv[:, t, :], st[:, t])
                        last.then_inc(S["dve_mv"], 1)
                        dve.wait_ge(S["dve_mv"], m + 1)
                        V.tensor_scalar(ve[:], mv[:, :, 1], EPS, None, ALU.add).then_inc(S["dve_var"], 1)
                    if kind == "j":
                        dve.wait_ge(S["pool_rs"], m + 1)
                        for t in range(NT):
                            V.tensor_scalar(nrm[:, t, 0:P], xmid[:, t, 0:P], mv[:, t, 0:1], rs[:, t:t + 1],
                                            ALU.subtract, ALU.mult)
                            last = V.tensor_scalar(nrm[:, t, P:D], nrm[:, t, P:D], mv[:, t, 0:1], rs[:, t:t + 1],
                                                   ALU.subtract, ALU.mult)
                        last.then_inc(S["dve_n"], 1)
                    if kind == "n":
                        for half in range(KD):
                            dve.wait_ge(S["act_n"], KD * m + half + 1)
                            V.tensor_tensor(nT[1][:, half, :], TB[half], f32(nT[0][:, half, :]), ALU.subtract
                                            ).then_inc(S["dve_nlo"], 1)
                    if kind == "a":
                        hr, s = (hid[:, i % 2, :], P) if i < FJ else (hid_r[0:HR, :], HR)
                        dve.wait_ge(S["act_gate"], (FJ + 1) * m + i + 1)
                        dve.wait_ge(S["pe_w1"], 12 * m + 2 * i + 2)
                        need(dve, S["pool_u"], (FJ + 1) * m + max(i - 1, 0))
                        V.scalar_tensor_tensor(hr, AV[0:s, :], b1t[0:s, 2 * i + 1:2 * i + 2], gate[0:s, i % 2, :],
                                               ALU.add, ALU.mult).then_inc(S["dve_hid"], 1)
                    if kind == "e":
                        dve.wait_ge(S["pe_w2"], (FJ + 1) * (m + 1))
                        for b in range(2):
                            xv = xmid[:, 2 * b:2 * b + 2, :].rearrange("p t d -> p (t d)")
                            ins = V.tensor_tensor(xv, ACC[b], xv, ALU.add)
                            ins.then_inc(S["dve_add" if final else "dve_w2"], 1)
                            if final:
                                continue
                        if final:
                            dve.wait_ge(S["xold_in"], 16 * finals(m))
                            dve.wait_ge(S["dve_add"], 2 * finals(m))
                            for b in range(2):
                                xv = xmid[:, 2 * b:2 * b + 2, :].rearrange("p t d -> p (t d)")
                                V.scalar_tensor_tensor(xv, xv, 0.5, nrm[:, 2 * b:2 * b + 2, :].rearrange("p t d -> p (t d)"),
                                                       ALU.mult, ALU.add).then_inc(S["dve_w2"], 1)

        def early(n, todo):
            phase1(n, None, False, todo)

        def a_round(n, f, final, nxt, ahead):
            phase1(n, f, final)
            dve.wait_ge(S["pool_r"], NT * (n + 1))
            need(dve, S["act_exp"], HEADS * n)
            V.tensor_scalar(rq[:, 0], rinv[:, :, 0:HEADS], QK_SCALE, None, ALU.mult)
            V.tensor_scalar(rq[:, 1], rinv[:, :, 0:HEADS], -QK_SCALE, None, ALU.mult).then_inc(S["dve_rq"], 1)
            for s in range(-1, SLOTS):
                if 0 <= s - 1 < HEADS:
                    h = s - 1
                    dve.wait_ge(S["act_exp"], HEADS * n + h + 1)
                    V.reciprocal(rz[:, h, :], zs[:, h, :]).then_inc(S["dve_rz"], 1)
                if 0 <= s - 2 < HEADS:
                    h = s - 2
                    for half in range(2):
                        dve.wait_ge(S["act_p"], 2 * (HEADS * n + h) + half + 1)
                        a, w = half * 4 * P, (4 - half) * P
                        V.tensor_tensor(pT[1][:, h % 2, a:a + w], TB[half][:, 0:w], f32(pT[0][:, h % 2, a:a + w]),
                                        ALU.subtract).then_inc(S["dve_p"], 1)
                if s in AV_OUT:
                    p = AV_OUT.index(s)
                    dve.wait_ge(S["act_av"], PAIRS * n + p + 1)
                    V.tensor_tensor(oT[1][:, p % 2, :], AV, f32(oT[0][:, p % 2, :]), ALU.subtract
                                    ).then_inc(S["dve_av"], 1)
                if s + 1 < HEADS:
                    h = s + 1
                    for half in range(2):
                        waits = [(S["pe_s"], 2 * (HEADS * n + h) + half + 1)]
                        if half == 0 and h == 0:
                            waits.append((S["pe_qk_t"], 2 * NT * (n + 1)))
                        if half == 0 and h >= 3:
                            waits.append((S["pe_p"], 2 * (HEADS * n + h - 2)))
                        need_apart(dve, *waits)
                        for i in (2 * half, 2 * half + 1):
                            a = P if i == 0 else 0
                            last = V.tensor_tensor_reduce(probs[:, h % 3, i, a:],
                                                          RB[half][:, (i % 2) * 2 * P + a:(i % 2 + 1) * 2 * P],
                                                          mask[:, a:], 1.0, -3e38, ALU.add, ALU.max, mx[:, h, i:i + 1])
                        last.then_inc(S["dve_s"], 1)
                    dve.wait_ge(S["dve_s"], 2 * (HEADS * n + h) + 2)
                    if h == 0:
                        dve.wait_ge(S["dve_rq"], n + 1)
                    V.tensor_tensor(nb[:, h, :], mx[:, h, :], rq[:, 1, :, h], ALU.mult).then_inc(S["dve_nb"], 1)
                if s == PREP and nxt:
                    prep(n + 1, None)
                if s in EARLY and ahead:
                    early(n + 1, EARLY[s])
            dve.wait_ge(S["pe_wo"], PAIRS * (n + 1))
            dve.wait_ge(S["act_x"], n + 1)
            if f is not None:
                dve.wait_ge(S["x_stored"], 16 * n)
            for b in range(2):
                V.tensor_tensor(xmid[:, 2 * b:2 * b + 2, :].rearrange("p t d -> p (t d)"), ACC[b],
                                xin[:, 2 * b:2 * b + 2, :].rearrange("p t d -> p (t d)"), ALU.add
                                ).then_inc(S["dve_wo"], 1)

        for call in range(2):
            def finals(m, call=call):
                return m + 1 - B * (call + 1)

            def last_f(m, call=call):
                phase1(None, m, True)
                stage_end(dve, 1 + 2 * call)

            rounds(dve, call, prep, early, a_round, w_a, w_f, last_f)
            if call == 0:
                for c in range(G_CHUNKS):
                    k = G_BASE + c
                    g2 = [g[:, c * G_COLS:(c + 1) * G_COLS, :].rearrange("p k d -> p (k d)") for g in gw]
                    split_lo(k, [(g2[1], g2[0], G_WBUF[k % 2][:, 0:G_COLS * D], None)])
                dve.wait_ge(S["w_lo"], G_BASE + G_CHUNKS)
                def statistics(b, src, s_st, s_mv):
                    for t in range(NT):
                        last = V.bn_stats(gst[:, t, :], src[:, t, :])
                    last.then_inc(S[s_st], 1)
                    need_apart(dve, (S[s_st], b + 1))
                    for t in range(NT):
                        last = V.bn_aggr(gmv[:, t, :], gst[:, t, :])
                    last.then_inc(S[s_mv], 1)

                def variance(b, s_mv, s_var):
                    dve.wait_ge(S[s_mv], b + 1)
                    V.tensor_scalar(gve[:], gmv[:, :, 1], EPS, None, ALU.add).then_inc(S[s_var], 1)

                def normalise(b, dst, src, s_rs, done):
                    dve.wait_ge(S[s_rs], b + 1)
                    for t in range(NT):
                        last = V.tensor_scalar(dst[:, t, :], src[:, t, :], gmv[:, t, 0:1], grs[:, t:t + 1],
                                               ALU.subtract, ALU.mult)
                    last.then_inc(S[done], 1)

                def y_lo(b, r):
                    dve.wait_ge(S["g_yhi"], b + 1)
                    V.tensor_tensor(gy[r][1].rearrange("p t d -> p (t d)"), gn[:].rearrange("p t d -> p (t d)"),
                                    f32(gy[r][0].rearrange("p t d -> p (t d)")), ALU.subtract).then_inc(S["g_ylo"], 1)

                def pack(b, r, quarter):
                    dve.wait_ge(S["g_ylo"], b + 1)
                    need(dve, S["g_t"], GH * b + 4 * quarter)
                    cols = slice(quarter * 4 * GS, (quarter + 1) * 4 * GS)
                    for side, parts in enumerate(((0, 1, 0, 1), (0, 0, 1, 1))):
                        for c, part in enumerate(parts):
                            last = V.tensor_copy(ga[:, side, :, :, c, :],
                                                 f32(gy[r][part][:, :, cols]).rearrange("p t (h g) -> p t h g", g=GS))
                    last.then_inc(S["g_pack"], 1)

                def sequence(b, r, which):
                    for k in steps(which, TAIL):
                        if k < G_STEPS:
                            dve.wait_ge(S["g_exp"], G_STEPS * b + k + 1)
                            if which != "first" or k >= 4:
                                dve.wait_ge(S["g_o"], KD * (G_STEPS * b + k - 3))
                            V.tensor_copy(ges[0][:, k % 4, :], ge[:, k % 4, :]).then_inc(S["g_hi"], 1)
                        if k % 16 == 4 and k < G_STEPS:
                            quarter = k // 16 + 1
                            if quarter < 4:
                                pack(b, r, quarter)
                            elif which != "last":
                                pack(b + 1, 1 - r, 0)
                        c, _, kk = back(b, r, which, k, LAG_OUT)
                        if kk is not None and kk % NT == NT - 1:
                            h = kk // NT
                            V.reciprocal(grz[:, h, :], gz[:, h, :]).then_inc(S["g_rz"], 1)
                            for half in range(KD):
                                dve.wait_ge(S["g_ohi"], KD * (GH * c + h) + half + 1)
                                V.tensor_tensor(goT[h % 2][1][:, half, :], psum[:, 4 + half, :],
                                                f32(goT[h % 2][0][:, half, :]), ALU.subtract).then_inc(S["g_olo"], 1)
                        c, q, kk = back(b, r, which, k, LAG_ADD)
                        if kk is not None and kk % NT == NT - 1:
                            h = kk // NT
                            dve.wait_ge(S["g_w"], GH * c + h + 1)
                            dve.wait_ge(S["g_rz"], GH * c + h + 1)
                            need(dve, S["g_acc"], NT * (GH * c + h))
                            for t in range(NT):
                                V.scalar_tensor_tensor(gx[q][:, t, :], ACC[t // 2][:, (t % 2) * D:(t % 2 + 1) * D],
                                                       grz[:, h, t:t + 1], gx[q][:, t, :], ALU.mult, ALU.add
                                                       ).then_inc(S["g_acc"], 1)
                        c, q, kk = back(b, r, which, k, END_ST)
                        if kk == G_STEPS - 1:
                            dve.wait_ge(S["g_acc"], NT * GH * (c + 1))
                            statistics(c, gx[q], "g_st2", "g_mv2")
                        c, q, kk = back(b, r, which, k, END_VAR)
                        if kk == G_STEPS - 1:
                            variance(c, "g_mv2", "g_var2")
                        c, q, kk = back(b, r, which, k, END_N)
                        if kk == G_STEPS - 1:
                            dve.wait_ge(S["g_out"], 16 * c + 1)
                            normalise(c, gout, gx[q], "g_rs2", "g_z")
                        if which != "last":
                            if k == NEXT_ST:
                                dve.wait_ge(S["g_in"], 16 * (b + 2))
                                statistics(b + 1, gx[1 - r], "g_st", "g_mv")
                            if k == NEXT_VAR:
                                variance(b + 1, "g_mv", "g_var")
                            if k == NEXT_N:
                                normalise(b + 1, gn, gx[1 - r], "g_rs", "g_y")
                            if k == NEXT_LO:
                                y_lo(b + 1, 1 - r)

                dve.wait_ge(S["g_in"], 16 * 2)
                statistics(0, gx[0], "g_st", "g_mv")
                variance(0, "g_mv", "g_var")
                normalise(0, gn, gx[0], "g_rs", "g_y")
                y_lo(0, 0)
                pack(0, 0, 0)
                sequences(dve, sequence)
                stage_end(dve, 2)

    @block.tensor
    def _(pe):
        mm, turn = nc.tensor.matmul, nc.tensor.transpose
        stage_end(pe, 0)

        def three(out_, lhs, rhs, start, stop, **kw):
            mm(out_, lhs[0], rhs[0], start=start, stop=False, **kw)
            mm(out_, lhs[1], rhs[0], start=False, stop=False, **kw)
            return mm(out_, lhs[0], rhs[1], start=False, stop=stop, **kw)

        def w_a(stage):
            weights_done(pe, w_base(stage) + W_A)

        def w_f(stage):
            k = w_base(stage) + W_A
            chunk_in(pe, k)
            chunk_in(pe, k + 1)
            pe.wait_ge(S["w_small"], 16 * (9 * stage + 9))
            need(pe, S["dve_hid"], (FJ + 1) * B * stage)
            for j in range(FJ + 1):
                s = P if j < FJ else HR
                for c in range(2):
                    lo = HID * (1 - c) + j * P
                    for kt in range(KD):
                        last = mm(UB[0:s, 2 * j + c:2 * j + c + 1], WBUF[(k + kt) % 2][:, lo:lo + s],
                                  lnp[:, 1, kt:kt + 1], start=kt == 0, stop=kt == KD - 1, skip_group_check=True)
            last.then_inc(S["bias_mm"], 1)
            pe.wait_ge(S["bias_ok"], stage + 1)
            weights_done(pe, k + W_F)

        def prep(n, stored):
            pe.wait_ge(S["x_in"], 16 * (n + 1))
            for half in range(KD):
                if stored == "inside":
                    pe.wait_ge(S["dve_p"], 2 * (HEADS * n - 1) + half + 1)
                for t in range(NT):
                    last = turn(TB[half][:, t * P:(t + 1) * P], xnext[:, t, half * P:(half + 1) * P], ident[:])
                last.then_inc(S["pe_z"], 1)

        def phase1(n, m, todo=PHASE1):
            for step in todo:
                kind, i = step[0], int(step[1])
                if n is not None:
                    if kind in "qkv":
                        w = "qkv".index(kind)
                        k = 3 * i + w
                        if k == 0:
                            pe.wait_ge(S["dve_z"], KD * (n + 1))
                        if k < 2:
                            need(pe, S["dve_s"], 2 * HEADS * n)
                        elif (k - 2) % 3 == 2:
                            pe.wait_ge(S["dve_v"], NT * n + (k - 2) // 3 + 1)
                        else:
                            r = 2 * ((k - 2) // 3) + (k - 2) % 3 + 1
                            pe.wait_ge(S["act_sq"], 2 * NT * n + r)
                        for kt in range(KD):
                            last = three(RB[k % 2], [h[:, kt, i * P:(i + 1) * P] for h in hT],
                                         [x_[:, kt, w * INNER:(w + 1) * INNER] for x_ in wqkv_s],
                                         kt == 0, kt == KD - 1)
                        last.then_inc(S["pe_qkv"], 1)
                    if kind in "QK":
                        w = "QK".index(kind)
                        if w == 0:
                            pe.wait_ge(S["pool_q"], NT * n + i + 1)
                        else:
                            pe.wait_ge(S["dve_k"], NT * n + i + 1)
                        last_use = before(step, kind if m is None else kind + "n")
                        if last_use is None:
                            need(pe, S["dve_p"], 2 * HEADS * n)
                        elif last_use[0] == "n":
                            pe.wait_ge(S["dve_nlo"], KD * m + w + 1)
                        else:
                            pe.wait_ge(S["act_qk"], 2 * (NT * n + i - 1) + w + 1)
                        for a in range(PAIRS):
                            last = turn(TB[w][:, a * P:(a + 1) * P], m1[w][i % 2][:, a * P:(a + 1) * P], ident[:])
                        last.then_inc(S["pe_qk_t"], 1)
                if m is not None:
                    if kind == "n":
                        pe.wait_ge(S["dve_n"], m + 1)
                        last_use = [before(step, kind_) for kind_ in "QK"]
                        if n is None or last_use[1] is None:
                            pe.wait_ge(S["dve_p"], 2 * HEADS * (m + 1))
                        for half in range(KD):
                            if n is not None and last_use[half] is not None:
                                pe.wait_ge(S["act_qk"], 2 * (NT * n + int(last_use[half][1])) + half + 1)
                            for t in range(NT):
                                last = turn(TB[half][:, t * P:(t + 1) * P], nrm[:, t, half * P:(half + 1) * P], ident[:])
                            last.then_inc(S["pe_n"], 1)
                    if kind in "ga":
                        c = "ga".index(kind)
                        s = P if i < FJ else HR
                        if c == 0:
                            if i == 0:
                                pe.wait_ge(S["dve_nlo"], KD * m + 2)
                            need(pe, S["act_gate"], (FJ + 1) * m + i)
                        elif i == 0:
                            pe.wait_ge(S["dve_av"], PAIRS * (m + 1))
                        else:
                            pe.wait_ge(S["dve_hid"], (FJ + 1) * m + i)
                        lo = HID * (1 - c) + i * P
                        for kt in range(KD):
                            last = three((UB, AV)[c][0:s, :], [w_[:, kt, lo:lo + s] for w_ in w1_s], [h[:, kt, :] for h in nT],
                                         kt == 0, kt == KD - 1)
                        last.then_inc(S["pe_w1"], 1)
                    if kind == "w":
                        s = P if i < FJ else HR + 1
                        pe.wait_ge(S["pool_u"], (FJ + 1) * m + i + 1)
                        if i == 0:
                            pe.wait_ge(S["dve_wo"], 2 * m + 2)
                        for t in range(NT):
                            last = three(ACC[t // 2][:, (t % 2) * D:(t % 2 + 1) * D],
                                         [u[0:s, i % 2, t * P:(t + 1) * P] for u in pT],
                                         [w_[0:s, i, :] for w_ in w2_s],
                                         i == 0 and t % 2 == 0, i == FJ, skip_group_check=True)
                        last.then_inc(S["pe_w2"], 1)

        def early(n, todo):
            phase1(n, None, todo)

        def a_round(n, f, final, nxt, ahead):
            phase1(n, f)
            for s in range(-1, SLOTS):
                if 0 <= s - 2 < HEADS:
                    h = s - 2
                    pe.wait_ge(S["pool_n"], HEADS * n + h + 1)
                    for half in range(2):
                        if h == 0:
                            pe.wait_ge(S["act_qk"], 2 * NT * (n + 1))
                        else:
                            pe.wait_ge(S["dve_p"], 2 * (HEADS * n + h - 1) + half + 1)
                        col = 0
                        for j in (2 * half, 2 * half + 1):
                            for i in (j, j + 1):
                                if i == NT:
                                    continue
                                a = P if i == j else 0
                                last = turn(TB[half][:, col:col + P], probs[:, h % 3, i, a:a + P], ident[:])
                                col += P
                        last.then_inc(S["pe_p"], 1)
                if s + 1 < HEADS:
                    h = s + 1
                    rows = slice((h % 2) * DH, (h % 2 + 1) * DH)
                    if h == 0:
                        pe.wait_ge(S["act_qk"], 2 * NT * (n + 1))
                    for half in range(2):
                        if h:
                            pe.wait_ge(S["dve_s"], 2 * (HEADS * n + h - 1) + half + 1)
                        elif half == 0:
                            pe.wait_ge(S["act_sq"], 2 * NT * (n + 1))
                        else:
                            pe.wait_ge(S["dve_v"], NT * (n + 1))
                        for i in (2 * half, 2 * half + 1):
                            a = P if i == 0 else 0
                            last = mm(RB[half][:, (i % 2) * 2 * P + a:(i % 2 + 1) * 2 * P],
                                      qT[rows, h // 2, i * P:(i + 1) * P], kT[rows, h // 2, (i - 1) * P + a:(i + 1) * P],
                                      start=True, stop=True)
                        last.then_inc(S["pe_s"], 1)
                if 0 <= s - 3 < HEADS:
                    h = s - 3
                    p, c = h // 2, (h % 2) * DH
                    pe.wait_ge(S["dve_p"], 2 * (HEADS * n + h) + 2)
                    if h == 0:
                        pe.wait_ge(S["dve_v"], NT * (n + 1))
                    if h % 2 == 0:
                        need(pe, S["dve_av"], PAIRS * n + p)
                    for j in range(NT):
                        w = 2 * P if j < NT - 1 else P
                        last = three(AV[:, j * P:j * P + w], [v[:, j, p, c:c + P] for v in v_s],
                                     [x_[:, h % 2, 2 * j * P:2 * j * P + w] for x_ in pT],
                                     h % 2 == 0 and j == 0, h % 2 == 1 and j == NT - 1, skip_group_check=True)
                    last.then_inc(S["pe_av"], 1)
                if s == PREP and nxt:
                    prep(n + 1, "inside")
                if s in EARLY and ahead:
                    early(n + 1, EARLY[s])
                if s in AV_OUT:
                    p = AV_OUT.index(s)
                    pe.wait_ge(S["dve_av"], PAIRS * n + p + 1)
                    if p == 0 and f is not None:
                        pe.wait_ge(S["dve_w2"], 2 * (f + 1))
                    for t in range(NT):
                        last = three(ACC[t // 2][:, (t % 2) * D:(t % 2 + 1) * D],
                                     [o[:, p % 2, t * P:(t + 1) * P] for o in oT], [w_[:, p, :] for w_ in wo_s],
                                     p == 0 and t % 2 == 0, p == PAIRS - 1, skip_group_check=True)
                    last.then_inc(S["pe_wo"], 1)

        for call in range(2):
            def last_f(m, call=call):
                phase1(None, m)
                stage_end(pe, 1 + 2 * call)

            rounds(pe, call, prep, early, a_round, w_a, w_f, last_f)
            if call == 0:
                weights_done(pe, G_BASE + G_CHUNKS)
                def turn_pair(b, pp):
                    pe.wait_ge(S["g_pack"], 4 * b + pp // 2 + 1)
                    for side in range(2):
                        need(pe, S["g_tc"], GH * b + 2 * (pp - 1) + side + 1)
                        for t in range(NT):
                            last = turn(TB[side][:, t * P:(t + 1) * P],
                                        ga[:, side, t, 2 * (pp % 2):2 * (pp % 2) + 2].rearrange("p h c g -> p (h c g)"),
                                        ident[:])
                        last.then_inc(S["g_t"], 1)

                def sequence(b, r, which):
                    for k in steps(which, TAIL):
                        if k % 8 == 1 and k < G_STEPS:
                            pp = k // 8 + 1
                            if pp < GH // 2:
                                turn_pair(b, pp)
                            elif which != "last":
                                turn_pair(b + 1, 0)
                        if k < G_STEPS:
                            h, t = k // NT, k % NT
                            rows = slice((h % 2) * 4 * GS, (h % 2 + 1) * 4 * GS)
                            if k % 8 == 0:
                                pe.wait_ge(S["g_tc"], GH * b + 2 * (h // 2) + 2)
                            if which != "first" or k >= 2:
                                pe.wait_ge(S["g_exp"], G_STEPS * b + k - 1)
                            mm(RB[k % 2], gaT[rows, (h // 2) % 2, 0, t * P:(t + 1) * P], gaT[rows, (h // 2) % 2, 1, :],
                               start=True, stop=True).then_inc(S["g_s"], 1)
                        c, q, kk = back(b, r, which, k, LAG_O)
                        if kk is not None:
                            h, t = kk // NT, kk % NT
                            pe.wait_ge(S["g_lo"], G_STEPS * c + kk + 1)
                            for half in range(KD):
                                if t == 0:
                                    need(pe, S["g_olo"], KD * (GH * c + h - 1) + half + 1)
                                three(psum[:, 4 + half, :], [y[:, t, half * P:(half + 1) * P] for y in gy[q]],
                                      [e[:, kk % 4, :] for e in ges], t == 0, t == NT - 1).then_inc(S["g_o"], 1)
                        c, _, kk = back(b, r, which, k, LAG_W)
                        if kk is not None and kk % NT == NT - 1:
                            h = kk // NT
                            need(pe, S["g_acc"], NT * (GH * c + h))
                            for half in range(KD):
                                pe.wait_ge(S["g_olo"], KD * (GH * c + h) + half + 1)
                                for t in range(NT):
                                    last = three(ACC[t // 2][:, (t % 2) * D:(t % 2 + 1) * D],
                                                 [o[:, half, t * P:(t + 1) * P] for o in goT[h % 2]],
                                                 [g[:, h * KD + half, :] for g in gw],
                                                 t % 2 == 0 and half == 0, half == KD - 1, skip_group_check=True)
                            last.then_inc(S["g_w"], 1)

                turn_pair(0, 0)
                sequences(pe, sequence)
                stage_end(pe, 2)


INPUTS = ["L0_attn_x", "L0_attn_weight", "L0_ffn_wqkv", "L0_ffn_q_scale", "L0_ffn_k_scale", "L0_ffn_wo",
          "L0_ffn_ln_g", "L0_ffn_ln_b", "L0_ffn_w1", "L0_ffn_b1", "L0_ffn_w2", "L0_ffn_b2"]


def kernel(**inputs):
    import concourse.bacc as bacc
    from concourse.bass_utils import run_bass_kernel_spmd

    nc = bacc.Bacc("TRN2", target_bir_lowering=False, num_devices=1)
    arrays, args = {}, []
    for name in INPUTS:
        a = np.ascontiguousarray(inputs[name])
        arrays[name] = a
        args.append(nc.dram_tensor(name, a.shape, mybir.dt.from_np(a.dtype), kind="ExternalInput").ap())
    arrays["rotary"] = rotary_tables()
    args.append(nc.dram_tensor("rotary", arrays["rotary"].shape, F32, kind="ExternalInput").ap())
    args.append(nc.dram_tensor("out", (B, N, D), F32, kind="ExternalOutput").ap())
    build_macaron(nc, *args)
    r = run_bass_kernel_spmd(nc, [arrays], core_ids=[0])
    return r.results[0]["out"]
```

```python
from contextlib import ExitStack

import numpy as np

import concourse.bass as bass
from concourse import mybir

ALU = mybir.AluOpType
ACT = mybir.ActivationFunctionType
AX = mybir.AxisListType
F32 = mybir.dt.float32
F32R = mybir.dt.float32r

P = 128
B, N, D = 8, 512, 256
NT = N // P
KD = D // P
HEADS, DH = 8, 64
PAIRS = HEADS // 2
INNER = HEADS * DH
HID = int(D * 4 * 2 / 3)
FJ = HID // P
HR = HID - FJ * P
QK_SCALE = 8.0
EPS = 1e-5
LAYERS = 2
ROUNDS = LAYERS * B
GH = 16
GS = D // GH
GSCALE = float(GS) ** -0.5
MASKED = -1e37

PHASE1 = ("s0 g0 v0 a0 q1 u0 b1 k1 s1 g1 d1 Q0 a1 c0 v1 u1 q2 w0 g2 K0 b2 x0 l0 k2 a2 d2 u2 s2 w1 "
          "v2 g3 a3 c1 Q1 u3 q3 b3 w2 j0 K1 k3 g4 s3 Q2 a4 d3 u4 v3 c2 w3 c3 g5 K2 Q3 a5 K3 n0").split()

SLOTS = 12
AV_OUT = (5, 7, 9, 11)
PREP = 9
LATE = {-1: ["u5", "w4"], 0: ["w5"], 4: ["e0"], 7: ["y0"]}
W_SLOT = 10
W_SWITCH = 9
EARLY = {11: ["q0", "b0", "k0", "d0"]}


def rotary_tables():
    f = np.float32
    half = np.arange(0, DH, 2, dtype=f)
    inv_freq = (f(1.0) / f(10000.0) ** (half / f(DH))).astype(f)
    t = np.arange(N, dtype=f)
    freqs = t[:, None] * inv_freq[None, :]
    freqs = np.concatenate([freqs, freqs], axis=-1)
    base = (half + f(0.4 * DH)) / f(1.4 * DH)
    power = (t - f(N // 2)) / f(P // 2)
    scale = (base[None, :] ** power[:, None]).astype(f)
    scale = np.concatenate([scale, scale], axis=-1)
    sign = np.where(np.arange(DH) < DH // 2, f(-1), f(1))[None, :]
    cos, sin = np.cos(freqs), np.sin(freqs) * sign
    tables = np.stack([cos * scale, sin * scale, cos / scale, sin / scale]).astype(f)
    return np.ascontiguousarray(tables.reshape(4, NT, P, DH).transpose(2, 0, 1, 3))


def build_macaron(nc, x, g_w, wqkv, q_scale, k_scale, wo, ln_g, ln_b, w1, b1, w2, b2, tables, out):
    with ExitStack() as ctx, nc.allow_non_contiguous_dma(reason="vectors by feature"):
        build(nc, ctx, x, g_w, wqkv, q_scale, k_scale, wo, ln_g, ln_b, w1, b1, w2, b2, tables, out)


def build(nc, ctx, x, g_w, wqkv, q_scale, k_scale, wo, ln_g, ln_b, w1, b1, w2, b2, tables, out):
    def sb(name, shape, dt=F32, c=ctx):
        return c.enter_context(nc.sbuf_tensor(name, shape, dt))

    def sem(name):
        return ctx.enter_context(nc.semaphore(name))

    def need(eng, s, value):
        if isinstance(value, int) and value <= 0:
            return
        eng.wait_ge(s, value)

    def need_apart(eng, *waits):
        for s, v in waits:
            need(eng, s, v)
            eng.sem_inc(S["apart"], 1)

    def f32(ap):
        return ap.bitcast(F32)

    stream = nc.dram_tensor("stream", (2 * ROUNDS, N, D), F32, kind="Internal").ap()
    x_mid = nc.dram_tensor("x_mid", (2, B, N, D), F32, kind="Internal").ap()

    def tokens(ap, row):
        if isinstance(row, int):
            return ap[row].rearrange("(t p) d -> p t d", p=P)
        return ap[bass.ds(row, 1)].rearrange("o (t p) d -> p (o t) d", p=P)

    ident = sb("ident", [P, P])
    mask = sb("mask", [P, 2 * P])
    minus_half = sb("minus_half", [P, 2 * HEADS])
    rope = sb("rope", [P, 4, NT, DH])
    qks = sb("qks", [P, 2, DH])
    lnp = sb("lnp", [P, 2, KD])
    b1t = sb("b1t", [P, 2 * (FJ + 1)])
    wqkv_s = [sb(f"wqkv_{s}", [P, KD, 3 * INNER], F32R) for s in ("hi", "lo")]
    wo_s = [sb(f"wo_{s}", [P, PAIRS, D], F32R) for s in ("hi", "lo")]
    w1_s = [sb(f"w1_{s}", [P, KD, 2 * HID], F32R) for s in ("hi", "lo")]
    w2_s = [sb(f"w2_{s}", [P, FJ + 1, D], F32R) for s in ("hi", "lo")]
    probs = sb("probs", [P, 3, NT, 2 * P])
    flat = probs[:].rearrange("p a b c -> p a (b c)")
    sq = [flat[:, 2, 0:N], flat[:, 2, N:2 * N]]
    raw = flat.rearrange("p a b -> p (a b)")

    wbuf = sb("wbuf", [P, 3 * INNER])

    ffn_mem = ExitStack()
    with ExitStack() as first:
        x_all = sb("x_all", [P, B * NT, D], c=first)
        st0 = sb("st0", [P, B * NT, 6], c=first)
        mv0 = sb("mv0", [P, B * NT, 2], c=first)
        ve0 = sb("ve0", [P, B * NT], c=first)
        rs0 = sb("rs0", [P, B * NT], c=first)
        half0 = sb("half0", [P, B * NT], c=first)
    xnext = sb("xnext", [P, NT, D], c=ffn_mem)
    xin = sb("xin", [P, NT, D], c=ffn_mem)
    xmids = [sb(f"xmid{r}", [P, NT, D], c=ffn_mem) for r in range(2)]
    nrm = sb("nrm", [P, NT, D], c=ffn_mem)
    hT = [sb(f"hT_{s}", [P, KD, N], F32R, ffn_mem) for s in ("hi", "lo")]
    nT = [sb(f"nT_{s}", [P, KD, N], F32R, ffn_mem) for s in ("hi", "lo")]
    turned_qk = sb("turned_qk", [P, 2, 2, INNER], c=ffn_mem)
    m1 = [[turned_qk[:, w, r, :] for r in range(2)] for w in range(2)]
    turned_sin = sb("turned_sin", [P, 2, INNER], c=ffn_mem)
    m2 = [turned_sin[:, w, :] for w in range(2)]
    qT = sb("qT", [P, PAIRS, N], c=ffn_mem)
    kT = sb("kT", [P, PAIRS, N], c=ffn_mem)
    v_s = [sb(f"v_{s}", [P, NT, PAIRS, 3 * DH], F32R, ffn_mem) for s in ("hi", "lo")]
    pT = [sb(f"pT_{s}", [P, 2, 7 * P], F32R, ffn_mem) for s in ("hi", "lo")]
    oT = [sb(f"oT_{s}", [P, 2, N], F32R, ffn_mem) for s in ("hi", "lo")]
    gate_hid = sb("gate_hid", [P, 3, N], c=ffn_mem)
    gate, hid_r = gate_hid[:, 0:2, :], gate_hid[:, 2, :]
    ssq = sb("ssq", [P, NT, 2 * HEADS], c=ffn_mem)
    rinv = sb("rinv", [P, NT, 2 * HEADS], c=ffn_mem)
    rq = sb("rq", [P, 2, NT, HEADS], c=ffn_mem)
    mx = sb("mx", [P, HEADS, NT], c=ffn_mem)
    nb = sb("nb", [P, HEADS, NT], c=ffn_mem)
    zs = sb("zs", [P, HEADS, NT], c=ffn_mem)
    rz = sb("rz", [P, HEADS, NT], c=ffn_mem)
    st = sb("st", [P, NT, 2, 6], c=ffn_mem)
    mv = sb("mv", [P, NT, 2], c=ffn_mem)
    ve = sb("ve", [P, NT], c=ffn_mem)
    rs = sb("rs", [P, NT], c=ffn_mem)
    ffn_mem.close()

    glb_mem = ExitStack()
    gw = [sb(f"gw_{s}", [P, GH * KD, D], F32R, glb_mem) for s in ("hi", "lo")]
    gx = [sb(f"gx{r}", [P, NT, D], c=glb_mem) for r in range(2)]
    flat_w1, flat_w2 = [[w_[:].rearrange("p k d -> p (k d)") for w_ in ws] for ws in (w1_s, w2_s)]
    gy0 = [sb(f"gy_{s}", [P, NT, D], F32R, glb_mem)[:] for s in ("hi", "lo")]
    gy = [gy0, [w_[:, 0:NT * D].rearrange("p (t d) -> p t d", d=D) for w_ in flat_w2]]
    goT = [[w_[:, r * KD * N:(r + 1) * KD * N].rearrange("p (c n) -> p c n", n=N) for w_ in flat_w1]
           for r in range(2)]
    ga = raw[:, 0:2 * NT * GH * GS].rearrange("p (s t h c g) -> p s t h c g", s=2, t=NT, h=GH // 4, c=4)
    gaT = [[w_[:, 2 * KD * N:2 * KD * N + N] for w_ in flat_w1], [w_[:, NT * D:NT * D + N] for w_ in flat_w2]]
    ge = sb("ge", [P, 4, N], c=glb_mem)
    ges = [sb(f"ge_{s}", [P, 4, N], F32R, glb_mem) for s in ("hi", "lo")]
    gz = sb("gz", [P, GH, NT], c=glb_mem)
    grz = sb("grz", [P, GH, NT], c=glb_mem)
    gst = sb("gst", [P, NT, 6], c=glb_mem)
    gmv = sb("gmv", [P, NT, 2], c=glb_mem)
    gve = sb("gve", [P, NT], c=glb_mem)
    grs = sb("grs", [P, NT], c=glb_mem)
    gn_wide = sb("gn", [P, 3 * INNER], c=glb_mem)
    gn = gn_wide[:, 0:NT * D].rearrange("p (t d) -> p t d", d=D)
    gout = sb("gout", [P, NT, D], c=glb_mem)
    glb_mem.close()

    psum = ctx.enter_context(nc.psum_tensor("psum", [P, 8, N], F32))
    RB = [psum[:, 0, :], psum[:, 1, :]]
    TB = [psum[:, 2, :], psum[:, 3, :]]
    AV = psum[:, 4, :]
    UB = psum[:, 5, :]
    PAIR = [AV, UB]
    ACC = [psum[:, 6, :], psum[:, 7, :]]

    names = """apart consts zeros x0_out x0_stats x0_var x0_rs x0_z stage
        w_in0 w_in1 w_hi w_lo w_small rope_ok bias_mm bias_ok
        x_in x_stored shift_in xold_in
        pe_z pe_qkv pe_qk_t pe_s pe_p pe_av pe_wo pe_n pe_w1 pe_w2
        act_x act_z act_sq act_v act_qk act_exp act_p act_av act_n act_gate act_u
        dve_z dve_rope dve_sum dve_ssq dve_v dve_rq dve_y dve_k dve_s dve_nb dve_rz dve_p dve_av dve_wo
        dve_st dve_mv dve_var dve_n dve_nlo dve_hid dve_w2
        pool_r pool_q pool_k pool_n pool_rs pool_u
        g_in g_sum g_out g_st g_mv g_var g_rs g_y g_yhi g_ylo g_pack g_t g_tc g_s g_exp g_hi g_lo g_o g_ohi g_olo
        g_rz g_w g_acc g_st2 g_mv2 g_var2 g_rs2 g_z""".split() + [f"x0_in{b}" for b in range(B)]
    S = {n: sem(n) for n in names}

    def stage_end(eng, k):
        eng.drain().then_inc(S["stage"], 1)
        eng.wait_ge(S["stage"], 5 * (k + 1))

    block = ctx.enter_context(nc.Block())

    NORM = "ljny"

    def rounds_before(n, m):
        return n if n is not None else (m // ROUNDS + 1) * ROUNDS

    F_STEPS = PHASE1 + sum(LATE.values(), [])

    def before(step, kinds):
        earlier = [x_ for x_ in PHASE1[:PHASE1.index(step)] if x_[0] in kinds]
        return earlier[-1] if earlier else None

    def rounds(eng, call, prep, early, a_round, start, w_a, last_f):
        n0 = call * ROUNDS
        start(2 * call)
        prep(n0, None)
        first_steps = sum(EARLY.values(), [])
        plain = B * (call + 1)
        early(n0, first_steps)

        def one(n, odd, at, norm=True, feed=True, ahead=True, **kw):
            a_round(n, n - 2 if feed else None, n - 1 if norm else None, odd, ahead=ahead,
                    f_final=at >= B + 2, g_final=plain if at >= B + 1 else 0, nxt="loop0" if at < B else "loop1", **kw)

        one(n0, 0, 0, norm=False, feed=False, load=2 * call)
        one(n0 + 1, 1, 1, feed=False)
        one(n0 + 2, 0, 2)
        with eng.Fori(0, (B - 4) // 2) as j:
            one(n0 + 3 + 2 * j, 1, 3)
            one(n0 + 4 + 2 * j, 0, 4)
        one(n0 + B - 1, 1, B - 1, ahead=False, switch=2 * call + 1)
        w_a(2 * call + 1)
        early(n0 + B, first_steps)
        one(n0 + B, 0, B, fresh=2 * call + 1)
        one(n0 + B + 1, 1, B + 1, load=2 * call + 1)
        with eng.Fori(0, (B - 4) // 2) as j:
            one(n0 + B + 2 + 2 * j, 0, B + 2)
            one(n0 + B + 3 + 2 * j, 1, B + 3)
        one(n0 + ROUNDS - 2, 0, ROUNDS - 2)
        a_round(n0 + ROUNDS - 1, n0 + ROUNDS - 3, n0 + ROUNDS - 2, 1, ahead=False, f_final=True, g_final=plain, nxt=None)
        last_f(n0 + ROUNDS - 1)

    W_A, W_F = 3, 3
    G_CHUNKS = 8
    G_COLS = GH * KD // G_CHUNKS

    gate_hid_flat = gate_hid[:].rearrange("p a n -> p (a n)")

    def w_buf(k):
        if k % 2 == 0:
            return wbuf[:]
        if k == w_base(0) + 1:
            return raw[:, 0:3 * INNER]
        return gn_wide[:] if k == w_base(2) + 1 else gate_hid_flat[:, 0:3 * INNER]

    def g_buf(c):
        return (wbuf, raw[:, 2 * NT * GH * GS:])[c % 2][:, 0:G_COLS * D]

    def w_base(stage):
        return stage * (W_A + W_F) + (G_CHUNKS if stage >= 2 else 0)

    G_BASE = 2 * (W_A + W_F)
    CHUNK_DMAS = [1, 1, 1, 1, 1, 3] * 2 + [1] * G_CHUNKS + [1, 1, 1, 1, 1, 3] * 2

    def chunk_in(eng, k):
        eng.wait_ge(S[f"w_in{k % 2}"], 16 * sum(CHUNK_DMAS[k % 2:k + 1:2]))

    def weights_done(eng, k):
        eng.wait_ge(S["w_lo"], k)

    G_STEPS = GH * NT

    def sequences(eng, body):
        body(0, 0, "first")
        with eng.Fori(0, B // 2 - 1) as pair:
            body(2 * pair + 1, 1, "middle")
            body(2 * pair + 2, 0, "middle")
        body(B - 1, 1, "last")

    def steps(which, tail):
        return range(G_STEPS + (tail if which == "last" else 0))

    def back(b, r, which, k, lag):
        if k >= lag:
            return (b, r, k - lag) if k - lag < G_STEPS else (None, None, None)
        return (None, None, None) if which == "first" else (b - 1, 1 - r, k - lag + G_STEPS)

    LAG_O = 2
    LAG_W = LAG_O + NT
    LAG_OUT = 5 - (NT - 1)
    LAG_ADD = 11 - (NT - 1)
    LAG_END = LAG_ADD + 1
    TAIL = LAG_END + 4
    NEXT_ST, NEXT_VAR, NEXT_POW, NEXT_N, NEXT_HI, NEXT_LO = 24, 26, 26, 28, 30, 32
    W_G, W_NEXT = 3, 40
    END_ST, END_VAR, END_POW, END_N = LAG_END, LAG_END + 1, LAG_END + 1, LAG_END + 3

    @block.sync
    def _(sp):
        for b in range(B):
            sp.dma_start(x_all[:, b * NT:(b + 1) * NT, :], tokens(x, b)).then_inc(S[f"x0_in{b}"], 16)
        def chunk(k, dst_src):
            if k >= 2:
                sp.wait_ge(S["w_lo"], k - 1)
            for dst, src in dst_src:
                sp.dma_start(dst, src).then_inc(S[f"w_in{k % 2}"], 16)

        def w_qkv(stage):
            l, k = stage % LAYERS, w_base(stage)
            if stage:
                sp.wait_ge(S["dve_rope"], 2 * NT * B * stage)
                sp.wait_ge(S["dve_w2"], 2 * (B * stage - 2))
            sp.dma_start(rope[:], tables).then_inc(S["w_small"], 16)
            for i, ap in enumerate((q_scale, k_scale)):
                sp.dma_start(qks[:, i, :], ap[l:l + 1, :].to_broadcast([P, DH])).then_inc(S["w_small"], 16)
            for kt in range(KD):
                chunk(k + kt, [(w_buf(k + kt), wqkv[l, kt * P:(kt + 1) * P, :])])

        def w_o(stage):
            l, k = stage % LAYERS, w_base(stage)
            chunk(k + 2, [(w_buf(k + 2)[:, 0:PAIRS * D].rearrange("p (k d) -> p k d", d=D),
                           wo[l].rearrange("(k p) d -> p k d", p=P))])

        def w_a(stage):
            w_qkv(stage)
            w_o(stage)

        def w_f(stage):
            l, k = stage % LAYERS, w_base(stage) + W_A
            need(sp, S["dve_w2"], 2 * B * stage)
            sp.dma_start(lnp[:, 0, :], ln_g[l].rearrange("(k p) -> p k", p=P)).then_inc(S["w_small"], 16)
            sp.dma_start(lnp[:, 1, :], ln_b[l].rearrange("(k p) -> p k", p=P)).then_inc(S["w_small"], 16)
            b1v = b1t[:].rearrange("p (j c) -> p c j", c=2)
            for c in range(2):
                lo = HID * (1 - c)
                sp.dma_start(b1v[:, c, 0:FJ], b1[l, lo:lo + FJ * P].rearrange("(j p) -> p j", p=P)
                             ).then_inc(S["w_small"], 16)
                sp.dma_start(b1v[0:HR, c, FJ:FJ + 1], b1[l, lo + FJ * P:lo + HID].rearrange("(p o) -> p o", o=1)
                             ).then_inc(S["w_small"], 16)
            for kt in range(KD):
                chunk(k + kt, [(w_buf(k + kt)[:, 0:2 * HID], w1[l, kt * P:(kt + 1) * P, :])])
            v = w_buf(k + 2).rearrange("p (k d) -> p k d", d=D)
            sp.wait_ge(S["bias_mm"], stage + 1)
            chunk(k + 2, [(v[:, 0:FJ, :], w2[l, 0:FJ * P, :].rearrange("(k p) d -> p k d", p=P)),
                          (v[0:HR, FJ, :], w2[l, FJ * P:HID, :]), (v[HR:HR + 1, FJ, :], b2[l:l + 1, :])])

        def start(stage):
            pass

        w_qkv(0)
        for b in range(B):
            sp.wait_ge(S["x0_z"], NT * (b + 1))
            sp.dma_start(tokens(stream, b), x_all[:, b * NT:(b + 1) * NT, :]).then_inc(S["x0_out"], 16)
        w_o(0)
        sp.wait_ge(S["x0_out"], 16 * B)
        stage_end(sp, 0)

        def prep(n, stored):
            waits = [(S["pe_z"], KD * n), (S["act_x"], n)]
            if stored is not None:
                waits.append((S["x_stored"], stored))
            need_apart(sp, *waits)
            sp.dma_start(xnext[:], tokens(stream, n)).then_inc(S["x_in"], 16)

        def shift(m, xmid):
            sp.wait_ge(S["dve_wo"], 2 * m + 2)
            need(sp, S["pe_n"], KD * m)
            need(sp, S["dve_y"], m)
            sp.dma_start(nrm[1:P, :, P:D], xmid[0:P - 1, :, P:D]).then_inc(S["shift_in"], 16)
            sp.dma_start(nrm[0:1, 1:NT, P:D], xmid[P - 1:P, 0:NT - 1, P:D]).then_inc(S["shift_in"], 16)

        def x_old(m, call):
            need_apart(sp, (S["pe_n"], KD * (m + 1)))
            before_ = x if call == 0 else x_mid[1]
            sp.dma_start(nrm[:], tokens(before_, m - call * ROUNDS - B)).then_inc(S["xold_in"], 16)

        def keep(m, xmid, final, call):
            need_apart(sp, (S["dve_w2"], 2 * m + 2))
            if final:
                after = x_mid[0] if call == 0 else out
                sp.dma_start(tokens(after, m - call * ROUNDS - B), xmid[:]).then_inc(S["x_stored"], 16)
            else:
                sp.dma_start(tokens(stream, m + B), xmid[:]).then_inc(S["x_stored"], 16)

        for call in range(2):
            def a_round(n, f, g, odd, f_final, g_final, nxt, ahead, load=None, switch=None, fresh=None, call=call):
                if g is not None:
                    shift(g, xmids[1 - odd])
                if nxt:
                    prep(n + 1, 16 * (n - 2) if nxt == "loop0" else 16 * (n - 6))
                if g is not None and g_final:
                    x_old(g, call)
                if f is not None:
                    keep(f, xmids[odd], f_final, call)
                if load is not None:
                    w_f(load)

            def last_f(m, call=call):
                shift(m, xmids[1])
                x_old(m, call)
                keep(m - 1, xmids[0], True, call)
                keep(m, xmids[1], True, call)
                sp.wait_ge(S["x_stored"], 16 * (m + 1))
                stage_end(sp, 1 + 2 * call)

            rounds(sp, call, prep, lambda n, todo: None, a_round, start, w_a, last_f)
            if call == 0:
                sp.sem_inc(S["g_out"], 1)
                for b in range(2):
                    sp.dma_start(gx[b][:], tokens(x_mid[0], b)).then_inc(S["g_in"], 16)
                for c in range(G_CHUNKS):
                    chunk(G_BASE + c, [(g_buf(c).rearrange("p (k d) -> p k d", d=D),
                                        g_w[c * G_COLS * P:(c + 1) * G_COLS * P, :].rearrange("(k p) d -> p k d", p=P))])

                def store(b, r):
                    need_apart(sp, (S["g_acc"], NT * GH * (b + 1)))
                    sp.dma_start(tokens(x_mid[1], b), gx[r][:]).then_inc(S["g_sum"], 16)
                    need_apart(sp, (S["g_z"], b + 1))
                    sp.dma_start(tokens(stream, b + ROUNDS), gout[:]).then_inc(S["g_out"], 16)

                def sequence(b, r, which):
                    if which != "first":
                        store(b - 1, 1 - r)
                        if which != "last":
                            need_apart(sp, (S["g_sum"], 16 * b))
                            sp.dma_start(gx[1 - r][:], tokens(x_mid[0], b + 1)).then_inc(S["g_in"], 16)
                        else:
                            w_a(2)

                sequences(sp, sequence)
                store(B - 1, 1)
                sp.wait_ge(S["g_sum"], 16 * B)
                sp.wait_ge(S["g_out"], 16 * B + 1)
                stage_end(sp, 2)

    @block.gpsimd
    def _(pool):
        nc.gpsimd.memset(ident[:], 0.0)
        nc.gpsimd.memset(mask[:], 0.0)
        nc.gpsimd.memset(half0[:], -0.5)
        nc.gpsimd.memset(minus_half[:], -0.5).then_inc(S["consts"], 1)
        pool.wait_ge(S["consts"], 1)
        nc.gpsimd.affine_select(out=ident[:], in_=ident[:], compare_op=ALU.not_equal, fill=1.0, base=0,
                                pattern=[[-1, P]], channel_multiplier=1)
        nc.gpsimd.affine_select(out=mask[:, 0:P], in_=mask[:, 0:P], compare_op=ALU.is_ge, fill=MASKED, base=0,
                                pattern=[[1, P]], channel_multiplier=-1)
        nc.gpsimd.affine_select(out=mask[:, P:2 * P], in_=mask[:, P:2 * P], compare_op=ALU.is_ge, fill=MASKED,
                                base=0, pattern=[[-1, P]], channel_multiplier=1).then_inc(S["consts"], 1)
        pool.wait_ge(S["consts"], 2)
        for half in range(2):
            cols = slice(half * B * NT // 2, (half + 1) * B * NT // 2)
            pool.wait_ge(S["x0_var"], half + 1)
            nc.gpsimd.tensor_tensor(rs0[:, cols], ve0[:, cols], half0[:, cols], ALU.pow).then_inc(S["x0_rs"], 1)
        stage_end(pool, 0)

        def prep(n, stored):
            pass

        def start(stage):
            nc.gpsimd.memset(f32(v_s[0][:, :, :, DH:2 * DH]), 0.0)
            nc.gpsimd.memset(f32(v_s[1][:, :, :, DH:2 * DH]), 0.0).then_inc(S["zeros"], 1)

        def w_a(stage):
            pass

        def phase1(n, f, g, todo=PHASE1):
            for step in todo:
                kind, i = step[0], int(step[1])
                m = g if kind in NORM else f
                if kind == "b" and n is not None:
                    r = i % 2
                    pool.wait_ge(S["dve_rope"], 2 * (NT * n + i) + 1)
                    nc.gpsimd.tensor_tensor(m1[0][r], m1[0][r], m2[0], ALU.add).then_inc(S["pool_q"], 1)
                if kind == "d" and n is not None:
                    r = i % 2
                    pool.wait_ge(S["dve_rope"], 2 * (NT * n + i) + 2)
                    nc.gpsimd.tensor_tensor(m1[1][r], m1[1][r], m2[1], ALU.add).then_inc(S["pool_k"], 1)
                if kind == "s" and n is not None:
                    pool.wait_ge(S["dve_ssq"], NT * n + i + 1)
                    need(pool, S["act_exp"], HEADS * n)
                    nc.gpsimd.tensor_tensor(rinv[:, i, :], ssq[:, i, :], minus_half[:], ALU.pow
                                            ).then_inc(S["pool_r"], 1)
                if m is None:
                    continue
                if kind == "l":
                    pool.wait_ge(S["dve_var"], m + 1)
                    nc.gpsimd.tensor_tensor(rs[:], ve[:], minus_half[:, 0:NT], ALU.pow).then_inc(S["pool_rs"], 1)
                if kind == "u":
                    hr, s = (gate[:, i % 2, :], P) if i < FJ else (hid_r[0:HR + 1], HR + 1)
                    pool.wait_ge(S["act_u"], (FJ + 1) * m + i + 1)
                    nc.gpsimd.tensor_tensor(pT[1][0:s, i % 2, 0:N], hr, f32(pT[0][0:s, i % 2, 0:N]), ALU.subtract
                                            ).then_inc(S["pool_u"], 1)

        def early(n, todo):
            phase1(n, None, None, todo)

        def a_round(n, f, g, odd, f_final, g_final, nxt, ahead, load=None, switch=None, fresh=None):
            phase1(n, f, g)
            for s in range(-1, SLOTS):
                if s in LATE:
                    phase1(None, f, g, LATE[s])
                if s in EARLY and ahead:
                    early(n + 1, EARLY[s])
                h = s - 1
                if not 0 <= h < HEADS:
                    continue
                need_apart(pool, (S["dve_rz"], HEADS * n + h + 1))
                for i in range(NT):
                    a = P if i == 0 else 0
                    last = nc.gpsimd.tensor_scalar(probs[:, h % 3, i, a:], probs[:, h % 3, i, a:], rz[:, h, i:i + 1],
                                                   1.0, ALU.mult, ALU.mult)
                last.then_inc(S["pool_n"], 1)

        for call in range(2):
            def last_f(m, call=call):
                phase1(None, m - 1, m, F_STEPS)
                phase1(None, m, None, F_STEPS)
                stage_end(pool, 1 + 2 * call)

            rounds(pool, call, prep, early, a_round, start, w_a, last_f)
            if call == 0:
                def power(s_in, s_out, b):
                    pool.wait_ge(S[s_in], b + 1)
                    nc.gpsimd.tensor_tensor(grs[:], gve[:], minus_half[:, 0:NT], ALU.pow).then_inc(S[s_out], 1)

                def sequence(b, r, which):
                    for k in steps(which, TAIL):
                        if k < G_STEPS:
                            pool.wait_ge(S["g_hi"], G_STEPS * b + k + 1)
                            if which != "first" or k >= 4:
                                pool.wait_ge(S["g_o"], KD * (G_STEPS * b + k - 3))
                            nc.gpsimd.tensor_tensor(ges[1][:, k % 4, :], ge[:, k % 4, :], f32(ges[0][:, k % 4, :]),
                                                    ALU.subtract).then_inc(S["g_lo"], 1)
                        if k == NEXT_POW and which != "last":
                            power("g_var", "g_rs", b + 1)
                        c, _, kk = back(b, r, which, k, END_POW)
                        if kk == G_STEPS - 1:
                            power("g_var2", "g_rs2", c)

                power("g_var", "g_rs", 0)
                sequences(pool, sequence)
                stage_end(pool, 2)

    @block.scalar
    def _(act):
        copy = nc.scalar.copy

        def split_hi(k, outs):
            chunk_in(act, k)
            for o, i, scale in outs:
                if scale is None:
                    last = copy(o, i)
                else:
                    last = nc.scalar.activation(o, i, ACT.Copy, scale=scale)
            last.then_inc(S["w_hi"], 1)

        def w_qkv(stage):
            k = w_base(stage)
            need(act, S["pe_qkv"], 12 * B * stage)
            for kt in range(KD):
                split_hi(k + kt, [(wqkv_s[0][:, kt, :], w_buf(k + kt), None)])

        def w_o(stage):
            k = w_base(stage)
            need(act, S["pe_wo"], PAIRS * B * stage)
            split_hi(k + 2, [(wo_s[0][:].rearrange("p k d -> p (k d)"), w_buf(k + 2)[:, 0:PAIRS * D], None)])
            weights_done(act, k + W_A)

        w_a = w_o

        def w_f(stage):
            k = w_base(stage) + W_A
            need(act, S["dve_w2"], 2 * B * stage)
            act.wait_ge(S["w_small"], 16 * (9 * stage + 9))
            for kt in range(KD):
                split_hi(k + kt, [(w1_s[0][:, kt, :], w_buf(k + kt)[:, 0:2 * HID], lnp[:, 0, kt:kt + 1])])
            v = w_buf(k + 2).rearrange("p (k d) -> p k d", d=D)
            split_hi(k + 2, [(w2_s[0][:, 0:FJ, :], v[:, 0:FJ, :], None),
                             (w2_s[0][0:HR + 1, FJ, :], v[0:HR + 1, FJ, :], None)])
            weights_done(act, k + W_F)

        def start(stage):
            weights_done(act, w_base(stage) + W_A)

        w_qkv(0)
        w_o(0)
        stage_end(act, 0)

        def prep(n, stored):
            need(act, S["pe_qkv"], 12 * n)
            for half in range(KD):
                act.wait_ge(S["pe_z"], KD * n + half + 1)
                if half == 0:
                    copy(hT[0][:, 0, :], RB[0]).then_inc(S["act_z"], 1)
                else:
                    copy(hT[0][:, 1, 1:N], RB[1][:, 0:N - 1]).then_inc(S["act_z"], 1)

        def phase1(n, f, g, todo=PHASE1):
            for step in todo:
                kind, i = step[0], int(step[1])
                m = g if kind in NORM else f
                if n is not None:
                    if kind == "x":
                        act.wait_ge(S["x_in"], 16 * (n + 1))
                        need(act, S["dve_wo"], 2 * n)
                        copy(xin[:], xnext[:]).then_inc(S["act_x"], 1)
                    if kind in "qk":
                        w = "qk".index(kind)
                        act.wait_ge(S["dve_rope"], 2 * (NT * n + i) + w + 1)
                        if i == 0:
                            need(act, S["pe_p"], 2 * HEADS * n - 4)
                        else:
                            act.wait_ge(S["dve_sum"], 2 * (NT * n + i) - 1 + w)
                        nc.scalar.activation(sq[w], RB[(3 * i + w) % 2], ACT.Square).then_inc(S["act_sq"], 1)
                    if kind == "v":
                        act.wait_ge(S["pe_qkv"], 12 * n + 3 * i + 3)
                        need(act, S["pe_av"], HEADS * n)
                        copy(v_s[0][:, i].rearrange("p a (s d) -> p a s d", s=3)[:, :, ::2, :],
                             RB[(3 * i + 2) % 2].rearrange("p (a s d) -> p a s d", a=PAIRS, s=2)).then_inc(S["act_v"], 1)
                    if kind in "QK":
                        w = "QK".index(kind)
                        act.wait_ge(S["pe_qk_t"], 2 * (NT * n + i) + w + 1)
                        need(act, S["pe_s"], 2 * HEADS * n)
                        copy((qT, kT)[w][:, :, i * P:(i + 1) * P],
                             TB[(2 * i + w) % 2].rearrange("p (a q) -> p a q", a=PAIRS)).then_inc(S["act_qk"], 1)
                if m is not None:
                    if kind == "n":
                        need(act, S["pe_w1"], 12 * m)
                        for half in range(KD):
                            act.wait_ge(S["pe_n"], KD * m + half + 1)
                            copy(nT[0][:, half, :], TB[half]).then_inc(S["act_n"], 1)
                    if kind == "g":
                        s = P if i < FJ else HR
                        act.wait_ge(S["pe_w1"], 12 * m + 2 * i + 1)
                        act.wait_ge(S["bias_ok"], 1)
                        need(act, S["pool_u"], (FJ + 1) * m + i - 1)
                        nc.scalar.activation(gate[0:s, i % 2, :], UB[0:s, :], ACT.Gelu,
                                             bias=b1t[0:s, 2 * i:2 * i + 1]).then_inc(S["act_gate"], 1)
                    if kind == "u":
                        hr, s = (gate[:, i % 2, :], P) if i < FJ else (hid_r[0:HR + 1], HR + 1)
                        act.wait_ge(S["dve_hid"], (FJ + 1) * m + i + 1)
                        if i < 2:
                            act.wait_ge(S["pe_av"], HEADS * rounds_before(n, m))
                            if n is None:
                                act.wait_ge(S["pe_w2"], (FJ + 1) * m + i - 1)
                        else:
                            act.wait_ge(S["pe_w2"], (FJ + 1) * m + i - 1)
                        copy(pT[0][0:s, i % 2, 0:N], hr).then_inc(S["act_u"], 1)

        def early(n, todo):
            phase1(n, None, None, todo)

        def a_round(n, f, g, odd, f_final, g_final, nxt, ahead, load=None, switch=None, fresh=None):
            phase1(n, f, g)
            for s in range(-1, SLOTS):
                if 0 <= s - 2 < HEADS:
                    h = s - 2
                    for half in range(2):
                        act.wait_ge(S["pe_p"], 2 * (HEADS * n + h) + half + 1)
                        if half == 0 and h >= 2:
                            act.wait_ge(S["pe_av"], HEADS * n + h - 1)
                        elif half == 0 and f is not None:
                            act.wait_ge(S["pe_w2"], (FJ + 1) * (f + 1))
                        w = 4 * P if half == 0 else 3 * P
                        copy(pT[0][:, h % 2, half * 4 * P:half * 4 * P + w], TB[half][:, 0:w]).then_inc(S["act_p"], 1)
                if s in AV_OUT:
                    p = AV_OUT.index(s)
                    act.wait_ge(S["pe_av"], HEADS * n + 2 * p + 2)
                    if p >= 2:
                        act.wait_ge(S["pe_wo"], PAIRS * n + p - 1)
                    copy(oT[0][:, p % 2, :], PAIR[p % 2]).then_inc(S["act_av"], 1)
                if 0 <= s < HEADS:
                    act.wait_ge(S["dve_nb"], HEADS * n + s + 1)
                    if s == 0:
                        act.wait_ge(S["dve_rq"], n + 1)
                    for i in range(NT):
                        a = P if i == 0 else 0
                        last = nc.scalar.activation(probs[:, s % 3, i, a:], probs[:, s % 3, i, a:], ACT.Exp,
                                                    bias=nb[:, s, i:i + 1], scale=rq[:, 0, i, s:s + 1],
                                                    accum_out=zs[:, s, i:i + 1])
                    last.then_inc(S["act_exp"], 1)
                if s in LATE:
                    phase1(None, f, g, LATE[s])
                if s == PREP and nxt:
                    prep(n + 1, None)
                if s in EARLY and ahead:
                    early(n + 1, EARLY[s])
                if s == W_SLOT and load is not None:
                    w_f(load)
                if s == W_SWITCH and switch is not None:
                    w_qkv(switch)

        for call in range(2):
            def last_f(m, call=call):
                phase1(None, m - 1, m, F_STEPS)
                phase1(None, m, None, F_STEPS)
                stage_end(act, 1 + 2 * call)

            rounds(act, call, prep, early, a_round, start, w_a, last_f)
            if call == 0:
                def w_g(c):
                    split_hi(G_BASE + c, [(gw[0][:, c * G_COLS:(c + 1) * G_COLS, :].rearrange("p k d -> p (k d)"),
                                           g_buf(c), None)])

                def y_hi(b, r):
                    act.wait_ge(S["g_y"], b + 1)
                    need(act, S["g_o"], KD * G_STEPS * (b - 1))
                    copy(gy[r][0].rearrange("p t d -> p (t d)"), gn_wide[:, 0:NT * D]
                         ).then_inc(S["g_yhi"], 1)

                def turned(b, pp):
                    for side in range(2):
                        act.wait_ge(S["g_t"], GH * b + 2 * pp + side + 1)
                        need(act, S["g_s"], G_STEPS * b + 8 * (pp - 1))
                        copy(gaT[pp % 2][side], TB[side]).then_inc(S["g_tc"], 1)

                def sequence(b, r, which):
                    for k in steps(which, TAIL):
                        if k % 8 == 2 and k < G_STEPS:
                            pp = k // 8 + 1
                            if pp < GH // 2:
                                turned(b, pp)
                            elif which != "last":
                                turned(b + 1, 0)
                        if k < G_STEPS:
                            h, t = k // NT, k % NT
                            act.wait_ge(S["g_s"], G_STEPS * b + k + 1)
                            if which != "first" or k >= 4:
                                act.wait_ge(S["g_lo"], G_STEPS * b + k - 3)
                            nc.scalar.activation(ge[:, k % 4, :], RB[k % 2], ACT.Exp, scale=GSCALE,
                                                 accum_out=gz[:, h, t:t + 1]).then_inc(S["g_exp"], 1)
                        c, _, kk = back(b, r, which, k, LAG_OUT)
                        if kk is not None and kk % NT == NT - 1:
                            h = kk // NT
                            for half in range(KD):
                                act.wait_ge(S["g_o"], KD * (NT * (GH * c + h) + NT - 1) + half + 1)
                                need(act, S["g_w"], GH * c + h - 1)
                                copy(goT[h % 2][0][:, half, :], psum[:, 4 + half, :]).then_inc(S["g_ohi"], 1)
                        if k == NEXT_HI and which != "last":
                            y_hi(b + 1, 1 - r)
                        if which == "first" and k % 8 == W_G:
                            w_g(k // 8)
                        if which == "last" and k == W_NEXT:
                            w_qkv(2)
                            w_o(2)

                y_hi(0, 0)
                turned(0, 0)
                sequences(act, sequence)
                stage_end(act, 2)

    @block.vector
    def _(dve):
        V = nc.vector
        H0 = B * NT // 2
        for half in range(2):
            for b in range(half * B // 2, (half + 1) * B // 2):
                dve.wait_ge(S[f"x0_in{b}"], 16)
                for t in range(b * NT, (b + 1) * NT):
                    V.bn_stats(st0[:, t, :], x_all[:, t, :]).then_inc(S["x0_stats"], 1)
            dve.wait_ge(S["x0_stats"], H0 * (2 * half + 1))
            for t in range(half * H0, (half + 1) * H0):
                V.bn_aggr(mv0[:, t, :], st0[:, t, :]).then_inc(S["x0_stats"], 1)
            dve.wait_ge(S["x0_stats"], H0 * (2 * half + 2))
            cols = slice(half * H0, (half + 1) * H0)
            V.tensor_scalar(ve0[:, cols], mv0[:, cols, 1], EPS, None, ALU.add).then_inc(S["x0_var"], 1)

        def split_lo(k, outs):
            dve.wait_ge(S["w_hi"], k + 1)
            for lo, hi, i, scale in outs:
                if scale is None:
                    last = V.tensor_tensor(lo, i, f32(hi), ALU.subtract)
                else:
                    last = V.scalar_tensor_tensor(lo, i, scale, f32(hi), ALU.mult, ALU.subtract)
            last.then_inc(S["w_lo"], 1)

        def w_qkv(stage):
            k = w_base(stage)
            dve.wait_ge(S["w_small"], 16 * (9 * stage + 3))
            for i in range(2):
                V.tensor_tensor(rope[:, 2 * i], rope[:, 2 * i], qks[:, i].unsqueeze(1).to_broadcast([P, NT, DH]), ALU.mult)
                for half in range(2):
                    a, o = half * DH // 2, (1 - half) * DH // 2
                    last = V.tensor_tensor(rope[:, 2 * i + 1, :, a:a + DH // 2], rope[:, 2 * i + 1, :, a:a + DH // 2],
                                           qks[:, i, o:o + DH // 2].unsqueeze(1).to_broadcast([P, NT, DH // 2]), ALU.mult)
            last.then_inc(S["rope_ok"], 1)
            for kt in range(KD):
                split_lo(k + kt, [(wqkv_s[1][:, kt, :], wqkv_s[0][:, kt, :], w_buf(k + kt), None)])
            dve.wait_ge(S["rope_ok"], stage + 1)

        def w_o(stage):
            k = w_base(stage)
            flat_wo = [w[:].rearrange("p k d -> p (k d)") for w in wo_s]
            split_lo(k + 2, [(flat_wo[1], flat_wo[0], w_buf(k + 2)[:, 0:PAIRS * D], None)])
            if stage % LAYERS:
                weights_done(dve, k + W_A)
                V.memset(hid_r, 1.0)

        w_a = w_o

        def w_f(stage):
            k = w_base(stage) + W_A
            for kt in range(KD):
                split_lo(k + kt, [(w1_s[1][:, kt, :], w1_s[0][:, kt, :], w_buf(k + kt)[:, 0:2 * HID],
                                   lnp[:, 0, kt:kt + 1])])
            v = w_buf(k + 2).rearrange("p (k d) -> p k d", d=D)
            split_lo(k + 2, [(w2_s[1][:, 0:FJ, :], w2_s[0][:, 0:FJ, :], v[:, 0:FJ, :], None),
                             (w2_s[1][0:HR + 1, FJ, :], w2_s[0][0:HR + 1, FJ, :], v[0:HR + 1, FJ, :], None)])
            weights_done(dve, k + W_F)
            V.memset(hid_r, 1.0)
            dve.wait_ge(S["bias_mm"], stage + 1)
            V.tensor_tensor(b1t[:, 0:2 * FJ], b1t[:, 0:2 * FJ], AV[:, 0:2 * FJ], ALU.add)
            V.tensor_tensor(b1t[0:HR, 2 * FJ:], b1t[0:HR, 2 * FJ:], AV[0:HR, 2 * FJ:2 * FJ + 2], ALU.add
                            ).then_inc(S["bias_ok"], 1)
            dve.wait_ge(S["bias_ok"], stage + 1)

        def start(stage):
            V.memset(f32(hT[0][:, 1, 0:1]), 0.0)
            V.memset(f32(hT[1][:, 1, 0:1]), 0.0)
            V.memset(hid_r, 1.0)

        for t in range(B * NT):
            if t % H0 == 0:
                dve.wait_ge(S["x0_rs"], t // H0 + 1)
            V.tensor_scalar(x_all[:, t, :], x_all[:, t, :], mv0[:, t, 0:1], rs0[:, t:t + 1], ALU.subtract, ALU.mult
                            ).then_inc(S["x0_z"], 1)
        w_qkv(0)
        w_o(0)
        stage_end(dve, 0)

        def prep(n, stored):
            for half in range(KD):
                dve.wait_ge(S["act_z"], KD * n + half + 1)
                a = half
                V.tensor_tensor(hT[1][:, half, a:N], RB[half][:, 0:N - a], f32(hT[0][:, half, a:N]), ALU.subtract
                                ).then_inc(S["dve_z"], 1)

        def phase1(n, f, g, odd, f_final, g_final, todo=PHASE1):
            for step in todo:
                kind, i = step[0], int(step[1])
                m = g if kind in NORM else f
                if n is not None:
                    if kind in "qk":
                        w = "qk".index(kind)
                        dve.wait_ge(S["pe_qkv"], 12 * n + 3 * i + w + 1)
                        need(dve, S["pe_qk_t"], 2 * (NT * n + i) - 3 + w)
                        need(dve, S[("pool_q", "pool_k")[w]], NT * n + i)
                        src = RB[(3 * i + w) % 2]
                        h64 = "p (h d) -> p h d"
                        V.tensor_tensor(m1[w][i % 2].rearrange(h64, h=HEADS), src.rearrange(h64, h=HEADS),
                                        rope[:, 2 * w, i].unsqueeze(1).to_broadcast([P, HEADS, DH]), ALU.mult)
                        h232 = "p (h s d) -> p h s d"
                        sin = rope[:, 2 * w + 1, i].rearrange("p (s d) -> p s d", s=2)
                        V.tensor_tensor(m2[w].rearrange(h232, h=HEADS, s=2), src.rearrange(h232, h=HEADS, s=2)[:, :, ::-1, :],
                                        sin.unsqueeze(1).to_broadcast([P, HEADS, 2, DH // 2]), ALU.mult
                                        ).then_inc(S["dve_rope"], 1)
                    if kind == "v":
                        dve.wait_ge(S["act_v"], NT * n + i + 1)
                        v3 = [v[:, i].rearrange("p a (s d) -> p a s d", s=3)[:, :, ::2, :] for v in v_s]
                        V.tensor_tensor(v3[1], RB[(3 * i + 2) % 2].rearrange("p (a s d) -> p a s d", a=PAIRS, s=2),
                                        f32(v3[0]), ALU.subtract).then_inc(S["dve_v"], 1)
                    if kind == "s":
                        for w in range(2):
                            dve.wait_ge(S["act_sq"], 2 * (NT * n + i) + w + 1)
                            V.tensor_reduce(ssq[:, i, w * HEADS:(w + 1) * HEADS],
                                            sq[w].rearrange("p (h d) -> p h d", h=HEADS), AX.X, ALU.add
                                            ).then_inc(S["dve_sum"], 1)
                        dve.wait_ge(S["dve_sum"], 2 * (NT * n + i) + 2)
                        V.tensor_scalar(ssq[:, i, :], ssq[:, i, :], 1e-24, None, ALU.max).then_inc(S["dve_ssq"], 1)
                    if kind == "c":
                        kr = m1[1][i % 2]
                        dve.wait_ge(S["pool_k"], NT * n + i + 1)
                        dve.wait_ge(S["pool_r"], NT * n + i + 1)
                        kv = kr.rearrange("p (h d) -> p h d", h=HEADS)
                        V.tensor_tensor(kv, kv, rinv[:, i, HEADS:2 * HEADS].unsqueeze(2).to_broadcast([P, HEADS, DH]),
                                        ALU.mult).then_inc(S["dve_k"], 1)
                if m is not None:
                    xmid = xmids[1 - odd if kind in NORM else odd]
                    if kind == "l":
                        need(dve, S["pe_n"], KD * m)
                        V.memset(nrm[0:1, 0, P:D], 0.0).then_inc(S["dve_st"], 1)
                        dve.wait_ge(S["dve_wo"], 2 * m + 2)
                        for t in range(NT):
                            V.bn_stats(st[:, t, 0, :], xmid[:, t, 0:P])
                        dve.wait_ge(S["shift_in"], 32 * (m + 1))
                        dve.wait_ge(S["dve_st"], 2 * m + 1)
                        for t in range(NT):
                            last = V.bn_stats(st[:, t, 1, :], nrm[:, t, P:D])
                        last.then_inc(S["dve_st"], 1)
                        need_apart(dve, (S["dve_st"], 2 * m + 2))
                        for t in range(NT):
                            last = V.bn_aggr(mv[:, t, :], st[:, t])
                        last.then_inc(S["dve_mv"], 1)
                        dve.wait_ge(S["dve_mv"], m + 1)
                        V.tensor_scalar(ve[:], mv[:, :, 1], EPS, None, ALU.add).then_inc(S["dve_var"], 1)
                    if kind == "j":
                        dve.wait_ge(S["pool_rs"], m + 1)
                        for t in range(NT):
                            V.tensor_scalar(nrm[:, t, 0:P], xmid[:, t, 0:P], mv[:, t, 0:1], rs[:, t:t + 1],
                                            ALU.subtract, ALU.mult)
                            last = V.tensor_scalar(nrm[:, t, P:D], nrm[:, t, P:D], mv[:, t, 0:1], rs[:, t:t + 1],
                                                   ALU.subtract, ALU.mult)
                        last.then_inc(S["dve_n"], 1)
                    if kind == "n":
                        for half in range(KD):
                            dve.wait_ge(S["act_n"], KD * m + half + 1)
                            V.tensor_tensor(nT[1][:, half, :], TB[half], f32(nT[0][:, half, :]), ALU.subtract
                                            ).then_inc(S["dve_nlo"], 1)
                    if kind == "a":
                        hr, s = (gate[:, i % 2, :], P) if i < FJ else (hid_r[0:HR], HR)
                        dve.wait_ge(S["act_gate"], (FJ + 1) * m + i + 1)
                        dve.wait_ge(S["pe_w1"], 12 * m + 2 * i + 2)
                        if i == FJ:
                            need(dve, S["pool_u"], (FJ + 1) * m)
                        V.scalar_tensor_tensor(hr, AV[0:s, :], b1t[0:s, 2 * i + 1:2 * i + 2], gate[0:s, i % 2, :],
                                               ALU.add, ALU.mult).then_inc(S["dve_hid"], 1)
                    if kind == "y":
                        if g_final:
                            dve.wait_ge(S["xold_in"], 16 * (m + 1 - g_final))
                            for b in range(2):
                                xv = xmid[:, 2 * b:2 * b + 2, :].rearrange("p t d -> p (t d)")
                                last = V.scalar_tensor_tensor(xv, xv, 0.5, nrm[:, 2 * b:2 * b + 2, :].rearrange("p t d -> p (t d)"),
                                                              ALU.mult, ALU.add)
                            last.then_inc(S["dve_y"], 1)
                        else:
                            dve.sem_inc(S["dve_y"], 1)
                    if kind == "e":
                        dve.wait_ge(S["pe_w2"], (FJ + 1) * (m + 1))
                        dve.wait_ge(S["dve_y"], m + 1)
                        for b in range(2):
                            xv = xmid[:, 2 * b:2 * b + 2, :].rearrange("p t d -> p (t d)")
                            if f_final:
                                ins = V.scalar_tensor_tensor(xv, ACC[b], 0.5, xv, ALU.mult, ALU.add)
                            else:
                                ins = V.tensor_tensor(xv, ACC[b], xv, ALU.add)
                            ins.then_inc(S["dve_w2"], 1)

        def early(n, todo):
            phase1(n, None, None, 0, False, 0, todo)

        def a_round(n, f, g, odd, f_final, g_final, nxt, ahead, load=None, switch=None, fresh=None):
            phase1(n, f, g, odd, f_final, g_final)
            dve.wait_ge(S["pool_r"], NT * (n + 1))
            need(dve, S["act_exp"], HEADS * n)
            V.tensor_scalar(rq[:, 0], rinv[:, :, 0:HEADS], QK_SCALE, None, ALU.mult)
            V.tensor_scalar(rq[:, 1], rinv[:, :, 0:HEADS], -QK_SCALE, None, ALU.mult).then_inc(S["dve_rq"], 1)
            for s in range(-1, SLOTS):
                if 0 <= s - 1 < HEADS:
                    h = s - 1
                    dve.wait_ge(S["act_exp"], HEADS * n + h + 1)
                    V.reciprocal(rz[:, h, :], zs[:, h, :]).then_inc(S["dve_rz"], 1)
                if 0 <= s - 2 < HEADS:
                    h = s - 2
                    for half in range(2):
                        dve.wait_ge(S["act_p"], 2 * (HEADS * n + h) + half + 1)
                        a, w = half * 4 * P, (4 - half) * P
                        V.tensor_tensor(pT[1][:, h % 2, a:a + w], TB[half][:, 0:w], f32(pT[0][:, h % 2, a:a + w]),
                                        ALU.subtract).then_inc(S["dve_p"], 1)
                if s in AV_OUT:
                    p = AV_OUT.index(s)
                    dve.wait_ge(S["act_av"], PAIRS * n + p + 1)
                    V.tensor_tensor(oT[1][:, p % 2, :], PAIR[p % 2], f32(oT[0][:, p % 2, :]), ALU.subtract
                                    ).then_inc(S["dve_av"], 1)
                if s + 1 < HEADS:
                    h = s + 1
                    for half in range(2):
                        waits = [(S["pe_s"], 2 * (HEADS * n + h) + half + 1)]
                        if half == 0 and h >= 3:
                            waits.append((S["pe_p"], 2 * (HEADS * n + h - 2)))
                        need_apart(dve, *waits)
                        for i in (2 * half, 2 * half + 1):
                            a = P if i == 0 else 0
                            last = V.tensor_tensor_reduce(probs[:, h % 3, i, a:],
                                                          RB[half][:, (i % 2) * 2 * P + a:(i % 2 + 1) * 2 * P],
                                                          mask[:, a:], 1.0, -3e38, ALU.add, ALU.max, mx[:, h, i:i + 1])
                        last.then_inc(S["dve_s"], 1)
                    dve.wait_ge(S["dve_s"], 2 * (HEADS * n + h) + 2)
                    if h == 0:
                        dve.wait_ge(S["dve_rq"], n + 1)
                    V.tensor_tensor(nb[:, h, :], mx[:, h, :], rq[:, 1, :, h], ALU.mult).then_inc(S["dve_nb"], 1)
                if s in LATE:
                    phase1(None, f, g, odd, f_final, g_final, LATE[s])
                if s == PREP and nxt:
                    prep(n + 1, None)
                if s in EARLY and ahead:
                    early(n + 1, EARLY[s])
                if s == W_SLOT and load is not None:
                    w_f(load)
                if s == W_SWITCH and switch is not None:
                    w_qkv(switch)
            dve.wait_ge(S["pe_wo"], PAIRS * (n + 1))
            dve.wait_ge(S["act_x"], n + 1)
            if f is not None:
                dve.wait_ge(S["x_stored"], 16 * (f + 1))
            for b in range(2):
                V.tensor_tensor(xmids[odd][:, 2 * b:2 * b + 2, :].rearrange("p t d -> p (t d)"), ACC[b],
                                xin[:, 2 * b:2 * b + 2, :].rearrange("p t d -> p (t d)"), ALU.add
                                ).then_inc(S["dve_wo"], 1)

        for call in range(2):
            def last_f(m, call=call):
                phase1(None, m - 1, m, 0, True, B * (call + 1), F_STEPS)
                phase1(None, m, None, 1, True, 0, F_STEPS)
                stage_end(dve, 1 + 2 * call)

            rounds(dve, call, prep, early, a_round, start, w_a, last_f)
            if call == 0:
                def w_g(c):
                    g2 = [g[:, c * G_COLS:(c + 1) * G_COLS, :].rearrange("p k d -> p (k d)") for g in gw]
                    split_lo(G_BASE + c, [(g2[1], g2[0], g_buf(c), None)])

                def statistics(b, src, s_st, s_mv):
                    for t in range(NT):
                        last = V.bn_stats(gst[:, t, :], src[:, t, :])
                    last.then_inc(S[s_st], 1)
                    need_apart(dve, (S[s_st], b + 1))
                    for t in range(NT):
                        last = V.bn_aggr(gmv[:, t, :], gst[:, t, :])
                    last.then_inc(S[s_mv], 1)

                def variance(b, s_mv, s_var):
                    dve.wait_ge(S[s_mv], b + 1)
                    V.tensor_scalar(gve[:], gmv[:, :, 1], EPS, None, ALU.add).then_inc(S[s_var], 1)

                def normalise(b, dst, src, s_rs, done):
                    dve.wait_ge(S[s_rs], b + 1)
                    for t in range(NT):
                        last = V.tensor_scalar(dst[:, t, :], src[:, t, :], gmv[:, t, 0:1], grs[:, t:t + 1],
                                               ALU.subtract, ALU.mult)
                    last.then_inc(S[done], 1)

                def y_lo(b, r):
                    dve.wait_ge(S["g_yhi"], b + 1)
                    V.tensor_tensor(gy[r][1].rearrange("p t d -> p (t d)"), gn_wide[:, 0:NT * D],
                                    f32(gy[r][0].rearrange("p t d -> p (t d)")), ALU.subtract).then_inc(S["g_ylo"], 1)

                def pack(b, r, quarter):
                    dve.wait_ge(S["g_ylo"], b + 1)
                    need(dve, S["g_t"], GH * b + 4 * quarter)
                    cols = slice(quarter * 4 * GS, (quarter + 1) * 4 * GS)
                    for side, parts in enumerate(((0, 1, 0, 1), (0, 0, 1, 1))):
                        for c, part in enumerate(parts):
                            last = V.tensor_copy(ga[:, side, :, :, c, :],
                                                 f32(gy[r][part][:, :, cols]).rearrange("p t (h g) -> p t h g", g=GS))
                    last.then_inc(S["g_pack"], 1)

                def sequence(b, r, which):
                    for k in steps(which, TAIL):
                        if k < G_STEPS:
                            dve.wait_ge(S["g_exp"], G_STEPS * b + k + 1)
                            if which != "first" or k >= 4:
                                dve.wait_ge(S["g_o"], KD * (G_STEPS * b + k - 3))
                            V.tensor_copy(ges[0][:, k % 4, :], ge[:, k % 4, :]).then_inc(S["g_hi"], 1)
                        if k % 16 == 4 and k < G_STEPS:
                            quarter = k // 16 + 1
                            if quarter < 4:
                                pack(b, r, quarter)
                            elif which != "last":
                                pack(b + 1, 1 - r, 0)
                        c, _, kk = back(b, r, which, k, LAG_OUT)
                        if kk is not None and kk % NT == NT - 1:
                            h = kk // NT
                            V.reciprocal(grz[:, h, :], gz[:, h, :]).then_inc(S["g_rz"], 1)
                            for half in range(KD):
                                dve.wait_ge(S["g_ohi"], KD * (GH * c + h) + half + 1)
                                V.tensor_tensor(goT[h % 2][1][:, half, :], psum[:, 4 + half, :],
                                                f32(goT[h % 2][0][:, half, :]), ALU.subtract).then_inc(S["g_olo"], 1)
                        c, q, kk = back(b, r, which, k, LAG_ADD)
                        if kk is not None and kk % NT == NT - 1:
                            h = kk // NT
                            dve.wait_ge(S["g_w"], GH * c + h + 1)
                            dve.wait_ge(S["g_rz"], GH * c + h + 1)
                            need(dve, S["g_acc"], NT * (GH * c + h))
                            for t in range(NT):
                                V.scalar_tensor_tensor(gx[q][:, t, :], ACC[t // 2][:, (t % 2) * D:(t % 2 + 1) * D],
                                                       grz[:, h, t:t + 1], gx[q][:, t, :], ALU.mult, ALU.add
                                                       ).then_inc(S["g_acc"], 1)
                        c, q, kk = back(b, r, which, k, END_ST)
                        if kk == G_STEPS - 1:
                            dve.wait_ge(S["g_acc"], NT * GH * (c + 1))
                            statistics(c, gx[q], "g_st2", "g_mv2")
                        c, q, kk = back(b, r, which, k, END_VAR)
                        if kk == G_STEPS - 1:
                            variance(c, "g_mv2", "g_var2")
                        c, q, kk = back(b, r, which, k, END_N)
                        if kk == G_STEPS - 1:
                            dve.wait_ge(S["g_out"], 16 * c + 1)
                            normalise(c, gout, gx[q], "g_rs2", "g_z")
                        if which != "last":
                            if k == NEXT_ST:
                                dve.wait_ge(S["g_in"], 16 * (b + 2))
                                statistics(b + 1, gx[1 - r], "g_st", "g_mv")
                            if k == NEXT_VAR:
                                variance(b + 1, "g_mv", "g_var")
                            if k == NEXT_N:
                                normalise(b + 1, gn, gx[1 - r], "g_rs", "g_y")
                            if k == NEXT_LO:
                                y_lo(b + 1, 1 - r)
                        if which == "first" and k % 8 == W_G:
                            w_g(k // 8)
                        if which == "last" and k == W_NEXT:
                            w_qkv(2)
                            w_o(2)

                dve.wait_ge(S["g_in"], 16 * 2)
                statistics(0, gx[0], "g_st", "g_mv")
                variance(0, "g_mv", "g_var")
                normalise(0, gn, gx[0], "g_rs", "g_y")
                y_lo(0, 0)
                pack(0, 0, 0)
                sequences(dve, sequence)
                stage_end(dve, 2)

    @block.tensor
    def _(pe):
        mm, turn = nc.tensor.matmul, nc.tensor.transpose
        stage_end(pe, 0)

        def three(out_, lhs, rhs, start, stop, **kw):
            mm(out_, lhs[0], rhs[0], start=start, stop=False, **kw)
            mm(out_, lhs[1], rhs[0], start=False, stop=False, **kw)
            return mm(out_, lhs[0], rhs[1], start=False, stop=stop, **kw)

        def w_a(stage):
            weights_done(pe, w_base(stage) + KD)

        def start(stage):
            weights_done(pe, w_base(stage) + W_A)

        def biases(stage):
            k = w_base(stage) + W_A
            chunk_in(pe, k)
            chunk_in(pe, k + 1)
            pe.wait_ge(S["w_small"], 16 * (9 * stage + 9))
            pe.wait_ge(S["dve_av"], PAIRS * (B * stage + stage % LAYERS) + 3)
            for j in range(FJ + 1):
                s = P if j < FJ else HR
                for c in range(2):
                    lo = HID * (1 - c) + j * P
                    for kt in range(KD):
                        last = mm(AV[0:s, 2 * j + c:2 * j + c + 1], w_buf(k + kt)[:, lo:lo + s],
                                  lnp[:, 1, kt:kt + 1], start=kt == 0, stop=kt == KD - 1, skip_group_check=True)
            last.then_inc(S["bias_mm"], 1)

        def prep(n, stored):
            pe.wait_ge(S["x_in"], 16 * (n + 1))
            for half in range(KD):
                if stored == "inside":
                    pe.wait_ge(S["dve_s"], 2 * (HEADS * n - 1) + half + 1)
                for t in range(NT):
                    last = turn(RB[half][:, t * P:(t + 1) * P], xnext[:, t, half * P:(half + 1) * P], ident[:])
                last.then_inc(S["pe_z"], 1)

        def phase1(n, f, g, todo=PHASE1):
            for step in todo:
                kind, i = step[0], int(step[1])
                m = g if kind in NORM else f
                if n is not None:
                    if kind in "qkv":
                        w = "qkv".index(kind)
                        k = 3 * i + w
                        if k == 0:
                            pe.wait_ge(S["dve_z"], KD * (n + 1))
                        if k < 2:
                            need(pe, S["dve_s"], 2 * HEADS * n)
                        elif (k - 2) % 3 == 2:
                            pe.wait_ge(S["dve_v"], NT * n + (k - 2) // 3 + 1)
                        else:
                            r = 2 * ((k - 2) // 3) + (k - 2) % 3 + 1
                            pe.wait_ge(S["act_sq"], 2 * NT * n + r)
                        for kt in range(KD):
                            last = three(RB[k % 2], [h[:, kt, i * P:(i + 1) * P] for h in hT],
                                         [x_[:, kt, w * INNER:(w + 1) * INNER] for x_ in wqkv_s],
                                         kt == 0, kt == KD - 1)
                        last.then_inc(S["pe_qkv"], 1)
                    if kind in "QK":
                        w = "QK".index(kind)
                        if w == 0:
                            pe.wait_ge(S["pool_q"], NT * n + i + 1)
                        else:
                            pe.wait_ge(S["dve_k"], NT * n + i + 1)
                        last_use = before(step, kind if g is None else kind + "n")
                        if last_use is None:
                            need(pe, S["dve_p"], 2 * HEADS * n)
                        elif last_use[0] == "n":
                            pe.wait_ge(S["dve_nlo"], KD * g + w + 1)
                        else:
                            pe.wait_ge(S["act_qk"], 2 * (NT * n + i - 1) + w + 1)
                        for a in range(PAIRS):
                            last = turn(TB[w][:, a * P:(a + 1) * P], m1[w][i % 2][:, a * P:(a + 1) * P], ident[:])
                        last.then_inc(S["pe_qk_t"], 1)
                if m is not None:
                    if kind == "n":
                        pe.wait_ge(S["dve_n"], m + 1)
                        last_use = [before(step, kind_) for kind_ in "QK"]
                        if n is None or last_use[1] is None:
                            pe.wait_ge(S["dve_p"], 2 * HEADS * (m + 1))
                        for half in range(KD):
                            if n is not None and last_use[half] is not None:
                                pe.wait_ge(S["act_qk"], 2 * (NT * n + int(last_use[half][1])) + half + 1)
                            for t in range(NT):
                                last = turn(TB[half][:, t * P:(t + 1) * P], nrm[:, t, half * P:(half + 1) * P], ident[:])
                            last.then_inc(S["pe_n"], 1)
                    if kind in "ga":
                        c = "ga".index(kind)
                        s = P if i < FJ else HR
                        if c == 0:
                            if i == 0:
                                pe.wait_ge(S["dve_nlo"], KD * m + 2)
                            if i:
                                pe.wait_ge(S["act_gate"], (FJ + 1) * m + i)
                            else:
                                pe.wait_ge(S["dve_av"], PAIRS * rounds_before(n, m))
                                if n is None:
                                    pe.wait_ge(S["act_gate"], (FJ + 1) * m)
                        elif i == 0:
                            pe.wait_ge(S["dve_av"], PAIRS * rounds_before(n, m))
                            if n is None:
                                pe.wait_ge(S["dve_hid"], (FJ + 1) * m)
                        else:
                            pe.wait_ge(S["dve_hid"], (FJ + 1) * m + i)
                        lo = HID * (1 - c) + i * P
                        for kt in range(KD):
                            last = three((UB, AV)[c][0:s, :], [w_[:, kt, lo:lo + s] for w_ in w1_s], [h[:, kt, :] for h in nT],
                                         kt == 0, kt == KD - 1)
                        last.then_inc(S["pe_w1"], 1)
                    if kind == "w":
                        s = P if i < FJ else HR + 1
                        pe.wait_ge(S["pool_u"], (FJ + 1) * m + i + 1)
                        if i == 0:
                            pe.wait_ge(S["dve_wo"], 2 * rounds_before(n, m))
                            if n is None:
                                pe.wait_ge(S["dve_w2"], 2 * m)
                        for t in range(NT):
                            last = three(ACC[t // 2][:, (t % 2) * D:(t % 2 + 1) * D],
                                         [u[0:s, i % 2, t * P:(t + 1) * P] for u in pT],
                                         [w_[0:s, i, :] for w_ in w2_s],
                                         i == 0 and t % 2 == 0, i == FJ, skip_group_check=True)
                        last.then_inc(S["pe_w2"], 1)

        def early(n, todo):
            phase1(n, None, None, todo)

        def a_round(n, f, g, odd, f_final, g_final, nxt, ahead, load=None, switch=None, fresh=None):
            phase1(n, f, g)
            if load is not None and load % LAYERS == 0:
                pe.wait_ge(S["zeros"], load // LAYERS + 1)
            if fresh is not None:
                weights_done(pe, w_base(fresh) + W_A)
            for s in range(-1, SLOTS):
                if 0 <= s - 2 < HEADS:
                    h = s - 2
                    pe.wait_ge(S["pool_n"], HEADS * n + h + 1)
                    for half in range(2):
                        if h == 0:
                            pe.wait_ge(S["act_qk"], 2 * NT * (n + 1))
                            if g is not None:
                                pe.wait_ge(S["dve_nlo"], KD * (g + 1))
                        else:
                            pe.wait_ge(S["dve_p"], 2 * (HEADS * n + h - 1) + half + 1)
                        col = 0
                        for j in (2 * half, 2 * half + 1):
                            for i in (j, j + 1):
                                if i == NT:
                                    continue
                                a = P if i == j else 0
                                last = turn(TB[half][:, col:col + P], probs[:, h % 3, i, a:a + P], ident[:])
                                col += P
                        last.then_inc(S["pe_p"], 1)
                if s + 1 < HEADS:
                    h = s + 1
                    rows = slice((h % 2) * DH, (h % 2 + 1) * DH)
                    if h == 0:
                        pe.wait_ge(S["act_qk"], 2 * NT * (n + 1))
                    for half in range(2):
                        if h:
                            pe.wait_ge(S["dve_s"], 2 * (HEADS * n + h - 1) + half + 1)
                        elif half == 0:
                            pe.wait_ge(S["act_sq"], 2 * NT * (n + 1))
                        else:
                            pe.wait_ge(S["dve_v"], NT * (n + 1))
                        for i in (2 * half, 2 * half + 1):
                            a = P if i == 0 else 0
                            last = mm(RB[half][:, (i % 2) * 2 * P + a:(i % 2 + 1) * 2 * P],
                                      qT[rows, h // 2, i * P:(i + 1) * P], kT[rows, h // 2, (i - 1) * P + a:(i + 1) * P],
                                      start=True, stop=True)
                        last.then_inc(S["pe_s"], 1)
                if 0 <= s - 3 < HEADS:
                    h = s - 3
                    p, c = h // 2, (h % 2) * DH
                    pe.wait_ge(S["dve_p"], 2 * (HEADS * n + h) + 2)
                    if h == 0:
                        pe.wait_ge(S["dve_v"], NT * (n + 1))
                    if h % 2 == 0:
                        need(pe, S["dve_av"], PAIRS * n + p - 1)
                    for j in range(NT):
                        w = 2 * P if j < NT - 1 else P
                        last = three(PAIR[p % 2][:, j * P:j * P + w], [v[:, j, p, c:c + P] for v in v_s],
                                     [x_[:, h % 2, 2 * j * P:2 * j * P + w] for x_ in pT],
                                     h % 2 == 0 and j == 0, h % 2 == 1 and j == NT - 1, skip_group_check=True)
                    last.then_inc(S["pe_av"], 1)
                if s in LATE:
                    phase1(None, f, g, LATE[s])
                if s == PREP and nxt:
                    prep(n + 1, "inside")
                if s in EARLY and ahead:
                    early(n + 1, EARLY[s])
                if s in AV_OUT:
                    p = AV_OUT.index(s)
                    pe.wait_ge(S["dve_av"], PAIRS * n + p + 1)
                    if p == 0 and f is not None:
                        pe.wait_ge(S["dve_w2"], 2 * (f + 1))
                    for t in range(NT):
                        last = three(ACC[t // 2][:, (t % 2) * D:(t % 2 + 1) * D],
                                     [o[:, p % 2, t * P:(t + 1) * P] for o in oT], [w_[:, p, :] for w_ in wo_s],
                                     p == 0 and t % 2 == 0, p == PAIRS - 1, skip_group_check=True)
                    last.then_inc(S["pe_wo"], 1)
                if s == W_SLOT and load is not None:
                    biases(load)
            if load is not None:
                pe.wait_ge(S["bias_ok"], load + 1)
                weights_done(pe, w_base(load) + W_A + W_F)

        for call in range(2):
            def last_f(m, call=call):
                phase1(None, m - 1, m, F_STEPS)
                phase1(None, m, None, F_STEPS)
                stage_end(pe, 1 + 2 * call)

            rounds(pe, call, prep, early, a_round, start, w_a, last_f)
            if call == 0:
                def turn_pair(b, pp):
                    pe.wait_ge(S["g_pack"], 4 * b + pp // 2 + 1)
                    for side in range(2):
                        need(pe, S["g_tc"], GH * b + 2 * (pp - 1) + side + 1)
                        for t in range(NT):
                            last = turn(TB[side][:, t * P:(t + 1) * P],
                                        ga[:, side, t, 2 * (pp % 2):2 * (pp % 2) + 2].rearrange("p h c g -> p (h c g)"),
                                        ident[:])
                        last.then_inc(S["g_t"], 1)

                def sequence(b, r, which):
                    for k in steps(which, TAIL):
                        if k % 8 == 1 and k < G_STEPS:
                            pp = k // 8 + 1
                            if pp < GH // 2:
                                turn_pair(b, pp)
                            elif which != "last":
                                turn_pair(b + 1, 0)
                        if k < G_STEPS:
                            h, t = k // NT, k % NT
                            rows = slice((h % 2) * 4 * GS, (h % 2 + 1) * 4 * GS)
                            if k % 8 == 0:
                                pe.wait_ge(S["g_tc"], GH * b + 2 * (h // 2) + 2)
                            if which != "first" or k >= 2:
                                pe.wait_ge(S["g_exp"], G_STEPS * b + k - 1)
                            mm(RB[k % 2], gaT[(h // 2) % 2][0][rows, t * P:(t + 1) * P], gaT[(h // 2) % 2][1][rows, :],
                               start=True, stop=True).then_inc(S["g_s"], 1)
                        c, q, kk = back(b, r, which, k, LAG_O)
                        if kk is not None:
                            h, t = kk // NT, kk % NT
                            pe.wait_ge(S["g_lo"], G_STEPS * c + kk + 1)
                            for half in range(KD):
                                if t == 0:
                                    need(pe, S["g_olo"], KD * (GH * c + h - 1) + half + 1)
                                three(psum[:, 4 + half, :], [y[:, t, half * P:(half + 1) * P] for y in gy[q]],
                                      [e[:, kk % 4, :] for e in ges], t == 0, t == NT - 1).then_inc(S["g_o"], 1)
                        c, _, kk = back(b, r, which, k, LAG_W)
                        if kk is not None and kk % NT == NT - 1:
                            h = kk // NT
                            need(pe, S["g_acc"], NT * (GH * c + h))
                            if which == "first":
                                weights_done(pe, G_BASE + h * KD // G_COLS + 1)
                            for half in range(KD):
                                pe.wait_ge(S["g_olo"], KD * (GH * c + h) + half + 1)
                                for t in range(NT):
                                    last = three(ACC[t // 2][:, (t % 2) * D:(t % 2 + 1) * D],
                                                 [o[:, half, t * P:(t + 1) * P] for o in goT[h % 2]],
                                                 [g[:, h * KD + half, :] for g in gw],
                                                 t % 2 == 0 and half == 0, half == KD - 1, skip_group_check=True)
                            last.then_inc(S["g_w"], 1)

                turn_pair(0, 0)
                sequences(pe, sequence)
                stage_end(pe, 2)


INPUTS = ["L0_attn_x", "L0_attn_weight", "L0_ffn_wqkv", "L0_ffn_q_scale", "L0_ffn_k_scale", "L0_ffn_wo",
          "L0_ffn_ln_g", "L0_ffn_ln_b", "L0_ffn_w1", "L0_ffn_b1", "L0_ffn_w2", "L0_ffn_b2"]


def kernel(**inputs):
    import concourse.bacc as bacc
    from concourse.bass_utils import run_bass_kernel_spmd

    nc = bacc.Bacc("TRN2", target_bir_lowering=False, num_devices=1)
    arrays, args = {}, []
    for name in INPUTS:
        a = np.ascontiguousarray(inputs[name])
        arrays[name] = a
        args.append(nc.dram_tensor(name, a.shape, mybir.dt.from_np(a.dtype), kind="ExternalInput").ap())
    arrays["rotary"] = rotary_tables()
    args.append(nc.dram_tensor("rotary", arrays["rotary"].shape, F32, kind="ExternalInput").ap())
    args.append(nc.dram_tensor("out", (B, N, D), F32, kind="ExternalOutput").ap())
    build_macaron(nc, *args)
    r = run_bass_kernel_spmd(nc, [arrays], core_ids=[0])
    return r.results[0]["out"]
```
